# Optimizing a Trainium2 kernel written in Bass

```python
import numpy as np
import jax
import jax.numpy as jnp

def _softmax(x, axis=-1):
    return jax.nn.softmax(x, axis=axis)

def _gelu(x):
    return jax.nn.gelu(x, approximate=True)

def _silu(x):
    return jax.nn.silu(x)

def _sigmoid(x):
    return jax.nn.sigmoid(x)

def _layernorm(x, axis=-1, eps=1e-05):
    m = jnp.mean(x, axis=axis, keepdims=True)
    v = jnp.var(x, axis=axis, keepdims=True)
    return (x - m) / jnp.sqrt(v + eps)

def _scatter_add(tgt, idx, src, axis=0):
    return tgt.at[idx].add(src)

def _segment_sum(src, seg, n):
    return jax.ops.segment_sum(src, seg, n)
kernel_name = 'mk_decoder_preln_d1_seqx_r4_1d4873'

def setup_inputs(seed: int=0):
    np.random.seed(seed)
    _w = jnp.asarray

    def _rec_inputs():
        import jax
        import jax.numpy as jnp
        _rk = jax.random.key(seed)
        x = -0.0003929 + 0.9999 * jax.random.normal(jax.random.fold_in(_rk, 1), (8, 256, 256), jnp.float32)
        _lenS = 256 - jax.random.randint(jax.random.fold_in(_rk, 7), (8,), 0, max(1, 256 // 4) + 1, jnp.int32)
        _lenS2 = 256 - jax.random.randint(jax.random.fold_in(_rk, 8), (8,), 0, max(1, 256 // 4) + 1, jnp.int32)
        _ctx_1024P = jax.random.normal(jax.random.fold_in(_rk, 11), (8, 16, 256), jnp.float32)
        _ctx_1024c = jax.random.dirichlet(jax.random.fold_in(_rk, 511), 0.3 * jnp.ones((16,), jnp.float32), (8, 256))
        _ctx_1024t = jnp.einsum('bsk,bkd->bsd', _ctx_1024c, _ctx_1024P)
        _ctx_1024t = _ctx_1024t * jax.lax.rsqrt(jnp.mean(jnp.square(_ctx_1024t)) + 1e-12) * 0.953939
        ctx_1024 = 2.81802e-05 + 1.00001 * (_ctx_1024t + 0.3 * jax.random.normal(jax.random.fold_in(_rk, 611), (8, 256, 256), jnp.float32))
        return (x, ctx_1024)
    x, ctx_1024 = _rec_inputs()

    def _L0_attn_setup():
        import jax, jax.numpy as jnp
        import numpy as np
        from jax.scipy.special import erf
        INV_SQRT2 = 0.7071067811865476
        INV_SQRT2PI = 0.3989422804014327
        ETA, BETA, ALPHA = (0.1, 0.9, 0.99)

        def gelu(x):
            return 0.5 * x * (1.0 + erf(x * INV_SQRT2))

        def gelu_grad(x):
            cdf = 0.5 * (1.0 + erf(x * INV_SQRT2))
            pdf = jnp.exp(-0.5 * x * x) * INV_SQRT2PI
            return cdf + x * pdf

        def _reference_tuple_inner(x, W_K, W_V, W1, W2, m1, m2):
            B, T, H = x.shape
            denom = B * H
            K = jnp.einsum('bth,kh->btk', x, W_K)
            V = jnp.einsum('bth,vh->btv', x, W_V)
            reads = jnp.einsum('btd,hd->bth', gelu(jnp.einsum('btk,dk->btd', K, W1)), W2)
            assoc_losses = jnp.mean((reads - V) ** 2, axis=(0, 2))

            def step(carry, kv):
                W1c, W2c, m1c, m2c = carry
                k_t, v_t = kv
                h = k_t @ W1c.T
                a = gelu(h)
                pred = a @ W2c.T
                dpred = 2.0 / denom * (pred - v_t)
                g2 = dpred.T @ a
                dh = dpred @ W2c * gelu_grad(h)
                g1 = dh.T @ k_t
                n1 = jnp.linalg.norm(g1)
                n2 = jnp.linalg.norm(g2)
                surprise = 0.5 * (n1 + n2)
                g1 = jnp.where(n1 > 1.0, g1 / n1, g1)
                g2 = jnp.where(n2 > 1.0, g2 / n2, g2)
                m1n = BETA * m1c - ETA * g1
                m2n = BETA * m2c - ETA * g2
                W1n = ALPHA * W1c + m1n
                W2n = ALPHA * W2c + m2n
                return ((W1n, W2n, m1n, m2n), surprise)
            Kt = jnp.swapaxes(K, 0, 1)
            Vt = jnp.swapaxes(V, 0, 1)
            (W1f, W2f, m1f, m2f), surprises = jax.lax.scan(step, (W1, W2, m1, m2), (Kt, Vt))
            return (reads, surprises, assoc_losses, W1f, W2f)
        key = jax.random.key(seed)
        k0, k1, k2, k3, k4 = jax.random.split(key, 5)
        B, T, H, D = (32, 256, 256, 64)
        x = jax.random.normal(k0, (B, T, H), dtype=jnp.float32)
        W_K = jax.random.normal(k1, (H, H), dtype=jnp.float32) / np.float32(np.sqrt(H))
        W_V = jax.random.normal(k2, (H, H), dtype=jnp.float32) / np.float32(np.sqrt(H))
        W1 = jax.random.normal(k3, (D, H), dtype=jnp.float32) * 0.02
        W2 = jax.random.normal(k4, (H, D), dtype=jnp.float32) * 0.02
        m1 = jnp.zeros((D, H), dtype=jnp.float32)
        m2 = jnp.zeros((H, D), dtype=jnp.float32)
        return {'x': x, 'W_K': W_K, 'W_V': W_V, 'W1': W1, 'W2': W2, 'm1': m1, 'm2': m2}
    _L0_attn_all = _L0_attn_setup()
    _L0_attn_in = {k: v for k, v in _L0_attn_all.items() if k in ('W_K', 'W_V', 'W1', 'W2', 'm1', 'm2')}
    del _L0_attn_all

    def _L0_xattn_setup():
        import jax, jax.numpy as jnp
        import numpy as np
        EMBED = 256
        B, I, J = (8, 512, 512)
        SCALE = EMBED ** (-0.5)
        key = jax.random.key(seed)
        ks = jax.random.split(key, 5)
        s = EMBED ** (-0.5)
        return {'q_in': jax.random.normal(ks[0], (B, I, EMBED), dtype=jnp.float32), 'k_v': jax.random.normal(ks[1], (B, J, EMBED), dtype=jnp.float32), 'Wq': jax.random.normal(ks[2], (EMBED, EMBED), dtype=jnp.float32) * s, 'bq': jnp.zeros((EMBED,), dtype=jnp.float32), 'Wk': jax.random.normal(ks[3], (EMBED, EMBED), dtype=jnp.float32) * s, 'bk': jnp.zeros((EMBED,), dtype=jnp.float32), 'Wv': jax.random.normal(ks[4], (EMBED, EMBED), dtype=jnp.float32) * s, 'bv': jnp.zeros((EMBED,), dtype=jnp.float32)}
    _L0_xattn_all = _L0_xattn_setup()
    _L0_xattn_in = {k: v for k, v in _L0_xattn_all.items() if k in ('Wq', 'bq', 'Wk', 'bk', 'Wv', 'bv')}
    del _L0_xattn_all

    def _L0_ffn_setup():
        import jax, jax.numpy as jnp
        import numpy as np
        DIM = 256
        DEPTH = 6
        HEADS = 16
        DIM_HEAD = 64
        WINDOW = 64
        INNER = HEADS * DIM_HEAD
        DIM_INNER = int(DIM * 4 * 2 / 3)
        QK_SCALE = 8.0

        def shift_tokens(t):
            a, s = jnp.split(t, 2, -1)
            s = jnp.pad(s, ((0, 0), (1, 0), (0, 0)))[:, :-1]
            return jnp.concatenate([a, s], -1)

        def l2norm(t):
            return t / jnp.maximum(jnp.linalg.norm(t, axis=-1, keepdims=True), 1e-12)

        def rotate_half(x):
            x1, x2 = jnp.split(x, 2, -1)
            return jnp.concatenate([-x2, x1], -1)

        def rotary_tables(n):
            half = jnp.arange(0, DIM_HEAD, 2, dtype=jnp.float32)
            inv_freq = 1.0 / 10000.0 ** (half / DIM_HEAD)
            t = jnp.arange(n, dtype=jnp.float32)
            freqs = t[:, None] * inv_freq[None, :]
            freqs = jnp.concatenate([freqs, freqs], -1)
            base_scale = (half + 0.4 * DIM_HEAD) / (1.4 * DIM_HEAD)
            power = (t - n // 2) / (WINDOW // 2)
            scale = base_scale[None, :] ** power[:, None]
            scale = jnp.concatenate([scale, scale], -1)
            return (freqs, scale)

        def local_attention(q, k, v):
            b, h, n, d = q.shape
            w = WINDOW
            nw = n // w
            bq = q.reshape(b, h, nw, w, d)
            bk = k.reshape(b, h, nw, w, d)
            bv = v.reshape(b, h, nw, w, d)

            def look(t):
                p = jnp.pad(t, ((0, 0), (0, 0), (1, 0), (0, 0), (0, 0)))
                return jnp.concatenate([p[:, :, :nw], p[:, :, 1:]], axis=3)
            bk2, bv2 = (look(bk), look(bv))
            seq = jnp.arange(n).reshape(nw, w)
            seq_p = jnp.pad(seq, ((1, 0), (0, 0)), constant_values=-1)
            jt = jnp.concatenate([seq_p[:nw], seq_p[1:]], axis=1)
            it = seq[:, :, None]
            jb = jt[:, None, :]
            mask = (it < jb) | (it > jb + w) | (jb == -1)
            sim = jnp.einsum('bhwie,bhwje->bhwij', bq, bk2) * QK_SCALE
            sim = jnp.where(mask, -jnp.finfo(sim.dtype).max, sim)
            attn = jax.nn.softmax(sim, -1)
            out = jnp.einsum('bhwij,bhwje->bhwie', attn, bv2)
            return out.reshape(b, h, n, d)

        def attn_layer(x, Wqkv, qs, ksc, Wo):
            b, n, _ = x.shape
            qkv = x @ Wqkv
            q, k, v = jnp.split(qkv, 3, -1)
            sh = lambda t: t.reshape(b, n, HEADS, DIM_HEAD).transpose(0, 2, 1, 3)
            q, k, v = (sh(q), sh(k), sh(v))
            q = l2norm(q) * qs
            k = l2norm(k) * ksc
            freqs, scale = rotary_tables(n)
            cos, sin = (jnp.cos(freqs), jnp.sin(freqs))
            q = q * cos * scale + rotate_half(q) * sin * scale
            inv = 1.0 / scale
            k = k * cos * inv + rotate_half(k) * sin * inv
            out = local_attention(q, k, v)
            out = out.transpose(0, 2, 1, 3).reshape(b, n, INNER)
            return out @ Wo

        def ffn_layer(x, g, bln, W1, b1, W2, b2):
            mu = x.mean(-1, keepdims=True)
            var = ((x - mu) ** 2).mean(-1, keepdims=True)
            xn = (x - mu) / jnp.sqrt(var + 1e-05) * g + bln
            hg = xn @ W1 + b1
            a, gate = jnp.split(hg, 2, -1)
            return a * jax.nn.gelu(gate, approximate=False) @ W2 + b2
        key = jax.random.key(seed)
        ks = jax.random.split(key, 8)
        B, N = (2, 512)
        init = lambda k, shape: jax.random.normal(k, shape, jnp.float32) * 0.02
        return {'x': jax.random.normal(ks[0], (B, N, DIM), jnp.float32), 'Wqkv': init(ks[1], (DEPTH, DIM, 3 * INNER)), 'q_scale': jnp.ones((DEPTH, DIM_HEAD), jnp.float32), 'k_scale': jnp.ones((DEPTH, DIM_HEAD), jnp.float32), 'Wo': init(ks[2], (DEPTH, INNER, DIM)), 'ln_g': jnp.ones((DEPTH, DIM), jnp.float32), 'ln_b': jnp.zeros((DEPTH, DIM), jnp.float32), 'W1': init(ks[3], (DEPTH, DIM, 2 * DIM_INNER)), 'b1': jnp.zeros((DEPTH, 2 * DIM_INNER), jnp.float32), 'W2': init(ks[4], (DEPTH, DIM_INNER, DIM)), 'b2': jnp.zeros((DEPTH, DIM), jnp.float32)}
    _L0_ffn_all = _L0_ffn_setup()
    _L0_ffn_in = {k: v for k, v in _L0_ffn_all.items() if k in ('Wqkv', 'q_scale', 'k_scale', 'Wo', 'ln_g', 'ln_b', 'W1', 'b1', 'W2', 'b2')}
    del _L0_ffn_all
    return {'x': x, 'ctx_1024': ctx_1024, 'L0_attn_W_K': _L0_attn_in['W_K'], 'L0_attn_W_V': _L0_attn_in['W_V'], 'L0_attn_W1': _L0_attn_in['W1'], 'L0_attn_W2': _L0_attn_in['W2'], 'L0_attn_m1': _L0_attn_in['m1'], 'L0_attn_m2': _L0_attn_in['m2'], 'L0_xattn_Wq': _L0_xattn_in['Wq'], 'L0_xattn_bq': _L0_xattn_in['bq'], 'L0_xattn_Wk': _L0_xattn_in['Wk'], 'L0_xattn_bk': _L0_xattn_in['bk'], 'L0_xattn_Wv': _L0_xattn_in['Wv'], 'L0_xattn_bv': _L0_xattn_in['bv'], 'L0_ffn_Wqkv': _L0_ffn_in['Wqkv'], 'L0_ffn_q_scale': _L0_ffn_in['q_scale'], 'L0_ffn_k_scale': _L0_ffn_in['k_scale'], 'L0_ffn_Wo': _L0_ffn_in['Wo'], 'L0_ffn_ln_g': _L0_ffn_in['ln_g'], 'L0_ffn_ln_b': _L0_ffn_in['ln_b'], 'L0_ffn_W1': _L0_ffn_in['W1'], 'L0_ffn_b1': _L0_ffn_in['b1'], 'L0_ffn_W2': _L0_ffn_in['W2'], 'L0_ffn_b2': _L0_ffn_in['b2']}

def reference(x, ctx_1024, L0_attn_W_K, L0_attn_W_V, L0_attn_W1, L0_attn_W2, L0_attn_m1, L0_attn_m2, L0_xattn_Wq, L0_xattn_bq, L0_xattn_Wk, L0_xattn_bk, L0_xattn_Wv, L0_xattn_bv, L0_ffn_Wqkv, L0_ffn_q_scale, L0_ffn_k_scale, L0_ffn_Wo, L0_ffn_ln_g, L0_ffn_ln_b, L0_ffn_W1, L0_ffn_b1, L0_ffn_W2, L0_ffn_b2):
    import jax
    import jax.numpy as jnp

    def _L0_attn_ref(x, W_K, W_V, W1, W2, m1, m2):
        import jax, jax.numpy as jnp
        import numpy as np
        from jax.scipy.special import erf
        INV_SQRT2 = 0.7071067811865476
        INV_SQRT2PI = 0.3989422804014327
        ETA, BETA, ALPHA = (0.1, 0.9, 0.99)

        def gelu(x):
            return 0.5 * x * (1.0 + erf(x * INV_SQRT2))

        def gelu_grad(x):
            cdf = 0.5 * (1.0 + erf(x * INV_SQRT2))
            pdf = jnp.exp(-0.5 * x * x) * INV_SQRT2PI
            return cdf + x * pdf

        def _reference_tuple_inner(x, W_K, W_V, W1, W2, m1, m2):
            B, T, H = x.shape
            denom = B * H
            K = jnp.einsum('bth,kh->btk', x, W_K)
            V = jnp.einsum('bth,vh->btv', x, W_V)
            reads = jnp.einsum('btd,hd->bth', gelu(jnp.einsum('btk,dk->btd', K, W1)), W2)
            assoc_losses = jnp.mean((reads - V) ** 2, axis=(0, 2))

            def step(carry, kv):
                W1c, W2c, m1c, m2c = carry
                k_t, v_t = kv
                h = k_t @ W1c.T
                a = gelu(h)
                pred = a @ W2c.T
                dpred = 2.0 / denom * (pred - v_t)
                g2 = dpred.T @ a
                dh = dpred @ W2c * gelu_grad(h)
                g1 = dh.T @ k_t
                n1 = jnp.linalg.norm(g1)
                n2 = jnp.linalg.norm(g2)
                surprise = 0.5 * (n1 + n2)
                g1 = jnp.where(n1 > 1.0, g1 / n1, g1)
                g2 = jnp.where(n2 > 1.0, g2 / n2, g2)
                m1n = BETA * m1c - ETA * g1
                m2n = BETA * m2c - ETA * g2
                W1n = ALPHA * W1c + m1n
                W2n = ALPHA * W2c + m2n
                return ((W1n, W2n, m1n, m2n), surprise)
            Kt = jnp.swapaxes(K, 0, 1)
            Vt = jnp.swapaxes(V, 0, 1)
            (W1f, W2f, m1f, m2f), surprises = jax.lax.scan(step, (W1, W2, m1, m2), (Kt, Vt))
            return (reads, surprises, assoc_losses, W1f, W2f)
        return _reference_tuple_inner(x, W_K, W_V, W1, W2, m1, m2)[0]

    def _L0_xattn_ref(q_in, k_v, Wq, bq, Wk, bk, Wv, bv):
        import jax, jax.numpy as jnp
        import numpy as np
        EMBED = 256
        B, I, J = (8, 512, 512)
        SCALE = EMBED ** (-0.5)
        q = q_in @ Wq + bq
        k = k_v @ Wk + bk
        v = k_v @ Wv + bv
        sim = jnp.einsum('bid,bjd->bij', q, k) * SCALE
        attn = jax.nn.softmax(sim, axis=-1)
        out = jnp.einsum('bij,bjd->bid', attn, v)
        return out

    def _L0_ffn_ref(x, Wqkv, q_scale, k_scale, Wo, ln_g, ln_b, W1, b1, W2, b2):
        import jax, jax.numpy as jnp
        import numpy as np
        DIM = 256
        DEPTH = 6
        HEADS = 16
        DIM_HEAD = 64
        WINDOW = 64
        INNER = HEADS * DIM_HEAD
        DIM_INNER = int(DIM * 4 * 2 / 3)
        QK_SCALE = 8.0

        def shift_tokens(t):
            a, s = jnp.split(t, 2, -1)
            s = jnp.pad(s, ((0, 0), (1, 0), (0, 0)))[:, :-1]
            return jnp.concatenate([a, s], -1)

        def l2norm(t):
            return t / jnp.maximum(jnp.linalg.norm(t, axis=-1, keepdims=True), 1e-12)

        def rotate_half(x):
            x1, x2 = jnp.split(x, 2, -1)
            return jnp.concatenate([-x2, x1], -1)

        def rotary_tables(n):
            half = jnp.arange(0, DIM_HEAD, 2, dtype=jnp.float32)
            inv_freq = 1.0 / 10000.0 ** (half / DIM_HEAD)
            t = jnp.arange(n, dtype=jnp.float32)
            freqs = t[:, None] * inv_freq[None, :]
            freqs = jnp.concatenate([freqs, freqs], -1)
            base_scale = (half + 0.4 * DIM_HEAD) / (1.4 * DIM_HEAD)
            power = (t - n // 2) / (WINDOW // 2)
            scale = base_scale[None, :] ** power[:, None]
            scale = jnp.concatenate([scale, scale], -1)
            return (freqs, scale)

        def local_attention(q, k, v):
            b, h, n, d = q.shape
            w = WINDOW
            nw = n // w
            bq = q.reshape(b, h, nw, w, d)
            bk = k.reshape(b, h, nw, w, d)
            bv = v.reshape(b, h, nw, w, d)

            def look(t):
                p = jnp.pad(t, ((0, 0), (0, 0), (1, 0), (0, 0), (0, 0)))
                return jnp.concatenate([p[:, :, :nw], p[:, :, 1:]], axis=3)
            bk2, bv2 = (look(bk), look(bv))
            seq = jnp.arange(n).reshape(nw, w)
            seq_p = jnp.pad(seq, ((1, 0), (0, 0)), constant_values=-1)
            jt = jnp.concatenate([seq_p[:nw], seq_p[1:]], axis=1)
            it = seq[:, :, None]
            jb = jt[:, None, :]
            mask = (it < jb) | (it > jb + w) | (jb == -1)
            sim = jnp.einsum('bhwie,bhwje->bhwij', bq, bk2) * QK_SCALE
            sim = jnp.where(mask, -jnp.finfo(sim.dtype).max, sim)
            attn = jax.nn.softmax(sim, -1)
            out = jnp.einsum('bhwij,bhwje->bhwie', attn, bv2)
            return out.reshape(b, h, n, d)

        def attn_layer(x, Wqkv, qs, ksc, Wo):
            b, n, _ = x.shape
            qkv = x @ Wqkv
            q, k, v = jnp.split(qkv, 3, -1)
            sh = lambda t: t.reshape(b, n, HEADS, DIM_HEAD).transpose(0, 2, 1, 3)
            q, k, v = (sh(q), sh(k), sh(v))
            q = l2norm(q) * qs
            k = l2norm(k) * ksc
            freqs, scale = rotary_tables(n)
            cos, sin = (jnp.cos(freqs), jnp.sin(freqs))
            q = q * cos * scale + rotate_half(q) * sin * scale
            inv = 1.0 / scale
            k = k * cos * inv + rotate_half(k) * sin * inv
            out = local_attention(q, k, v)
            out = out.transpose(0, 2, 1, 3).reshape(b, n, INNER)
            return out @ Wo

        def ffn_layer(x, g, bln, W1, b1, W2, b2):
            mu = x.mean(-1, keepdims=True)
            var = ((x - mu) ** 2).mean(-1, keepdims=True)
            xn = (x - mu) / jnp.sqrt(var + 1e-05) * g + bln
            hg = xn @ W1 + b1
            a, gate = jnp.split(hg, 2, -1)
            return a * jax.nn.gelu(gate, approximate=False) @ W2 + b2
        for i in range(DEPTH):
            x = attn_layer(shift_tokens(x), Wqkv[i], q_scale[i], k_scale[i], Wo[i]) + x
            x = ffn_layer(shift_tokens(x), ln_g[i], ln_b[i], W1[i], b1[i], W2[i], b2[i]) + x
        return x
    x = x + _L0_attn_ref(_layernorm(x, axis=-1), L0_attn_W_K, L0_attn_W_V, L0_attn_W1, L0_attn_W2, L0_attn_m1, L0_attn_m2)
    x = x + _L0_xattn_ref(_layernorm(x, axis=-1), ctx_1024, L0_xattn_Wq, L0_xattn_bq, L0_xattn_Wk, L0_xattn_bk, L0_xattn_Wv, L0_xattn_bv)
    x = x + _L0_ffn_ref(_layernorm(x, axis=-1), L0_ffn_Wqkv, L0_ffn_q_scale, L0_ffn_k_scale, L0_ffn_Wo, L0_ffn_ln_g, L0_ffn_ln_b, L0_ffn_W1, L0_ffn_b1, L0_ffn_W2, L0_ffn_b2)
    return x

_drawn_inputs = setup_inputs


def setup_inputs(seed=0):
    import zlib

    import numpy as np

    out = dict(_drawn_inputs(seed))
    spreads = {'L0_attn_m1': (0.0, 0.1),
     'L0_attn_m2': (0.0, 0.1),
     'L0_xattn_bq': (0.0, 0.458),
     'L0_xattn_bk': (0.0, 0.8),
     'L0_xattn_bv': (0.0, 0.1),
     'L0_ffn_q_scale': (1.0, 0.6),
     'L0_ffn_k_scale': (1.0, 0.6),
     'L0_ffn_ln_g': (1.0, 0.6),
     'L0_ffn_ln_b': (0.0, 0.8),
     'L0_ffn_b1': (0.0, 0.491),
     'L0_ffn_b2': (0.0, 0.1)}
    factors = {}
    for name, (base, spread) in spreads.items():
        noise = np.random.default_rng([zlib.crc32(name.encode()), seed]).standard_normal(out[name].shape)
        drawn = base * np.exp(spread * noise) if base else spread * noise
        out[name] = jnp.asarray(drawn.astype(out[name].dtype))
    for name, factor in factors.items():
        out[name] = (out[name] * factor).astype(out[name].dtype)
    return out
```

```python
import concourse.bass as bass
from concourse import mybir
from contextlib import ExitStack

FP32 = mybir.dt.float32
FP32R = mybir.dt.float32r
ALU = mybir.AluOpType
ACT = mybir.ActivationFunctionType
AXIS_X = mybir.AxisListType.X

P = 128
BATCH, TOKENS, DIM = 8, 256, 256
TILES = TOKENS // P
HALVES = DIM // P
MEMORY = 64
DEPTH, HEADS, HEAD_DIM, WINDOW = 6, 16, 64, 64
INNER = HEADS * HEAD_DIM
FFN = int(DIM * 4 * 2 / 3)
FFN_TILES = (FFN + P - 1) // P
FFN_REST = FFN - (FFN_TILES - 1) * P
QK_SCALE = 8.0
EPS = 1e-5
NORM_FLOOR = 1e-24
MASKED = 1e30

STEPS = DEPTH * BATCH
PAIRS = HEADS // 2
GROUPS = 2
GROUP_HEADS = HEADS // GROUPS
GROUP = GROUP_HEADS * HEAD_DIM
W1_COLS = 2 * FFN + FFN_TILES * P - FFN
BAND0, BAND1 = P, P + WINDOW
BAND = BAND0 + BAND1
PROBS = P + WINDOW + BAND1

FILLS = 22
DVE_READS = 10
ROTATIONS = 8
WIDE_FILLS = 7
WEIGHT_BLOCKS = 5
WEIGHT_LOADS = (32, 64, 80, 96, 128)
UNIT_AT = (1, 2, 3, 5, 7, 9)
TRANSPOSE_AT = (4, 6, 8, 10)

SCHEDULE = {
    0: [("unit", 1, 0)],
    1: [("unit", 1, 1)],
    2: [("unit", 1, 2), ("turn", 1, 0)],
    3: [("project_out", 0)],
    4: [("project_out", 1)],
    5: [("unit", 1, 3), ("turn", 1, 1), ("norm",)],
    6: [("unit", 1, 4), ("turn", 1, 2)],
    7: [("unit", 1, 5), ("turn", 1, 3), ("norm_turn",)],
    8: [("input",), ("unit", 0, 0), ("gate", 0)],
    9: [("unit", 0, 1), ("gate", 1)],
    10: [("unit", 0, 2), ("turn", 0, 0), ("gate", 2)],
    11: [("unit", 0, 3), ("turn", 0, 1), ("gelu",), ("value", 0)],
    12: [("unit", 0, 4), ("turn", 0, 2), ("value", 1), ("down", 0)],
    13: [("unit", 0, 5), ("turn", 0, 3), ("value", 2), ("down", 1)],
    14: [("down", 2)],
    15: [("residual",)],
}


def wait(eng, semaphore, value):
    if not isinstance(value, int) or value > 0:
        eng.wait_ge(semaphore, value)


def wait_apart(eng, semaphore, value, passed):
    eng.wait_ge(semaphore, value)
    eng.sem_inc(passed, 1)


class Slot:

    def __init__(self, n, layer=0, attend=True, ffn=True, late=True, early=True,
                 late_layer=None, early_layer=None, switch=None, next_batch=None, ffn_batch=None):
        self.n, self.layer, self.attend, self.ffn, self.late, self.early = n, layer, attend, ffn, late, early
        self.late_layer = layer if late_layer is None else late_layer
        self.early_layer = layer if early_layer is None else early_layer
        self.switch = switch
        self.next_batch, self.ffn_batch = next_batch, ffn_batch

    def head(self, t, lag):
        if isinstance(self.n, int) and HEADS * self.n + t - lag < 0:
            return None
        if not self.attend and t >= lag:
            return None
        return HEADS * self.n + t - lag

    def dense(self, t):
        for item in SCHEDULE[t]:
            kind = item[0]
            if kind == "unit" or kind == "turn":
                if (self.late if item[1] else self.early):
                    yield item
            elif kind == "input":
                if self.early:
                    yield item
            elif self.ffn:
                yield item


def run_slots(eng, slot, before_layer=None):
    slot(Slot(-1, attend=False, ffn=False, late=False, next_batch=0))
    slot(Slot(0, ffn=False, next_batch=1))
    with eng.Fori(0, DEPTH - 1) as layer:
        if before_layer:
            before_layer(layer)
        with eng.Fori(1, BATCH - 1) as b:
            slot(Slot(layer * BATCH + b, layer, next_batch=b + 1, ffn_batch=b - 1))
        slot(Slot(layer * BATCH + (BATCH - 1), layer, early_layer=layer + 1, switch="projections",
                  next_batch=0, ffn_batch=BATCH - 2))
        slot(Slot(layer * BATCH + BATCH, layer, late_layer=layer + 1, early_layer=layer + 1,
                  switch="ffn", next_batch=1, ffn_batch=BATCH - 1))
    last = DEPTH - 1
    with eng.Fori(1, BATCH - 1) as b:
        slot(Slot(last * BATCH + b, last, next_batch=b + 1, ffn_batch=b - 1))
    slot(Slot(STEPS - 1, last, early=False, ffn_batch=BATCH - 2))
    slot(Slot(STEPS, last, attend=False, late=False, early=False, ffn_batch=BATCH - 1))


def front(nc, T, D, weights):
    with ExitStack() as ctx:
        def sb(name, shape, dt=FP32):
            return ctx.enter_context(nc.sbuf_tensor(name, shape, dt))

        def sem(name):
            return ctx.enter_context(nc.semaphore(name))

        DUO = 2
        wk_mem = sb("wk_mem", [P, HALVES, DIM])
        w1t_mem = sb("w1t_mem", [P, HALVES, MEMORY])
        hidden_w = sb("hidden_w", [P, HALVES, MEMORY])
        w2t_mem = sb("w2t_mem", [MEMORY, DIM])
        wq = sb("wq_cross", [P, HALVES, DIM])
        wk = sb("wk_cross", [P, HALVES, DIM])
        wv = sb("wv_cross", [P, HALVES, DIM])
        bqk = sb("bqk", [P, 2 * HALVES])
        bv = sb("bv", [P, DIM])
        x = [sb(f"x{j}", [P, TILES, DIM]) for j in range(DUO)]
        xn = [sb(f"xn{j}", [P, TILES, DIM]) for j in range(DUO)]
        xnT = [sb(f"xnT{j}", [P, HALVES, TOKENS]) for j in range(DUO)]
        ctxT = [sb(f"ctxT{j}", [P, HALVES, TOKENS]) for j in range(DUO)]
        hidT = [sb(f"hidT{j}", [MEMORY, TOKENS]) for j in range(DUO)]
        qT = [sb(f"fqT{j}", [P, HALVES, TOKENS]) for j in range(DUO)]
        kT = [sb(f"fkT{j}", [P, HALVES, TOKENS]) for j in range(DUO)]
        v = [sb(f"fv{j}", [P, TILES, DIM]) for j in range(DUO)]
        pr = [sb(f"fp{j}", [P, TILES, TOKENS]) for j in range(DUO)]
        prT = [sb(f"fpT{j}", [P, TILES, TOKENS]) for j in range(DUO)]
        yo = [sb(f"yo{j}", [P, TILES, DIM]) for j in range(DUO)]
        st = sb("fst", [P, TILES, 6])
        mv = sb("fmv", [P, TILES, 2])
        rstd = sb("frstd", [P, TILES])
        mx = [sb(f"fmx{j}", [P, TILES]) for j in range(DUO)]
        nb = [sb(f"fnb{j}", [P, TILES]) for j in range(DUO)]
        sm = [sb(f"fsm{j}", [P, TILES]) for j in range(DUO)]
        rs = [sb(f"frs{j}", [P, TILES]) for j in range(DUO)]
        bank = [[ctx.enter_context(nc.psum_tensor(f"fb{j}{i}", [P, 2, DIM], FP32)) for i in range(4)]
                for j in range(DUO)]

        weights_in = sem("f_weights_in")
        x_in, ctx_in = sem("f_x_in"), sem("f_ctx_in")
        folded_ready, folded = sem("f_folded_ready"), sem("f_folded")
        stats, moments, root, normed = sem("f_stats"), sem("f_moments"), sem("f_root"), sem("f_normed")
        pool_step = sem("f_pool_step")
        turned, turned_out = sem("f_turned"), sem("f_turned_out")
        hid_ready, hid_act = sem("f_hid_ready"), sem("f_hid_act")
        read_ready, read_added = sem("f_read_ready"), sem("f_read_added")
        kv_ready, k_out, v_out = sem("f_kv_ready"), sem("f_k_out"), sem("f_v_out")
        q_ready, q_out = sem("f_q_ready"), sem("f_q_out")
        score_ready, top, shift = sem("f_score_ready"), sem("f_top"), sem("f_shift")
        probs, inverse = sem("f_probs"), sem("f_inverse")
        probs_turned, probs_out = sem("f_probs_turned"), sem("f_probs_out")
        cross_ready, cross_added = sem("f_cross_ready"), sem("f_cross_added")
        x2_stored, y_stored = sem("f_x2_stored"), sem("f_y_stored")
        passed = sem("f_passed")
        block = ctx.enter_context(nc.Block())
        ident = T["ident"]
        DUOS = BATCH // DUO

        def as_tiles(seq):
            return seq.rearrange("(t p) d -> p t d", p=P)

        def ln_index(i, s, j):
            return i * (3 * DUO) + s * DUO + j

        @block.sync
        def _(sp):
            sp.dma_start(T["ident"][:], D["ident"]).then_inc(weights_in, 16)
            sp.dma_start(T["mask"][:], D["mask"]).then_inc(weights_in, 16)
            sp.dma_start(T["rope"][:], D["rope"]).then_inc(weights_in, 16)
            for dst, src in ((wk_mem, "mem_wk"), (w1t_mem, "mem_w1t"), (wq, "cross_wq"), (wk, "cross_wk"), (wv, "cross_wv")):
                sp.dma_start(dst[:], D[src].rearrange("(k p) n -> p k n", p=P)).then_inc(weights_in, 16)
            sp.dma_start(w2t_mem[:], D["mem_w2t"]).then_inc(weights_in, 16)
            sp.dma_start(bqk[:], D["cross_bqk"]).then_inc(weights_in, 16)
            sp.dma_start(bv[:], D["cross_bv"].broadcast_to([P, DIM])).then_inc(weights_in, 16)
            for j in range(DUO):
                sp.dma_start(x[j][:], as_tiles(D["x"][j])).then_inc(x_in, 16)
                sp.dma_start(ctxT[j][:], D["ctxT"][j].rearrange("(k p) t -> p k t", p=P)).then_inc(ctx_in, 16)
                sp.wait_ge(x_in, 16 * (j + 1))
            def store(k, j, i):
                sp.wait_ge(cross_added, k + 1)
                sp.dma_start(as_tiles(D["x2"][k]), x[j][:]).then_inc(x2_stored, 16)
                sp.wait_ge(normed, ln_index(i, 2, j) + 1)
                sp.dma_start(as_tiles(D["y"][k]), yo[j][:]).then_inc(y_stored, 16)
                sp.wait_ge(x2_stored, (k + 1) * 16)
                sp.wait_ge(y_stored, (k + 1) * 16)

            with sp.Fori(0, DUOS - 1) as i:
                for j in range(DUO):
                    k = i * DUO + j
                    store(k, j, i)
                    sp.dma_start(x[j][:], as_tiles(D["x"][k + DUO])).then_inc(x_in, 16)
                    sp.dma_start(ctxT[j][:], D["ctxT"][k + DUO].rearrange("(k p) t -> p k t", p=P)).then_inc(ctx_in, 16)
            for j in range(DUO):
                store(BATCH - DUO + j, j, DUOS - 1)

        @block.tensor
        def _(pe):
            pe.wait_ge(weights_in, 16 * 11)
            for h in range(HALVES):
                for k in range(HALVES):
                    last = pe.matmul(bank[0][1][:, h, 0:MEMORY], wk_mem[:, k, h * P:(h + 1) * P], w1t_mem[:, k, :],
                                     start=(k == 0), stop=(k == HALVES - 1))
            last.then_inc(folded_ready, 1)
            pe.wait_ge(folded, 1)

            def turn(i, s, j):
                pe.wait_ge(normed, ln_index(i, s, j) + 1)
                for h in range(HALVES):
                    for t in range(TILES):
                        last = pe.transpose(bank[j][0][:, h, t * P:(t + 1) * P], xn[j][:, t, h * P:(h + 1) * P], ident[:])
                last.then_inc(turned, 1)

            with pe.Fori(0, DUOS) as i:
                for j in range(DUO):
                    turn(i, 0, j)
                for j in range(DUO):
                    pe.wait_ge(turned_out, (i * 2 + 0) * DUO + j + 1)
                    for h in range(HALVES):
                        last = pe.matmul(bank[j][1][0:MEMORY, 0, :], hidden_w[:, h, :], xnT[j][:, h, :],
                                         start=(h == 0), stop=(h == HALVES - 1))
                    last.then_inc(hid_ready, 1)
                for j in range(DUO):
                    pe.wait_ge(hid_act, i * DUO + j + 1)
                    for t in range(TILES):
                        last = pe.matmul(bank[j][2][:, t, :], hidT[j][:, t * P:(t + 1) * P], w2t_mem[:],
                                         start=True, stop=True)
                    last.then_inc(read_ready, 1)
                for j in range(DUO):
                    pe.wait_ge(ctx_in, (i * DUO + j + 1) * 16)
                    for m in range(HALVES):
                        for h in range(HALVES):
                            last = pe.matmul(bank[j][3][:, m, :], wk[:, h, m * P:(m + 1) * P], ctxT[j][:, h, :],
                                             start=(h == 0), stop=(h == HALVES - 1))
                    last.then_inc(kv_ready, 1)
                for j in range(DUO):
                    turn(i, 1, j)
                for j in range(DUO):
                    pe.wait_ge(k_out, i * DUO + j + 1)
                    for t in range(TILES):
                        for h in range(HALVES):
                            last = pe.matmul(bank[j][3][:, t, :], ctxT[j][:, h, t * P:(t + 1) * P], wv[:, h, :],
                                             start=(h == 0), stop=(h == HALVES - 1))
                    last.then_inc(kv_ready, 1)
                for j in range(DUO):
                    pe.wait_ge(turned_out, (i * 2 + 1) * DUO + j + 1)
                    for m in range(HALVES):
                        for h in range(HALVES):
                            last = pe.matmul(bank[j][1][:, m, :], wq[:, h, m * P:(m + 1) * P], xnT[j][:, h, :],
                                             start=(h == 0), stop=(h == HALVES - 1))
                    last.then_inc(q_ready, 1)
                for j in range(DUO):
                    pe.wait_ge(q_out, i * DUO + j + 1)
                    for t in range(TILES):
                        for h in range(HALVES):
                            last = pe.matmul(bank[j][1][:, t, :], qT[j][:, h, t * P:(t + 1) * P], kT[j][:, h, :],
                                             start=(h == 0), stop=(h == HALVES - 1))
                    last.then_inc(score_ready, 1)
                for j in range(DUO):
                    pe.wait_ge(probs, i * DUO + j + 1)
                    for kt in range(TILES):
                        for t in range(TILES):
                            last = pe.transpose(bank[j][0][:, kt, t * P:(t + 1) * P], pr[j][:, t, kt * P:(kt + 1) * P], ident[:])
                    last.then_inc(probs_turned, 1)
                for j in range(DUO):
                    pe.wait_ge(probs_out, i * DUO + j + 1)
                    pe.wait_ge(v_out, i * DUO + j + 1)
                    for t in range(TILES):
                        for kt in range(TILES):
                            last = pe.matmul(bank[j][2][:, t, :], prT[j][:, kt, t * P:(t + 1) * P], v[j][:, kt, :],
                                             start=(kt == 0), stop=(kt == TILES - 1))
                    last.then_inc(cross_ready, 1)

        @block.scalar
        def _(act):
            with act.Fori(0, DUOS) as i:
                for j in range(DUO):
                    act.wait_ge(turned, (i * 2 + 0) * DUO + j + 1)
                    act.copy(xnT[j][:], bank[j][0][:]).then_inc(turned_out, 1)
                for j in range(DUO):
                    act.wait_ge(hid_ready, i * DUO + j + 1)
                    act.activation(hidT[j][:], bank[j][1][0:MEMORY, 0, :], ACT.Gelu).then_inc(hid_act, 1)
                for j in range(DUO):
                    act.wait_ge(turned, (i * 2 + 1) * DUO + j + 1)
                    act.copy(xnT[j][:], bank[j][0][:]).then_inc(turned_out, 1)
                for j in range(DUO):
                    act.wait_ge(shift, i * DUO + j + 1)
                    for t in range(TILES):
                        last = act.activation(pr[j][:, t, :], bank[j][1][:, t, :], ACT.Exp, bias=nb[j][:, t:t + 1],
                                              scale=DIM ** -0.5, accum_out=sm[j][:, t:t + 1])
                    last.then_inc(probs, 1)
                for j in range(DUO):
                    act.wait_ge(probs_turned, i * DUO + j + 1)
                    act.copy(prT[j][:], bank[j][0][:]).then_inc(probs_out, 1)

        @block.gpsimd
        def _(pool):
            nc.gpsimd.memset(T["half"][:], -0.5).then_inc(pool_step, 1)
            pool.wait_ge(pool_step, 1)
            with pool.Fori(0, DUOS) as i:
                for s in range(3):
                    for j in range(DUO):
                        k = ln_index(i, s, j)
                        wait_apart(pool, moments, k + 1, passed)
                        pool.tensor_scalar(mv[:, :, 1], mv[:, :, 1], EPS, None, ALU.add).then_inc(pool_step, 1)
                        pool.wait_ge(pool_step, k + 2)
                        pool.tensor_tensor(rstd[:], mv[:, :, 1], T["half"][:, 0:TILES], ALU.pow).then_inc(root, 1)

        @block.vector
        def _(dve):
            dve.wait_ge(folded_ready, 1)
            dve.tensor_copy(hidden_w[:], bank[0][1][:, :, 0:MEMORY]).then_inc(folded, 1)

            def layer_norm(i, s, j, source, out):
                k = ln_index(i, s, j)
                for t in range(TILES):
                    last = dve.bn_stats(st[:, t, :], source[:, t, :])
                last.then_inc(stats, 1)
                wait_apart(dve, stats, k + 1, passed)
                for t in range(TILES):
                    last = dve.bn_aggr(mv[:, t, :], st[:, t, :])
                last.then_inc(moments, 1)
                dve.wait_ge(root, k + 1)
                for t in range(TILES):
                    last = dve.tensor_scalar(out[:, t, :], source[:, t, :], mv[:, t, 0:1], rstd[:, t:t + 1],
                                             ALU.subtract, ALU.mult)
                last.then_inc(normed, 1)

            with dve.Fori(0, DUOS) as i:
                for j in range(DUO):
                    dve.wait_ge(x_in, (i * DUO + j + 1) * 16)
                    layer_norm(i, 0, j, x[j], xn[j])
                for j in range(DUO):
                    dve.wait_ge(read_ready, i * DUO + j + 1)
                    dve.tensor_tensor(x[j][:], bank[j][2][:], x[j][:], ALU.add).then_inc(read_added, 1)
                for j in range(DUO):
                    dve.wait_ge(read_added, i * DUO + j + 1)
                    layer_norm(i, 1, j, x[j], xn[j])
                for j in range(DUO):
                    dve.wait_ge(kv_ready, i * (2 * DUO) + j + 1)
                    for m in range(HALVES):
                        last = dve.tensor_scalar(kT[j][:, m, :], bank[j][3][:, m, :], bqk[:, HALVES + m:HALVES + m + 1],
                                                 None, ALU.add)
                    last.then_inc(k_out, 1)
                for j in range(DUO):
                    dve.wait_ge(kv_ready, i * (2 * DUO) + DUO + j + 1)
                    dve.tensor_tensor(v[j][:], bank[j][3][:], bv[:].unsqueeze(1).broadcast_to([P, TILES, DIM]),
                                      ALU.add).then_inc(v_out, 1)
                for j in range(DUO):
                    dve.wait_ge(q_ready, i * DUO + j + 1)
                    for m in range(HALVES):
                        last = dve.tensor_scalar(qT[j][:, m, :], bank[j][1][:, m, :], bqk[:, m:m + 1], None, ALU.add)
                    last.then_inc(q_out, 1)
                for j in range(DUO):
                    k = i * DUO + j
                    dve.wait_ge(score_ready, k + 1)
                    dve.tensor_reduce(mx[j][:], bank[j][1][:], AXIS_X, ALU.max).then_inc(top, 1)
                    dve.wait_ge(top, k + 1)
                    dve.tensor_scalar(nb[j][:], mx[j][:], -(DIM ** -0.5), None, ALU.mult).then_inc(shift, 1)
                for j in range(DUO):
                    dve.wait_ge(probs, i * DUO + j + 1)
                    dve.reciprocal(rs[j][:], sm[j][:]).then_inc(inverse, 1)
                for j in range(DUO):
                    k = i * DUO + j
                    dve.wait_ge(cross_ready, k + 1)
                    dve.wait_ge(inverse, k + 1)
                    for t in range(TILES):
                        last = dve.scalar_tensor_tensor(x[j][:, t, :], bank[j][2][:, t, :], rs[j][:, t:t + 1],
                                                        x[j][:, t, :], ALU.mult, ALU.add)
                    last.then_inc(cross_added, 1)
                for j in range(DUO):
                    dve.wait_ge(cross_added, i * DUO + j + 1)
                    layer_norm(i, 2, j, x[j], yo[j])


def layers(nc, T, D):
    with ExitStack() as ctx:
        def sb(name, shape, dt=FP32):
            return ctx.enter_context(nc.sbuf_tensor(name, shape, dt))

        def sem(name):
            return ctx.enter_context(nc.semaphore(name))

        w_qkv = [sb(f"w_qkv{s}", [P, HALVES, 3, GROUPS, GROUP], FP32R) for s in range(2)]
        w_out = [sb(f"w_out{s}", [P, PAIRS, DIM], FP32R) for s in range(2)]
        w_up = [sb(f"w_up{s}", [P, HALVES, W1_COLS], FP32R) for s in range(2)]
        w_down = [sb(f"w_down{s}", [P, FFN_TILES, DIM], FP32R) for s in range(2)]
        staging = sb("staging", [P, HALVES * 3 * GROUP])
        params = sb("params", [P, 2 * FFN_TILES + 2 * HALVES])
        b_down = sb("b_down", [P, DIM])
        qk_scales = sb("qk_scales", [P, 2, 2, HEAD_DIM // 2])
        tables = sb("tables", [P, 4, TILES, HEAD_DIM])

        y_in = sb("y_in", [P, TILES, DIM])
        xT = [sb(f"xT{s}", [P, HALVES, TOKENS + 2], FP32R) for s in range(2)]
        square = sb("square", [P, GROUP])
        sums_sq = sb("sums_sq", [P, 2, GROUP_HEADS])
        inv_norm = sb("inv_norm", [P, 2, GROUP_HEADS])
        query_scale = sb("query_scale", [P, TILES, HEADS])
        with_cos = sb("with_cos", [P, 2, GROUP])
        with_sin = sb("with_sin", [P, 2, GROUP])
        qT = sb("qT", [P, PAIRS, TOKENS])
        kT = sb("kT", [P, PAIRS, TOKENS])
        v = sb("v", [P, TILES, INNER])

        masked = sb("masked", [P, 2, BAND])
        shift = sb("shift", [P, 2, TILES])
        sums = sb("sums", [P, 4, TILES])
        inv_sums = sb("inv_sums", [P, 4, TILES])
        probs = sb("probs", [P, 4, PROBS])
        probsT = sb("probsT", [P, 2, BAND])
        oT = [sb(f"oT{s}", [P, PAIRS, TOKENS], FP32R) for s in range(2)]

        res = sb("res", [P, TILES, DIM])
        late_half = sb("late_half", [P, TILES, P])
        ln_stats = sb("ln_stats", [P, TILES, HALVES, 6])
        ln_mv = sb("ln_mv", [P, TILES, 2])
        ln_rstd = sb("ln_rstd", [P, TILES])
        xn = sb("xn", [P, TILES, DIM])
        xnT = [sb(f"nT{s}", [P, HALVES, TOKENS], FP32R) for s in range(2)]
        gates = sb("gates", [P, FFN_TILES, TOKENS])
        hT = [sb(f"hT{s}", [P, 2, TOKENS], FP32R) for s in range(2)]

        project = [ctx.enter_context(nc.psum_tensor(f"project{i}", [P, GROUP], FP32)) for i in range(2)]
        score = [ctx.enter_context(nc.psum_tensor(f"score{i}", [P, GROUP], FP32)) for i in range(2)]
        turned = ctx.enter_context(nc.psum_tensor("turned", [P, GROUP], FP32))
        mix = ctx.enter_context(nc.psum_tensor("mix", [P, 2, TOKENS], FP32))
        wide = ctx.enter_context(nc.psum_tensor("wide", [P, 2, TOKENS], FP32))
        acc = ctx.enter_context(nc.psum_tensor("acc", [P, TILES, DIM], FP32))

        w_loaded, w_high, w_low = sem("w_loaded"), sem("w_high"), sem("w_low")
        params_loaded, scales_loaded, tables_built = sem("params_loaded"), sem("scales_loaded"), sem("tables_built")
        cleared = sem("cleared")
        y_loaded, res_loaded, y_stored = sem("y_loaded"), sem("res_loaded"), sem("y_stored")
        filled, act_read, dve_read = sem("filled"), sem("act_read"), sem("dve_read")
        squares_summed, rotated, pool_step = sem("squares_summed"), sem("rotated"), sem("pool_step")
        scores_ready, scores_masked, exp_done = sem("scores_ready"), sem("scores_masked"), sem("exp_done")
        sums_inverted, probs_scaled = sem("sums_inverted"), sem("probs_scaled")
        probs_turned, probsT_copied, mixed = sem("probs_turned"), sem("probsT_copied"), sem("mixed")
        out_high, out_split = sem("out_high"), sem("out_split")
        attn_projected, acc_read, shifted = sem("attn_projected"), sem("acc_read"), sem("shifted")
        ln_stated, ln_moments, ln_root, ln_done = sem("ln_stated"), sem("ln_moments"), sem("ln_root"), sem("ln_done")
        ln_floor = sem("ln_floor")
        wide_filled, wide_read = sem("wide_filled"), sem("wide_read")
        xn_high, xn_low, gelu_done = sem("xn_high"), sem("xn_low"), sem("gelu_done")
        h_high, h_low, h_used, res_ready = sem("h_high"), sem("h_low"), sem("h_used"), sem("res_ready")
        final_in, final_added, final_out = sem("final_in"), sem("final_added"), sem("final_out")
        passed = sem("passed")
        block = ctx.enter_context(nc.Block())
        ident, mask, rope, half = T["ident"], T["mask"], T["rope"], T["half"]

        def as_tiles(seq):
            return seq.rearrange("(t p) d -> p t d", p=P)

        def unit_fill(m, g, u):
            return m * FILLS + (2 + 10 * g + UNIT_AT[u])

        def turn_fill(m, g, u):
            return m * FILLS + (2 + 10 * g + TRANSPOSE_AT[u])

        def unit_read(m, g, u):
            return m * DVE_READS + (2 + 4 * g + u + 1)

        def rotation(m, g, u):
            return m * ROTATIONS + (4 * g + u + 1)

        def last_use(blk, layer):
            m = layer * BATCH
            return [(filled, m * FILLS - FILLS + (2 + UNIT_AT[5])), (filled, m * FILLS - FILLS + (12 + UNIT_AT[5])),
                    (attn_projected, m), (wide_filled, m * WIDE_FILLS), (h_used, m * 3 + 1)][blk]

        def split_views(blk):
            if blk < 2:
                s = staging[:].rearrange("p (k c n) -> p k c n", k=HALVES, c=3)
                return [(s[:, k], w_qkv[0][:, k, :, blk, :], w_qkv[1][:, k, :, blk, :]) for k in range(HALVES)]
            if blk == 2:
                s = staging[:, 0:PAIRS * DIM].rearrange("p (k n) -> p k n", k=PAIRS)
                return [(s, w_out[0][:], w_out[1][:])]
            if blk == 3:
                s = staging[:, 0:HALVES * 2 * FFN].rearrange("p (k n) -> p k n", k=HALVES)
                return [(s, w_up[0][:, :, 0:2 * FFN], w_up[1][:, :, 0:2 * FFN])]
            s = staging[:, 0:FFN_TILES * DIM].rearrange("p (k n) -> p k n", k=FFN_TILES)
            return [(s[:, 0:FFN_TILES - 1], w_down[0][:, 0:FFN_TILES - 1], w_down[1][:, 0:FFN_TILES - 1]),
                    (s[0:FFN_REST, FFN_TILES - 1], w_down[0][0:FFN_REST, FFN_TILES - 1], w_down[1][0:FFN_REST, FFN_TILES - 1])]

        @block.sync
        def _(sp):
            def stage(blk, layer):
                wait(sp, w_low, layer * WEIGHT_BLOCKS + blk)
                if blk < 2:
                    src = D["w_qkv"][layer].rearrange("(k p) (c g n) -> k p c g n", p=P, c=3, g=GROUPS)
                    dst = staging[:].rearrange("p (k c n) -> p k c n", k=HALVES, c=3)
                    for k in range(HALVES):
                        sp.dma_start(dst[:, k], src[k, :, :, blk, :]).then_inc(w_loaded, 16)
                elif blk == 2:
                    sp.dma_start(staging[:, 0:PAIRS * DIM].rearrange("p (k n) -> p k n", k=PAIRS),
                                 D["w_out"][layer].rearrange("(k p) n -> p k n", p=P)).then_inc(w_loaded, 16)
                elif blk == 3:
                    sp.dma_start(staging[:, 0:HALVES * 2 * FFN].rearrange("p (k n) -> p k n", k=HALVES),
                                 D["w_up"][layer].rearrange("(k p) n -> p k n", p=P)).then_inc(w_loaded, 16)
                else:
                    full = (FFN_TILES - 1) * P
                    dst = staging[:, 0:FFN_TILES * DIM].rearrange("p (k n) -> p k n", k=FFN_TILES)
                    sp.dma_start(dst[:, 0:FFN_TILES - 1],
                                 D["w_down"][layer][0:full, :].rearrange("(k p) n -> p k n", p=P)).then_inc(w_loaded, 16)
                    sp.dma_start(dst[0:FFN_REST, FFN_TILES - 1], D["w_down"][layer][full:FFN, :]).then_inc(w_loaded, 16)

            def load_scales(layer):
                wait(sp, tables_built, layer)
                sp.dma_start(qk_scales[:], D["qk_scales"][layer].rearrange("(a b c) -> a b c", a=2, b=2).unsqueeze(0)
                             .broadcast_to([P, 2, 2, HEAD_DIM // 2])).then_inc(scales_loaded, 16)

            def load_params(layer):
                wait(sp, acc_read, layer * (2 * BATCH) + 1)
                sp.dma_start(params[:], D["params"][layer]).then_inc(params_loaded, 16)
                sp.dma_start(b_down[:], D["b_down"][layer].unsqueeze(0).broadcast_to([P, DIM])).then_inc(params_loaded, 16)

            def slot(s):
                n = s.n
                f = n - 1
                if s.early:
                    wait(sp, filled, n * FILLS + 2)
                    sp.dma_start(y_in[:], as_tiles(D["y"][s.next_batch])).then_inc(y_loaded, 16)
                if isinstance(n, int) and n == -1:
                    load_scales(0)
                    load_params(0)
                    for blk in range(WEIGHT_BLOCKS):
                        stage(blk, 0)
                if s.ffn:
                    wait(sp, y_stored, f * 16 + 1)
                    sp.dma_start(res[:], as_tiles(D["y"][s.ffn_batch])).then_inc(res_loaded, 16)
                    wait(sp, acc_read, f * 2 + 1 + 1)
                    wait(sp, ln_done, f + 1)
                    sp.dma_start(late_half[1:P, :, :], res[0:P - 1, :, P:DIM]).then_inc(shifted, 16)
                    sp.dma_start(late_half[0:1, 1, :], res[P - 1:P, 0, P:DIM]).then_inc(shifted, 16)
                if s.switch == "projections":
                    stage(1, s.layer + 1)
                    stage(2, s.layer + 1)
                if s.switch == "ffn":
                    stage(3, s.layer + 1)
                if s.ffn:
                    wait(sp, acc_read, f * 2 + 2 + 1)
                    sp.dma_start(as_tiles(D["y"][s.ffn_batch]), res[:]).then_inc(y_stored, 16)
                if s.switch == "ffn":
                    load_params(s.layer + 1)
                    stage(4, s.layer + 1)

            def before_layer(layer):
                stage(0, layer + 1)
                load_scales(layer + 1)

            sp.sem_inc(y_stored, 1)
            sp.sem_inc(final_out, 1)
            run_slots(sp, slot, before_layer)
            sp.wait_ge(y_stored, STEPS * 16 + 1)
            with sp.Fori(0, BATCH) as b:
                sp.wait_ge(final_out, b * 16 + 1)
                sp.dma_start(y_in[:], as_tiles(D["y"][b])).then_inc(final_in, 16)
                sp.dma_start(res[:], as_tiles(D["x2"][b])).then_inc(final_in, 16)
                sp.wait_ge(final_added, b + 1)
                sp.dma_start(as_tiles(D["out"][b]), res[:]).then_inc(final_out, 16)
            sp.wait_ge(final_out, BATCH * 16 + 1)

        @block.tensor
        def _(pe):
            PASSES = ((0, 0), (1, 0), (0, 1))

            def bank_free(x, m):
                y = x - 2
                step = m
                if y <= 0:
                    y, step = y + FILLS, m - 1
                if isinstance(step, int) and step < 0:
                    return
                wait(pe, act_read, step * FILLS + y)
                reads = {1: 1, 2: 2}
                for g in range(GROUPS):
                    for u in range(4):
                        reads[2 + 10 * g + UNIT_AT[u]] = 2 + 4 * g + u + 1
                if y in reads:
                    wait(pe, dve_read, step * DVE_READS + reads[y])

            def dense(s, item):
                n, kind = s.n, item[0]
                f = n - 1
                if kind == "input":
                    m = n + 1
                    pe.wait_ge(y_loaded, m * 16 + 16)
                    for h in range(HALVES):
                        bank_free(h + 1, m)
                        for t in range(TILES):
                            last = pe.transpose(project[h][:, t * P:(t + 1) * P], y_in[:, t, h * P:(h + 1) * P], ident[:])
                        last.then_inc(filled, 1)
                elif kind == "unit":
                    g, u = item[1:]
                    m = n if g else n + 1
                    c, t = (u % 2, u // 2) if u < 4 else (2, u - 4)
                    if u == 0:
                        pe.wait_ge(w_low, (s.late_layer if g else s.early_layer) * WEIGHT_BLOCKS + (g + 1))
                        pe.wait_ge(act_read, m * FILLS + 2)
                        pe.wait_ge(dve_read, m * DVE_READS + 2)
                    x = 2 + 10 * g + UNIT_AT[u]
                    bank_free(x, m)
                    for h in range(HALVES):
                        for a, w in PASSES:
                            last = pe.matmul(project[(x - 1) % 2][:], xT[a][:, h, t * P:(t + 1) * P], w_qkv[w][:, h, c, g, :],
                                             start=(h == 0 and (a, w) == PASSES[0]), stop=(h == HALVES - 1 and (a, w) == PASSES[-1]))
                    last.then_inc(filled, 1)
                elif kind == "turn":
                    g, u = item[1:]
                    m = n if g else n + 1
                    x = 2 + 10 * g + TRANSPOSE_AT[u]
                    pe.wait_ge(rotated, rotation(m, g, u))
                    bank_free(x, m)
                    for p in range(4):
                        last = pe.transpose(project[(x - 1) % 2][:, p * P:(p + 1) * P], with_cos[:, u % 2, p * P:(p + 1) * P], ident[:])
                    last.then_inc(filled, 1)
                elif kind == "project_out":
                    t = item[1]
                    if t == 0:
                        pe.wait_ge(w_low, s.layer * WEIGHT_BLOCKS + 3)
                        pe.wait_ge(out_split, f * PAIRS + PAIRS)
                        wait(pe, acc_read, f * 2 + 1)
                    for p in range(PAIRS):
                        for a, w in PASSES:
                            last = pe.matmul(acc[:, t, :], oT[a][:, p, t * P:(t + 1) * P], w_out[w][:, p, :],
                                             start=(p == 0 and (a, w) == PASSES[0]), stop=(p == PAIRS - 1 and (a, w) == PASSES[-1]))
                    if t == TILES - 1:
                        last.then_inc(attn_projected, 1)
                elif kind == "norm_turn":
                    pe.wait_ge(ln_done, f + 1 + 1)
                    wait(pe, wide_read, f * WIDE_FILLS + 1)
                    for h in range(HALVES):
                        for t in range(TILES):
                            last = pe.transpose(wide[:, h, t * P:(t + 1) * P], xn[:, t, h * P:(h + 1) * P], ident[:])
                    last.then_inc(wide_filled, 1)
                elif kind in ("gate", "value"):
                    i = item[1]
                    x = 2 + i if kind == "gate" else 5 + i
                    if x == 2:
                        pe.wait_ge(w_low, s.layer * WEIGHT_BLOCKS + 4)
                        pe.wait_ge(xn_low, f + 1)
                    pe.wait_ge(wide_read, f * WIDE_FILLS + x - 1 + 1)
                    for k in range(2):
                        col = (2 * i + k) * P + (FFN if kind == "gate" else 0)
                        for h in range(HALVES):
                            for a, w in PASSES:
                                last = pe.matmul(wide[:, k, :], w_up[w][:, h, col:col + P], xnT[a][:, h, :],
                                                 start=(h == 0 and (a, w) == PASSES[0]), stop=(h == HALVES - 1 and (a, w) == PASSES[-1]))
                    last.then_inc(wide_filled, 1)
                elif kind == "down":
                    i = item[1]
                    if i == 0:
                        pe.wait_ge(w_low, s.layer * WEIGHT_BLOCKS + 5)
                        pe.wait_ge(acc_read, f * 2 + 1 + 1)
                    pe.wait_ge(h_low, f * 3 + i + 1 + 1)
                    for k in range(2):
                        j = 2 * i + k
                        rows = P if j < FFN_TILES - 1 else FFN_REST
                        for t in range(TILES):
                            for a, w in PASSES:
                                last = pe.matmul(acc[:, t, :], hT[a][0:rows, k, t * P:(t + 1) * P], w_down[w][0:rows, j, :],
                                                 start=(j == 0 and t == 0 and (a, w) == PASSES[0]),
                                                 stop=(j == FFN_TILES - 1 and (a, w) == PASSES[-1]), skip_group_check=True)
                    last.then_inc(h_used, 1)

            def scores(s, t, H):
                g = t // GROUP_HEADS
                if t % GROUP_HEADS == 0:
                    pe.wait_ge(act_read, s.n * FILLS + (12 + 10 * g))
                wait(pe, scores_masked, H - 1)
                rows = slice(HEAD_DIM * (t % 2), HEAD_DIM * (t % 2) + HEAD_DIM)
                pe.matmul(score[t % 2][:, 0:BAND0], qT[rows, t // 2, 0:P], kT[rows, t // 2, 0:P], start=True, stop=True)
                pe.matmul(score[t % 2][:, BAND0:BAND], qT[rows, t // 2, P:TOKENS], kT[rows, t // 2, P - WINDOW:TOKENS],
                          start=True, stop=True).then_inc(scores_ready, 1)

            def turn_probs(t, H):
                pe.wait_ge(probs_scaled, H + 1)
                wait(pe, probsT_copied, H)
                pr = probs[:, t % 4, :]
                pe.transpose(turned[:, 0:P], pr[:, 0:P], ident[:])
                pe.transpose(turned[:, P:2 * P], pr[:, 2 * P:3 * P], ident[:])
                pe.transpose(turned[:, 2 * P:2 * P + WINDOW], pr[0:WINDOW, P:2 * P], ident[0:WINDOW, 0:WINDOW]).then_inc(probs_turned, 1)

            def mix_values(t, H, Q):
                pe.wait_ge(probsT_copied, H + 1)
                if t % 2 == 0:
                    wait(pe, out_split, Q)
                rows = slice(HEAD_DIM * (t % 2), HEAD_DIM * (t % 2) + HEAD_DIM)
                cols = slice(t * HEAD_DIM, (t + 1) * HEAD_DIM)
                o = mix[rows, (t // 2) % 2, :]
                pT = probsT[:, t % 2, :]
                pe.matmul(o[:, 0:P], v[:, 0, cols], pT[:, 0:P], start=True, stop=True)
                pe.matmul(o[:, P:TOKENS], v[:, 1, cols], pT[:, P:2 * P], start=True, stop=False)
                pe.matmul(o[:, P:P + WINDOW], v[:, 0, cols], pT[:, 2 * P:BAND], start=False, stop=True).then_inc(mixed, 1)

            def slot(s):
                if isinstance(s.n, int) and s.n == -1:
                    pe.wait_ge(cleared, 6)
                for t in range(HEADS):
                    if s.head(t, 0) is not None:
                        scores(s, t, s.head(t, 0))
                    items = list(s.dense(t))
                    for item in items[:1]:
                        dense(s, item)
                    if s.head(t, 2) is not None:
                        turn_probs((t - 2) % HEADS, s.head(t, 2))
                    for item in items[1:]:
                        dense(s, item)
                    if s.head(t, 3) is not None:
                        h = (t - 3) % HEADS
                        mix_values(h, s.head(t, 3), s.n * PAIRS + (t - 3) // 2)

            pe.sem_inc(h_used, 1)
            run_slots(pe, slot)

        @block.scalar
        def _(act):
            def split(blk, layer):
                act.wait_ge(w_loaded, layer * WEIGHT_LOADS[-1] + WEIGHT_LOADS[blk])
                if not isinstance(layer, int):
                    sem_used, value = last_use(blk, layer)
                    act.wait_ge(sem_used, value)
                for raw, high, _ in split_views(blk):
                    last = act.copy(high, raw)
                last.then_inc(w_high, 1)

            def dense(s, item):
                n, kind = s.n, item[0]
                f = n - 1
                if kind == "input":
                    m = n + 1
                    for h in range(HALVES):
                        act.wait_ge(filled, m * FILLS + h + 1)
                        act.copy(xT[0][:, h, h:h + TOKENS], project[h][:, 0:TOKENS]).then_inc(act_read, 1)
                elif kind == "unit":
                    g, u = item[1:]
                    m = n if g else n + 1
                    bank = project[(2 + 10 * g + UNIT_AT[u] - 1) % 2]
                    act.wait_ge(filled, unit_fill(m, g, u))
                    if u < 4:
                        wait(act, squares_summed, rotation(m, g, u) - 1)
                        act.activation(square[:], bank[:], ACT.Square, scale=1.0 if u % 2 else 1.0 / QK_SCALE).then_inc(act_read, 1)
                    else:
                        wait(act, mixed, m * HEADS - HEADS + GROUP_HEADS * (g + 1) if not (isinstance(m, int) and m == 0) else 0)
                        act.copy(v[:, u - 4, g * GROUP:(g + 1) * GROUP], bank[:]).then_inc(act_read, 1)
                elif kind == "turn":
                    g, u = item[1:]
                    m = n if g else n + 1
                    bank = project[(2 + 10 * g + TRANSPOSE_AT[u] - 1) % 2]
                    act.wait_ge(filled, turn_fill(m, g, u))
                    wait(act, scores_ready, m * HEADS - HEADS + GROUP_HEADS * (g + 1) if not (isinstance(m, int) and m == 0) else 0)
                    dst = (kT if u % 2 else qT)[:, 4 * g:4 * g + 4, (u // 2) * P:(u // 2 + 1) * P]
                    act.copy(dst, bank[:].rearrange("p (a b) -> p a b", a=4)).then_inc(act_read, 1)
                elif kind == "norm_turn":
                    act.wait_ge(wide_filled, f * WIDE_FILLS + 1)
                    act.wait_ge(params_loaded, s.layer * 32 + 32)
                    at = 2 * FFN_TILES
                    for h in range(HALVES):
                        last = act.activation(xn[:, h, :], wide[:, h, :], ACT.Identity, bias=params[:, at + HALVES + h:at + HALVES + h + 1],
                                              scale=params[:, at + h:at + h + 1])
                    last.then_inc(wide_read, 1)
                    act.wait_ge(wide_read, f * WIDE_FILLS + 1 + 1)
                    act.copy(xnT[0][:], xn[:]).then_inc(xn_high, 1)
                elif kind == "gelu":
                    act.wait_ge(wide_read, f * WIDE_FILLS + 4 + 1)
                    act.activation(gates[:], gates[:], ACT.Gelu).then_inc(gelu_done, 1)
                elif kind == "value":
                    i = item[1]
                    act.wait_ge(wide_read, f * WIDE_FILLS + 5 + i + 1)
                    wait(act, h_used, f * 3 + i + 1)
                    if i < 2:
                        act.copy(hT[0][:], gates[:, 2 * i:2 * i + 2, :]).then_inc(h_high, 1)
                    else:
                        act.copy(hT[0][:, 0, :], gates[:, 4, :])
                        act.copy(hT[0][0:FFN_REST, 1, :], gates[0:FFN_REST, 5, :]).then_inc(h_high, 1)

            def slot(s):
                if isinstance(s.n, int) and s.n == -1:
                    act.wait_ge(cleared, 6)
                    for blk in range(WEIGHT_BLOCKS):
                        split(blk, 0)
                for t in range(HEADS):
                    H = s.head(t, 0)
                    if H is not None:
                        act.wait_ge(scores_masked, H + 1)
                        wait(act, probs_turned, H - 3)
                        for i, (a, b, at) in enumerate(((0, BAND0, 0), (BAND0, BAND, P + WINDOW))):
                            last = act.activation(probs[:, t % 4, at:at + b - a], masked[:, t % 2, a:b], ACT.Exp,
                                                  bias=shift[:, t % 2, i:i + 1], scale=-1.0, accum_out=sums[:, t % 4, i:i + 1])
                        last.then_inc(exp_done, 1)
                    if s.switch == "projections" and t in (0, 8):
                        split(t // 8, s.layer + 1)
                    for item in s.dense(t):
                        dense(s, item)
                    if s.switch == "ffn" and t in (5, 14, 15):
                        split({5: 2, 14: 3, 15: 4}[t], s.layer + 1)
                    H = s.head(t, 2)
                    if H is not None and t % 2 == 0:
                        act.wait_ge(probs_turned, H + 1)
                        wait(act, mixed, H - 1)
                        act.copy(probsT[:, t % 2, :], turned[:, 0:BAND]).then_inc(probsT_copied, 1)
                    H = s.head(t, 3)
                    if H is not None and (t - 3) % 2 == 1:
                        pair = ((t - 3) % HEADS) // 2
                        act.wait_ge(mixed, H + 1)
                        if pair == 0:
                            wait(act, attn_projected, s.n)
                        act.copy(oT[0][:, pair, :], mix[:, pair % 2, :]).then_inc(out_high, 1)

            run_slots(act, slot)

        @block.gpsimd
        def _(pool):
            pool.sem_inc(h_low, 1)
            pool.memset(probs[:], 0.0).then_inc(cleared, 1)
            pool.memset(late_half[:], 0.0).then_inc(cleared, 1)
            for part in range(2):
                pool.memset(xT[part][:].bitcast(FP32), 0.0).then_inc(cleared, 1)
                pool.memset(w_up[part][:].bitcast(FP32), 0.0).then_inc(cleared, 1)

            def dense(s, item):
                n, kind = s.n, item[0]
                f = n - 1
                if kind == "unit" and item[2] < 4:
                    g, u = item[1:]
                    m = n if g else n + 1
                    k = rotation(m, g, u)
                    wait_apart(pool, squares_summed, k, passed)
                    floor = NORM_FLOOR if u % 2 else NORM_FLOOR / QK_SCALE ** 2
                    pool.tensor_scalar(sums_sq[:, u % 2, :], sums_sq[:, u % 2, :], floor, None, ALU.max).then_inc(pool_step, 1)
                    pool.wait_ge(pool_step, m * 12 + 6 * g + (1, 2, 4, 5)[u])
                    if u % 2 == 0:
                        wait(pool, scores_masked, m * HEADS - HEADS + GROUP_HEADS * (g + 1) if not (isinstance(m, int) and m == 0) else 0)
                        pool.tensor_tensor(query_scale[:, u // 2, g * GROUP_HEADS:(g + 1) * GROUP_HEADS], sums_sq[:, 0, :],
                                           half[:, 0:GROUP_HEADS], ALU.pow)
                    else:
                        pool.tensor_tensor(inv_norm[:, 1, :], sums_sq[:, 1, :], half[:, 0:GROUP_HEADS], ALU.pow)
                    pool.wait_ge(dve_read, unit_read(m, g, u))
                    add = pool.tensor_tensor(with_cos[:, u % 2, :], with_cos[:, u % 2, :], with_sin[:, u % 2, :], ALU.add)
                    if u % 2 == 0:
                        add.then_inc(rotated, 1)
                    else:
                        add.then_inc(pool_step, 1)
                        pool.wait_ge(pool_step, m * 12 + 6 * g + (0, 3, 0, 6)[u])
                        view = with_cos[:, 1, :].rearrange("p (h d) -> p h d", h=GROUP_HEADS)
                        pool.tensor_tensor(view, view, inv_norm[:, 1, :].unsqueeze(2).broadcast_to([P, GROUP_HEADS, HEAD_DIM]),
                                           ALU.mult).then_inc(rotated, 1)
                elif kind == "norm":
                    wait_apart(pool, ln_moments, f + 1, passed)
                    pool.tensor_scalar(ln_mv[:, :, 1], ln_mv[:, :, 1], EPS, None, ALU.add).then_inc(ln_floor, 1)
                    pool.wait_ge(ln_floor, f + 1)
                    pool.tensor_tensor(ln_rstd[:], ln_mv[:, :, 1], half[:, 0:TILES], ALU.pow).then_inc(ln_root, 1)
                elif kind == "norm_turn":
                    pool.wait_ge(xn_high, f + 1)
                    pool.tensor_tensor(xnT[1][:], xn[:], xnT[0][:].bitcast(FP32), ALU.subtract).then_inc(xn_low, 1)
                    pool.wait_ge(params_loaded, s.layer * 32 + 32)
                    pool.tensor_tensor(res[:], res[:], b_down[:].unsqueeze(1).broadcast_to([P, TILES, DIM]), ALU.add).then_inc(res_ready, 1)
                elif kind == "value":
                    i = item[1]
                    pool.wait_ge(h_high, f * 3 + i + 1)
                    if i < 2:
                        pool.tensor_tensor(hT[1][:], gates[:, 2 * i:2 * i + 2, :], hT[0][:].bitcast(FP32), ALU.subtract).then_inc(h_low, 1)
                    else:
                        pool.tensor_tensor(hT[1][:, 0, :], gates[:, 4, :], hT[0][:, 0, :].bitcast(FP32), ALU.subtract)
                        pool.tensor_tensor(hT[1][0:FFN_REST, 1, :], gates[0:FFN_REST, 5, :], hT[0][0:FFN_REST, 1, :].bitcast(FP32),
                                           ALU.subtract).then_inc(h_low, 1)

            def slot(s):
                for t in range(HEADS):
                    for item in s.dense(t):
                        dense(s, item)

            run_slots(pool, slot)

        @block.vector
        def _(dve):
            def split(blk, layer):
                dve.wait_ge(w_high, layer * WEIGHT_BLOCKS + blk + 1)
                for raw, high, low in split_views(blk):
                    last = dve.tensor_tensor(low, raw, high.bitcast(FP32), ALU.subtract)
                last.then_inc(w_low, 1)

            def build_tables(layer):
                dve.wait_ge(scales_loaded, layer * 16 + 16)
                wait(dve, dve_read, layer * (BATCH * DVE_READS))
                for part in range(2):
                    scale = qk_scales[:, part].unsqueeze(1).broadcast_to([P, TILES, 2, HEAD_DIM // 2])
                    for k, sc in ((0, scale), (1, scale[:, :, ::-1, :])):
                        last = dve.tensor_tensor(tables[:, 2 * part + k].rearrange("p t (a b) -> p t a b", a=2),
                                                 rope[:, 2 * part + k].rearrange("p t (a b) -> p t a b", a=2), sc, ALU.mult)
                last.then_inc(tables_built, 1)
                dve.wait_ge(tables_built, layer + 1)

            def dense(s, item):
                n, kind = s.n, item[0]
                f = n - 1
                if kind == "input":
                    m = n + 1
                    for h in range(HALVES):
                        dve.wait_ge(act_read, m * FILLS + h + 1)
                        dve.tensor_tensor(xT[1][:, h, h:h + TOKENS], project[h][:, 0:TOKENS], xT[0][:, h, h:h + TOKENS].bitcast(FP32),
                                          ALU.subtract).then_inc(dve_read, 1)
                elif kind == "unit" and item[2] < 4:
                    g, u = item[1:]
                    m = n if g else n + 1
                    bank = project[(2 + 10 * g + UNIT_AT[u] - 1) % 2]
                    c, t = u % 2, u // 2
                    dve.wait_ge(act_read, unit_fill(m, g, u))
                    if u >= 2:
                        dve.wait_ge(filled, turn_fill(m, g, u - 2))
                    elif g == 1:
                        dve.wait_ge(filled, turn_fill(m, 0, u + 2))
                    elif not (isinstance(m, int) and m == 0):
                        dve.wait_ge(filled, turn_fill(m - 1, 1, u + 2))

                    def heads(ap):
                        return ap.rearrange("p (h a b) -> p h a b", h=GROUP_HEADS, a=2)

                    def table(k):
                        return tables[:, k, t, :].rearrange("p (a b) -> p a b", a=2).unsqueeze(1)\
                            .broadcast_to([P, GROUP_HEADS, 2, HEAD_DIM // 2])

                    dve.tensor_tensor(heads(with_cos[:, c, :]), heads(bank[:]), table(2 * c), ALU.mult)
                    dve.tensor_tensor(heads(with_sin[:, c, :]), heads(bank[:])[:, :, ::-1, :], table(2 * c + 1),
                                      ALU.mult).then_inc(dve_read, 1)
                    dve.tensor_reduce(sums_sq[:, c, :], square[:].rearrange("p (h d) -> p h d", h=GROUP_HEADS), AXIS_X,
                                      ALU.add).then_inc(squares_summed, 1)
                elif kind == "project_out" and item[1] == 1:
                    dve.wait_ge(attn_projected, f + 1)
                    dve.wait_ge(res_loaded, f * 16 + 16)
                    dve.tensor_tensor(res[:], acc[:], res[:], ALU.add).then_inc(acc_read, 1)
                elif kind == "norm":
                    dve.wait_ge(shifted, f * 32 + 32)
                    dve.wait_ge(acc_read, f * 2 + 1 + 1)
                    for t in range(TILES):
                        dve.bn_stats(ln_stats[:, t, 0, :], res[:, t, 0:P])
                        last = dve.bn_stats(ln_stats[:, t, 1, :], late_half[:, t, :])
                    last.then_inc(ln_stated, 1)
                    wait_apart(dve, ln_stated, f + 1, passed)
                    for t in range(TILES):
                        last = dve.bn_aggr(ln_mv[:, t, :], ln_stats[:, t].rearrange("p a b -> p (a b)"))
                    last.then_inc(ln_moments, 1)
                    dve.wait_ge(ln_root, f + 1)
                    for t in range(TILES):
                        dve.tensor_scalar(xn[:, t, 0:P], res[:, t, 0:P], ln_mv[:, t, 0:1], ln_rstd[:, t:t + 1], ALU.subtract, ALU.mult)
                        last = dve.tensor_scalar(xn[:, t, P:DIM], late_half[:, t, :], ln_mv[:, t, 0:1], ln_rstd[:, t:t + 1],
                                                 ALU.subtract, ALU.mult)
                    last.then_inc(ln_done, 1)
                elif kind == "gate":
                    i = item[1]
                    dve.wait_ge(wide_filled, f * WIDE_FILLS + 2 + i)
                    if i == 0:
                        dve.wait_ge(params_loaded, s.layer * 32 + 32)
                        wait(dve, h_low, f * 3 + 1)
                    for k in range(2):
                        j = FFN_TILES + 2 * i + k
                        last = dve.tensor_scalar(gates[:, 2 * i + k, :], wide[:, k, :], params[:, j:j + 1], None, ALU.add)
                    last.then_inc(wide_read, 1)
                elif kind == "value":
                    i = item[1]
                    dve.wait_ge(wide_filled, f * WIDE_FILLS + 5 + i)
                    dve.wait_ge(gelu_done, f + 1)
                    for k in range(2):
                        j = 2 * i + k
                        rows = P if j < FFN_TILES - 1 else FFN_REST
                        last = dve.scalar_tensor_tensor(gates[0:rows, j, :], wide[0:rows, k, :], params[0:rows, j:j + 1],
                                                        gates[0:rows, j, :], ALU.add, ALU.mult)
                    last.then_inc(wide_read, 1)
                elif kind == "residual":
                    dve.wait_ge(h_used, f * 3 + 3 + 1)
                    dve.wait_ge(res_ready, f + 1)
                    dve.tensor_tensor(res[:], acc[:], res[:], ALU.add).then_inc(acc_read, 1)

            def slot(s):
                if isinstance(s.n, int) and s.n == -1:
                    for blk in range(WEIGHT_BLOCKS):
                        split(blk, 0)
                    build_tables(0)
                for t in range(HEADS):
                    h4 = (t - 1) % 4
                    before = s.head(t, 1)
                    if before is not None:
                        dve.wait_ge(exp_done, before + 1)
                        dve.reciprocal(inv_sums[:, h4, :], sums[:, h4, :]).then_inc(sums_inverted, 1)
                    H = s.head(t, 0)
                    if H is not None:
                        if t % GROUP_HEADS == 0:
                            dve.wait_ge(rotated, s.n * ROTATIONS + 4 * (t // GROUP_HEADS) + 4)
                        dve.wait_ge(scores_ready, H + 1)
                        wait(dve, exp_done, H - 1)
                        dve.sem_inc(passed, 1)
                        for i, (a, b) in enumerate(((0, BAND0), (BAND0, BAND))):
                            last = dve.tensor_tensor_reduce(out=masked[:, t % 2, a:b], in0=score[t % 2][:, a:b], in1=mask[:, a:b],
                                                            scale=query_scale[:, i, t:t + 1], scalar=3e38, op0=ALU.add, op1=ALU.min,
                                                            accum_out=shift[:, t % 2, i:i + 1])
                        last.then_inc(scores_masked, 1)
                    if before is not None:
                        dve.wait_ge(sums_inverted, before + 1)
                        for i, (a, b) in enumerate(((0, P), (P + WINDOW, PROBS))):
                            last = dve.tensor_scalar(probs[:, h4, a:b], probs[:, h4, a:b], inv_sums[:, h4, i:i + 1], None, ALU.mult)
                        last.then_inc(probs_scaled, 1)
                    if s.switch == "projections" and t in (0, 8):
                        split(t // 8, s.layer + 1)
                        if t == 8:
                            build_tables(s.layer + 1)
                    for item in s.dense(t):
                        dense(s, item)
                    if s.switch == "ffn" and t in (5, 14, 15):
                        split({5: 2, 14: 3, 15: 4}[t], s.layer + 1)
                    H = s.head(t, 2)
                    if H is not None and t % 2 == 1:
                        dve.wait_ge(probs_turned, H + 1)
                        wait(dve, mixed, H - 1)
                        dve.tensor_copy(probsT[:, t % 2, :], turned[:, 0:BAND]).then_inc(probsT_copied, 1)
                    H = s.head(t, 3)
                    if H is not None and (t - 3) % 2 == 1:
                        pair = ((t - 3) % HEADS) // 2
                        dve.wait_ge(out_high, s.n * PAIRS + (t - 3) // 2 + 1)
                        dve.tensor_tensor(oT[1][:, pair, :], mix[:, pair % 2, :], oT[0][:, pair, :].bitcast(FP32),
                                          ALU.subtract).then_inc(out_split, 1)

            for semaphore in (acc_read, ln_done, wide_read):
                dve.sem_inc(semaphore, 1)
            run_slots(dve, slot)
            with dve.Fori(0, BATCH) as b:
                dve.wait_ge(final_in, b * 32 + 32)
                dve.tensor_tensor(res[:], y_in[:], res[:], ALU.add).then_inc(final_added, 1)


def decoder_kernel(nc, D):
    with ExitStack() as ctx:
        T = {
            "ident": ctx.enter_context(nc.sbuf_tensor("ident", [P, P], FP32)),
            "mask": ctx.enter_context(nc.sbuf_tensor("mask", [P, BAND], FP32)),
            "rope": ctx.enter_context(nc.sbuf_tensor("rope", [P, 4, TILES, HEAD_DIM], FP32)),
            "half": ctx.enter_context(nc.sbuf_tensor("half", [P, GROUP_HEADS], FP32)),
        }
        front(nc, T, D, None)
        layers(nc, T, D)


def shape_constants():
    import numpy as np
    f32 = np.float32
    i = np.arange(TOKENS)
    allowed = (i[:, None] >= i[None, :]) & (i[:, None] <= i[None, :] + WINDOW)
    band = np.where(allowed, 0.0, MASKED).astype(f32)
    mask = np.concatenate([band[0:P, 0:P], band[P:TOKENS, P - WINDOW:TOKENS]], axis=1)
    halfdim = np.arange(0, HEAD_DIM, 2, dtype=f32)
    inv_freq = (f32(1.0) / f32(10000.0) ** (halfdim / f32(HEAD_DIM))).astype(f32)
    t = np.arange(TOKENS, dtype=f32)
    freqs = (t[:, None] * inv_freq[None, :]).astype(f32)
    base = ((halfdim + f32(0.4 * HEAD_DIM)) / f32(1.4 * HEAD_DIM)).astype(f32)
    power = ((t - TOKENS // 2) / f32(WINDOW // 2)).astype(f32)
    scale = (base[None, :] ** power[:, None]).astype(f32)
    cos, sin = np.cos(freqs), np.sin(freqs)
    parts = []
    for cs, sn, sign in ((cos * scale, sin * scale, 1.0), (cos / scale, sin / scale, -1.0)):
        parts += [sign * np.concatenate([cs, cs], 1), sign * np.concatenate([-sn, sn], 1)]
    rope = np.stack(parts).astype(f32).reshape(4, TILES, P, HEAD_DIM).transpose(2, 0, 1, 3)
    return {"ident": np.eye(P, dtype=f32), "mask": mask, "rope": np.ascontiguousarray(rope)}


def kernel(**inputs):
    import numpy as np
    import concourse.bacc as bacc
    from concourse.bass_utils import run_bass_kernel_spmd

    a = {k: np.asarray(v) for k, v in inputs.items()}

    def columns(rows):
        tiles = (rows.shape[1] + P - 1) // P
        padded = np.zeros((rows.shape[0], tiles * P), rows.dtype)
        padded[:, :rows.shape[1]] = rows
        return padded.reshape(rows.shape[0], tiles, P).transpose(0, 2, 1)

    b1 = a["L0_ffn_b1"]
    arrays = {
        "x": a["x"],
        "ctxT": a["ctx_1024"].transpose(0, 2, 1),
        "mem_wk": a["L0_attn_W_K"],
        "mem_w1t": a["L0_attn_W1"].T,
        "mem_w2t": a["L0_attn_W2"].T,
        "cross_wq": a["L0_xattn_Wq"],
        "cross_wk": a["L0_xattn_Wk"],
        "cross_wv": a["L0_xattn_Wv"],
        "cross_bqk": np.concatenate([columns(a["L0_xattn_bq"][None])[0], columns(a["L0_xattn_bk"][None])[0]], axis=1),
        "cross_bv": a["L0_xattn_bv"][None],
        "w_qkv": a["L0_ffn_Wqkv"],
        "w_out": a["L0_ffn_Wo"],
        "w_up": a["L0_ffn_W1"],
        "w_down": a["L0_ffn_W2"],
        "b_down": a["L0_ffn_b2"],
        "params": np.concatenate([columns(b1[:, :FFN]), columns(b1[:, FFN:]), columns(a["L0_ffn_ln_g"]),
                                  columns(a["L0_ffn_ln_b"])], axis=2),
        "qk_scales": np.concatenate([a["L0_ffn_q_scale"], a["L0_ffn_k_scale"]], axis=1),
    }
    arrays.update(shape_constants())
    arrays = {k: np.ascontiguousarray(v) for k, v in arrays.items()}

    nc = bacc.Bacc("TRN2", target_bir_lowering=False, num_devices=1)
    D = {name: nc.dram_tensor(f"in_{name}", v.shape, mybir.dt.from_np(v.dtype), kind="ExternalInput").ap()
         for name, v in arrays.items()}
    D["out"] = nc.dram_tensor("out", (BATCH, TOKENS, DIM), FP32, kind="ExternalOutput").ap()
    for name in ("x2", "y"):
        D[name] = nc.dram_tensor(f"{name}_scratch", (BATCH, TOKENS, DIM), FP32, kind="Internal").ap()
    decoder_kernel(nc, D)
    r = run_bass_kernel_spmd(nc, [{f"in_{name}": v for name, v in arrays.items()}], core_ids=[0])
    return r.results[0]["out"]
```

```python
import concourse.bass as bass
from concourse import mybir
from contextlib import ExitStack

FP32 = mybir.dt.float32
FP32R = mybir.dt.float32r
ALU = mybir.AluOpType
ACT = mybir.ActivationFunctionType
AXIS_X = mybir.AxisListType.X

P = 128
BATCH, TOKENS, DIM = 8, 256, 256
TILES = TOKENS // P
HALVES = DIM // P
MEMORY = 64
DEPTH, HEADS, HEAD_DIM, WINDOW = 6, 16, 64, 64
INNER = HEADS * HEAD_DIM
FFN = int(DIM * 4 * 2 / 3)
FFN_TILES = (FFN + P - 1) // P
FFN_REST = FFN - (FFN_TILES - 1) * P
QK_SCALE = 8.0
EPS = 1e-5
NORM_FLOOR = 1e-24
MASKED = 1e30

STEPS = DEPTH * BATCH
PAIRS = HEADS // 2
GROUPS = 2
GROUP_HEADS = HEADS // GROUPS
GROUP = GROUP_HEADS * HEAD_DIM
W1_COLS = 2 * FFN + FFN_TILES * P - FFN
BAND0, BAND1 = P, P + WINDOW
BAND = BAND0 + BAND1
PROBS = P + WINDOW + BAND1

FILLS = 22
DVE_READS = 2
ROTATIONS = 8
WIDE_FILLS = 7
WEIGHT_BLOCKS = 6
WEIGHT_LOADS = (32, 64, 80, 112, 112, 144)

SCHEDULE = {
    0: [("unit", 1, 0), ("unit", 1, 1)],
    1: [("unit", 1, 2)],
    2: [("unit", 1, 3), ("turn", 1, 0)],
    3: [("project_out", 0), ("turn", 1, 1)],
    4: [("project_out", 1), ("turn", 1, 2)],
    5: [("unit", 1, 4), ("turn", 1, 3)],
    6: [("unit", 1, 5), ("input",), ("norm_stats",)],
    7: [("unit", 0, 0), ("norm_apply",)],
    8: [("unit", 0, 1), ("norm_turn",)],
    9: [("gate", 0), ("unit", 0, 2), ("gate", 1)],
    10: [("gate", 2), ("unit", 0, 3), ("turn", 0, 0), ("gelu",)],
    11: [("value", 0), ("turn", 0, 1), ("unit", 0, 4)],
    12: [("value", 1), ("down", 0), ("turn", 0, 2)],
    13: [("value", 2), ("down", 1), ("turn", 0, 3)],
    14: [("down", 2)],
    15: [("unit", 0, 5), ("residual",)],
}
SPLITS = {"projections": {0: 0, 1: 8}, "ffn": {2: 5, 3: 11, 4: 14, 5: 15}}
TABLES_TICK = 6
UNIT_AT, TRANSPOSE_AT = [{}, {}], [{}, {}]
for _tick in range(HEADS):
    for _item in SCHEDULE[_tick]:
        if _item[0] in ("unit", "turn"):
            _g, _u = _item[1:]
            (UNIT_AT if _item[0] == "unit" else TRANSPOSE_AT)[_g][_u] = len(UNIT_AT[_g]) + len(TRANSPOSE_AT[_g]) + 1


def wait(eng, semaphore, value):
    if not isinstance(value, int) or value > 0:
        eng.wait_ge(semaphore, value)


def wait_apart(eng, semaphore, value, passed):
    eng.wait_ge(semaphore, value)
    eng.sem_inc(passed, 1)


class Slot:

    def __init__(self, n, layer=0, attend=True, ffn=True, late=True, early=True,
                 late_layer=None, early_layer=None, switch=None, next_batch=None, ffn_batch=None):
        self.n, self.layer, self.attend, self.ffn, self.late, self.early = n, layer, attend, ffn, late, early
        self.late_layer = layer if late_layer is None else late_layer
        self.early_layer = layer if early_layer is None else early_layer
        self.switch = switch
        self.next_batch, self.ffn_batch = next_batch, ffn_batch

    def head(self, t, lag):
        if isinstance(self.n, int) and HEADS * self.n + t - lag < 0:
            return None
        if not self.attend and t >= lag:
            return None
        return HEADS * self.n + t - lag

    def dense(self, t):
        for item in SCHEDULE[t]:
            kind = item[0]
            if kind == "unit" or kind == "turn":
                if (self.late if item[1] else self.early):
                    yield item
            elif kind == "input":
                if self.early:
                    yield item
            elif self.ffn:
                yield item

    def is_late(self, item):
        return item[0] == "unit" and item[2] < 4 or item == ("project_out", 1)

    def vector_dense(self, t):
        if t > 0:
            for item in self.dense(t - 1):
                if self.is_late(item):
                    yield item
        for item in self.dense(t):
            if not self.is_late(item):
                yield item

    def splits(self, t):
        return [blk for blk, tick in SPLITS.get(self.switch, {}).items() if tick == t]


def run_slots(eng, slot, before_layer=None):
    slot(Slot(-1, attend=False, ffn=False, late=False, next_batch=0))
    slot(Slot(0, ffn=False, next_batch=1))
    with eng.Fori(0, DEPTH - 1) as layer:
        if before_layer:
            before_layer(layer)
        with eng.Fori(1, BATCH - 1) as b:
            slot(Slot(layer * BATCH + b, layer, next_batch=b + 1, ffn_batch=b - 1))
        slot(Slot(layer * BATCH + (BATCH - 1), layer, early_layer=layer + 1, switch="projections",
                  next_batch=0, ffn_batch=BATCH - 2))
        slot(Slot(layer * BATCH + BATCH, layer, late_layer=layer + 1, early_layer=layer + 1,
                  switch="ffn", next_batch=1, ffn_batch=BATCH - 1))
    last = DEPTH - 1
    with eng.Fori(1, BATCH - 1) as b:
        slot(Slot(last * BATCH + b, last, next_batch=b + 1, ffn_batch=b - 1))
    slot(Slot(STEPS - 1, last, early=False, ffn_batch=BATCH - 2))
    slot(Slot(STEPS, last, attend=False, late=False, early=False, ffn_batch=BATCH - 1))


def front(nc, T, D, weights):
    with ExitStack() as ctx:
        def sb(name, shape, dt=FP32):
            return ctx.enter_context(nc.sbuf_tensor(name, shape, dt))

        def sem(name):
            return ctx.enter_context(nc.semaphore(name))

        DUO = 2
        wk_mem = sb("wk_mem", [P, HALVES, DIM])
        w1t_mem = sb("w1t_mem", [P, HALVES, MEMORY])
        hidden_w = sb("hidden_w", [P, HALVES, MEMORY])
        w2t_mem = sb("w2t_mem", [MEMORY, DIM])
        wq = sb("wq_cross", [P, HALVES, DIM])
        wk = sb("wk_cross", [P, HALVES, DIM])
        wv = sb("wv_cross", [P, HALVES, DIM])
        bqk = sb("bqk", [P, 2 * HALVES])
        bv = sb("bv", [P, DIM])
        x = [sb(f"x{j}", [P, TILES, DIM]) for j in range(DUO)]
        xn = [sb(f"xn{j}", [P, TILES, DIM]) for j in range(DUO)]
        xnT = [sb(f"xnT{j}", [P, HALVES, TOKENS]) for j in range(DUO)]
        ctxT = [sb(f"ctxT{j}", [P, HALVES, TOKENS]) for j in range(DUO)]
        hidT = [sb(f"hidT{j}", [MEMORY, TOKENS]) for j in range(DUO)]
        qT = [sb(f"fqT{j}", [P, HALVES, TOKENS]) for j in range(DUO)]
        kT = [sb(f"fkT{j}", [P, HALVES, TOKENS]) for j in range(DUO)]
        v = [sb(f"fv{j}", [P, TILES, DIM]) for j in range(DUO)]
        pr = [sb(f"fp{j}", [P, TILES, TOKENS]) for j in range(DUO)]
        prT = [sb(f"fpT{j}", [P, TILES, TOKENS]) for j in range(DUO)]
        yo = [sb(f"yo{j}", [P, TILES, DIM]) for j in range(DUO)]
        st = sb("fst", [P, TILES, 6])
        mv = sb("fmv", [P, TILES, 2])
        rstd = sb("frstd", [P, TILES])
        mx = [sb(f"fmx{j}", [P, TILES]) for j in range(DUO)]
        nb = [sb(f"fnb{j}", [P, TILES]) for j in range(DUO)]
        sm = [sb(f"fsm{j}", [P, TILES]) for j in range(DUO)]
        rs = [sb(f"frs{j}", [P, TILES]) for j in range(DUO)]
        bank = [[ctx.enter_context(nc.psum_tensor(f"fb{j}{i}", [P, 2, DIM], FP32)) for i in range(4)]
                for j in range(DUO)]

        weights_in = sem("f_weights_in")
        x_in, ctx_in = sem("f_x_in"), sem("f_ctx_in")
        folded_ready, folded = sem("f_folded_ready"), sem("f_folded")
        stats, moments, root, normed = sem("f_stats"), sem("f_moments"), sem("f_root"), sem("f_normed")
        pool_step = sem("f_pool_step")
        turned, turned_out = sem("f_turned"), sem("f_turned_out")
        hid_ready, hid_act = sem("f_hid_ready"), sem("f_hid_act")
        read_ready, read_added = sem("f_read_ready"), sem("f_read_added")
        kv_ready, k_out, v_out = sem("f_kv_ready"), sem("f_k_out"), sem("f_v_out")
        q_ready, q_out = sem("f_q_ready"), sem("f_q_out")
        score_ready, top, shift = sem("f_score_ready"), sem("f_top"), sem("f_shift")
        probs, inverse = sem("f_probs"), sem("f_inverse")
        probs_turned, probs_out = sem("f_probs_turned"), sem("f_probs_out")
        cross_ready, cross_added = sem("f_cross_ready"), sem("f_cross_added")
        x2_stored, y_stored = sem("f_x2_stored"), sem("f_y_stored")
        passed = sem("f_passed")
        block = ctx.enter_context(nc.Block())
        ident = T["ident"]
        DUOS = BATCH // DUO

        def as_tiles(seq):
            return seq.rearrange("(t p) d -> p t d", p=P)

        def ln_index(i, s, j):
            return i * (3 * DUO) + s * DUO + j

        @block.sync
        def _(sp):
            sp.dma_start(T["ident"][:], D["ident"]).then_inc(weights_in, 16)
            sp.dma_start(T["mask"][:], D["mask"]).then_inc(weights_in, 16)
            for dst, src in ((wk_mem, "mem_wk"), (w1t_mem, "mem_w1t"), (wq, "cross_wq"), (wk, "cross_wk"), (wv, "cross_wv")):
                sp.dma_start(dst[:], D[src].rearrange("(k p) n -> p k n", p=P)).then_inc(weights_in, 16)
            sp.dma_start(w2t_mem[:], D["mem_w2t"]).then_inc(weights_in, 16)
            sp.dma_start(bqk[:], D["cross_bqk"]).then_inc(weights_in, 16)
            sp.dma_start(bv[:], D["cross_bv"].broadcast_to([P, DIM])).then_inc(weights_in, 16)
            for j in range(DUO):
                sp.dma_start(x[j][:], as_tiles(D["x"][j])).then_inc(x_in, 16)
                sp.dma_start(ctxT[j][:], D["ctxT"][j].rearrange("(k p) t -> p k t", p=P)).then_inc(ctx_in, 16)
                sp.wait_ge(x_in, 16 * (j + 1))
            def store(k, j, i):
                sp.wait_ge(cross_added, k + 1)
                sp.dma_start(as_tiles(D["x2"][k]), x[j][:]).then_inc(x2_stored, 16)
                sp.wait_ge(normed, ln_index(i, 2, j) + 1)
                sp.dma_start(as_tiles(D["y"][k]), yo[j][:]).then_inc(y_stored, 16)
                sp.wait_ge(x2_stored, (k + 1) * 16)
                sp.wait_ge(y_stored, (k + 1) * 16)

            with sp.Fori(0, DUOS - 1) as i:
                for j in range(DUO):
                    k = i * DUO + j
                    store(k, j, i)
                    sp.dma_start(x[j][:], as_tiles(D["x"][k + DUO])).then_inc(x_in, 16)
                    sp.dma_start(ctxT[j][:], D["ctxT"][k + DUO].rearrange("(k p) t -> p k t", p=P)).then_inc(ctx_in, 16)
            for j in range(DUO):
                store(BATCH - DUO + j, j, DUOS - 1)

        @block.tensor
        def _(pe):
            pe.wait_ge(weights_in, 16 * 10)
            for h in range(HALVES):
                for k in range(HALVES):
                    last = pe.matmul(bank[0][1][:, h, 0:MEMORY], wk_mem[:, k, h * P:(h + 1) * P], w1t_mem[:, k, :],
                                     start=(k == 0), stop=(k == HALVES - 1))
            last.then_inc(folded_ready, 1)
            pe.wait_ge(folded, 1)

            def turn(i, s, j):
                pe.wait_ge(normed, ln_index(i, s, j) + 1)
                for h in range(HALVES):
                    for t in range(TILES):
                        last = pe.transpose(bank[j][0][:, h, t * P:(t + 1) * P], xn[j][:, t, h * P:(h + 1) * P], ident[:])
                last.then_inc(turned, 1)

            with pe.Fori(0, DUOS) as i:
                for j in range(DUO):
                    turn(i, 0, j)
                for j in range(DUO):
                    pe.wait_ge(turned_out, (i * 2 + 0) * DUO + j + 1)
                    for h in range(HALVES):
                        last = pe.matmul(bank[j][1][0:MEMORY, 0, :], hidden_w[:, h, :], xnT[j][:, h, :],
                                         start=(h == 0), stop=(h == HALVES - 1))
                    last.then_inc(hid_ready, 1)
                for j in range(DUO):
                    pe.wait_ge(hid_act, i * DUO + j + 1)
                    for t in range(TILES):
                        last = pe.matmul(bank[j][2][:, t, :], hidT[j][:, t * P:(t + 1) * P], w2t_mem[:],
                                         start=True, stop=True)
                    last.then_inc(read_ready, 1)
                for j in range(DUO):
                    pe.wait_ge(ctx_in, (i * DUO + j + 1) * 16)
                    for m in range(HALVES):
                        for h in range(HALVES):
                            last = pe.matmul(bank[j][3][:, m, :], wk[:, h, m * P:(m + 1) * P], ctxT[j][:, h, :],
                                             start=(h == 0), stop=(h == HALVES - 1))
                    last.then_inc(kv_ready, 1)
                for j in range(DUO):
                    turn(i, 1, j)
                for j in range(DUO):
                    pe.wait_ge(k_out, i * DUO + j + 1)
                    for t in range(TILES):
                        for h in range(HALVES):
                            last = pe.matmul(bank[j][3][:, t, :], ctxT[j][:, h, t * P:(t + 1) * P], wv[:, h, :],
                                             start=(h == 0), stop=(h == HALVES - 1))
                    last.then_inc(kv_ready, 1)
                for j in range(DUO):
                    pe.wait_ge(turned_out, (i * 2 + 1) * DUO + j + 1)
                    for m in range(HALVES):
                        for h in range(HALVES):
                            last = pe.matmul(bank[j][1][:, m, :], wq[:, h, m * P:(m + 1) * P], xnT[j][:, h, :],
                                             start=(h == 0), stop=(h == HALVES - 1))
                    last.then_inc(q_ready, 1)
                for j in range(DUO):
                    pe.wait_ge(q_out, i * DUO + j + 1)
                    for t in range(TILES):
                        for h in range(HALVES):
                            last = pe.matmul(bank[j][1][:, t, :], qT[j][:, h, t * P:(t + 1) * P], kT[j][:, h, :],
                                             start=(h == 0), stop=(h == HALVES - 1))
                    last.then_inc(score_ready, 1)
                for j in range(DUO):
                    pe.wait_ge(probs, i * DUO + j + 1)
                    for kt in range(TILES):
                        for t in range(TILES):
                            last = pe.transpose(bank[j][0][:, kt, t * P:(t + 1) * P], pr[j][:, t, kt * P:(kt + 1) * P], ident[:])
                    last.then_inc(probs_turned, 1)
                for j in range(DUO):
                    pe.wait_ge(probs_out, i * DUO + j + 1)
                    pe.wait_ge(v_out, i * DUO + j + 1)
                    for t in range(TILES):
                        for kt in range(TILES):
                            last = pe.matmul(bank[j][2][:, t, :], prT[j][:, kt, t * P:(t + 1) * P], v[j][:, kt, :],
                                             start=(kt == 0), stop=(kt == TILES - 1))
                    last.then_inc(cross_ready, 1)

        @block.scalar
        def _(act):
            with act.Fori(0, DUOS) as i:
                for j in range(DUO):
                    act.wait_ge(turned, (i * 2 + 0) * DUO + j + 1)
                    act.copy(xnT[j][:], bank[j][0][:]).then_inc(turned_out, 1)
                for j in range(DUO):
                    act.wait_ge(hid_ready, i * DUO + j + 1)
                    act.activation(hidT[j][:], bank[j][1][0:MEMORY, 0, :], ACT.Gelu).then_inc(hid_act, 1)
                for j in range(DUO):
                    act.wait_ge(turned, (i * 2 + 1) * DUO + j + 1)
                    act.copy(xnT[j][:], bank[j][0][:]).then_inc(turned_out, 1)
                for j in range(DUO):
                    act.wait_ge(shift, i * DUO + j + 1)
                    for t in range(TILES):
                        last = act.activation(pr[j][:, t, :], bank[j][1][:, t, :], ACT.Exp, bias=nb[j][:, t:t + 1],
                                              scale=DIM ** -0.5, accum_out=sm[j][:, t:t + 1])
                    last.then_inc(probs, 1)
                for j in range(DUO):
                    act.wait_ge(probs_turned, i * DUO + j + 1)
                    act.copy(prT[j][:], bank[j][0][:]).then_inc(probs_out, 1)

        @block.gpsimd
        def _(pool):
            nc.gpsimd.memset(T["half"][:], -0.5).then_inc(pool_step, 1)
            pool.wait_ge(pool_step, 1)
            with pool.Fori(0, DUOS) as i:
                for s in range(3):
                    for j in range(DUO):
                        k = ln_index(i, s, j)
                        wait_apart(pool, moments, k + 1, passed)
                        pool.tensor_scalar(mv[:, :, 1], mv[:, :, 1], EPS, None, ALU.add).then_inc(pool_step, 1)
                        pool.wait_ge(pool_step, k + 2)
                        pool.tensor_tensor(rstd[:], mv[:, :, 1], T["half"][:, 0:TILES], ALU.pow).then_inc(root, 1)

        @block.vector
        def _(dve):
            dve.wait_ge(folded_ready, 1)
            dve.tensor_copy(hidden_w[:], bank[0][1][:, :, 0:MEMORY]).then_inc(folded, 1)

            def layer_norm(i, s, j, source, out):
                k = ln_index(i, s, j)
                for t in range(TILES):
                    last = dve.bn_stats(st[:, t, :], source[:, t, :])
                last.then_inc(stats, 1)
                wait_apart(dve, stats, k + 1, passed)
                for t in range(TILES):
                    last = dve.bn_aggr(mv[:, t, :], st[:, t, :])
                last.then_inc(moments, 1)
                dve.wait_ge(root, k + 1)
                for t in range(TILES):
                    last = dve.tensor_scalar(out[:, t, :], source[:, t, :], mv[:, t, 0:1], rstd[:, t:t + 1],
                                             ALU.subtract, ALU.mult)
                last.then_inc(normed, 1)

            with dve.Fori(0, DUOS) as i:
                for j in range(DUO):
                    dve.wait_ge(x_in, (i * DUO + j + 1) * 16)
                    layer_norm(i, 0, j, x[j], xn[j])
                for j in range(DUO):
                    dve.wait_ge(read_ready, i * DUO + j + 1)
                    dve.tensor_tensor(x[j][:], bank[j][2][:], x[j][:], ALU.add).then_inc(read_added, 1)
                for j in range(DUO):
                    dve.wait_ge(read_added, i * DUO + j + 1)
                    layer_norm(i, 1, j, x[j], xn[j])
                for j in range(DUO):
                    dve.wait_ge(kv_ready, i * (2 * DUO) + j + 1)
                    for m in range(HALVES):
                        last = dve.tensor_scalar(kT[j][:, m, :], bank[j][3][:, m, :], bqk[:, HALVES + m:HALVES + m + 1],
                                                 None, ALU.add)
                    last.then_inc(k_out, 1)
                for j in range(DUO):
                    dve.wait_ge(kv_ready, i * (2 * DUO) + DUO + j + 1)
                    dve.tensor_tensor(v[j][:], bank[j][3][:], bv[:].unsqueeze(1).broadcast_to([P, TILES, DIM]),
                                      ALU.add).then_inc(v_out, 1)
                for j in range(DUO):
                    dve.wait_ge(q_ready, i * DUO + j + 1)
                    for m in range(HALVES):
                        last = dve.tensor_scalar(qT[j][:, m, :], bank[j][1][:, m, :], bqk[:, m:m + 1], None, ALU.add)
                    last.then_inc(q_out, 1)
                for j in range(DUO):
                    k = i * DUO + j
                    dve.wait_ge(score_ready, k + 1)
                    dve.tensor_reduce(mx[j][:], bank[j][1][:], AXIS_X, ALU.max).then_inc(top, 1)
                    dve.wait_ge(top, k + 1)
                    dve.tensor_scalar(nb[j][:], mx[j][:], -(DIM ** -0.5), None, ALU.mult).then_inc(shift, 1)
                for j in range(DUO):
                    dve.wait_ge(probs, i * DUO + j + 1)
                    dve.reciprocal(rs[j][:], sm[j][:]).then_inc(inverse, 1)
                for j in range(DUO):
                    k = i * DUO + j
                    dve.wait_ge(cross_ready, k + 1)
                    dve.wait_ge(inverse, k + 1)
                    for t in range(TILES):
                        last = dve.scalar_tensor_tensor(x[j][:, t, :], bank[j][2][:, t, :], rs[j][:, t:t + 1],
                                                        x[j][:, t, :], ALU.mult, ALU.add)
                    last.then_inc(cross_added, 1)
                for j in range(DUO):
                    dve.wait_ge(cross_added, i * DUO + j + 1)
                    layer_norm(i, 2, j, x[j], yo[j])


def layers(nc, T, D):
    with ExitStack() as ctx:
        def sb(name, shape, dt=FP32):
            return ctx.enter_context(nc.sbuf_tensor(name, shape, dt))

        def sem(name):
            return ctx.enter_context(nc.semaphore(name))

        w_qkv = [sb(f"w_qkv{s}", [P, HALVES, 3, GROUPS, GROUP], FP32R) for s in range(2)]
        w_out = [sb(f"w_out{s}", [P, PAIRS, DIM], FP32R) for s in range(2)]
        w_up = [sb(f"w_up{s}", [P, HALVES, W1_COLS], FP32R) for s in range(2)]
        w_down = [sb(f"w_down{s}", [P, FFN_TILES, DIM], FP32R) for s in range(2)]
        STAGING = HALVES * 3 * GROUP
        staging = sb("staging", [P, STAGING])
        params = sb("params", [P, 2 * FFN_TILES + 2 * HALVES])
        b_down = sb("b_down", [P, DIM])
        qk_scales = sb("qk_scales", [P, 2, 2, HEAD_DIM // 2])
        tables = sb("tables", [P, 4, TILES, HEAD_DIM])

        y_in = sb("y_in", [P, TILES, DIM])
        xT = [sb(f"xT{s}", [P, HALVES, TOKENS + 2], FP32R) for s in range(2)]
        sums_sq = sb("sums_sq", [P, 4, GROUP_HEADS])
        inv_norm = sb("inv_norm", [P, 2, GROUP_HEADS])
        query_scale = sb("query_scale", [P, TILES, HEADS])
        with_cos = sb("with_cos", [P, 4, GROUP])
        with_sin = sb("with_sin", [P, 4, GROUP])
        qT = sb("qT", [P, PAIRS, TOKENS])
        kT = sb("kT", [P, PAIRS, TOKENS])
        v = sb("v", [P, TILES, INNER])

        masked = sb("masked", [P, 2, BAND])
        shift = sb("shift", [P, 2, TILES])
        sums = sb("sums", [P, 4, TILES])
        inv_sums = sb("inv_sums", [P, 4, TILES])
        probs = sb("probs", [P, 4, PROBS])
        probsT = sb("probsT", [P, 2, BAND])
        oT = [sb(f"oT{s}", [P, PAIRS, TOKENS], FP32R) for s in range(2)]

        res = sb("res", [P, TILES, DIM])
        ln_stats = sb("ln_stats", [P, TILES, HALVES, 6])
        ln_mv = sb("ln_mv", [P, TILES, 2])
        ln_rstd = sb("ln_rstd", [P, TILES])
        xn = sb("xn", [P, TILES, DIM])
        xnT = [sb(f"nT{s}", [P, HALVES, TOKENS], FP32R) for s in range(2)]
        gates = sb("gates", [P, FFN_TILES, TOKENS])
        hT = [sb(f"hT{s}", [P, 2, TOKENS], FP32R) for s in range(2)]

        project = [ctx.enter_context(nc.psum_tensor(f"project{i}", [P, GROUP], FP32)) for i in range(2)]
        score = [ctx.enter_context(nc.psum_tensor(f"score{i}", [P, GROUP], FP32)) for i in range(2)]
        turned = ctx.enter_context(nc.psum_tensor("turned", [P, GROUP], FP32))
        mix = ctx.enter_context(nc.psum_tensor("mix", [P, 2, TOKENS], FP32))
        wide = ctx.enter_context(nc.psum_tensor("wide", [P, 2, TOKENS], FP32))
        acc = ctx.enter_context(nc.psum_tensor("acc", [P, TILES, DIM], FP32))

        w_loaded, w_high, w_low = sem("w_loaded"), sem("w_high"), sem("w_low")
        params_loaded, scales_loaded, tables_built = sem("params_loaded"), sem("scales_loaded"), sem("tables_built")
        cleared = sem("cleared")
        y_loaded, res_loaded, y_stored = sem("y_loaded"), sem("res_loaded"), sem("y_stored")
        filled, act_read, dve_read = sem("filled"), sem("act_read"), sem("dve_read")
        squares_summed, floored, parts_ready = sem("squares_summed"), sem("floored"), sem("parts_ready")
        rotated, pool_step, tables_loaded, row_cleared = sem("rotated"), sem("pool_step"), sem("tables_loaded"), sem("row_cleared")
        scores_ready, scores_masked, exp_done = sem("scores_ready"), sem("scores_masked"), sem("exp_done")
        sums_inverted, probs_scaled = sem("sums_inverted"), sem("probs_scaled")
        probs_turned, probsT_copied, mixed = sem("probs_turned"), sem("probsT_copied"), sem("mixed")
        out_high, out_split = sem("out_high"), sem("out_split")
        attn_projected, acc_read, shifted = sem("attn_projected"), sem("acc_read"), sem("shifted")
        ln_stated, ln_moments, ln_root, ln_done = sem("ln_stated"), sem("ln_moments"), sem("ln_root"), sem("ln_done")
        ln_floor = sem("ln_floor")
        wide_filled, wide_read = sem("wide_filled"), sem("wide_read")
        xn_high, xn_low, gelu_done = sem("xn_high"), sem("xn_low"), sem("gelu_done")
        h_high, h_low, h_used, res_ready = sem("h_high"), sem("h_low"), sem("h_used"), sem("res_ready")
        final_in, final_added, final_out = sem("final_in"), sem("final_added"), sem("final_out")
        passed = sem("passed")
        block = ctx.enter_context(nc.Block())
        ident, mask, half = T["ident"], T["mask"], T["half"]

        def as_tiles(seq):
            return seq.rearrange("(t p) d -> p t d", p=P)

        def unit_fill(m, g, u):
            return m * FILLS + (2 + 10 * g + UNIT_AT[g][u])

        def turn_fill(m, g, u):
            return m * FILLS + (2 + 10 * g + TRANSPOSE_AT[g][u])

        def rotation(m, g, u):
            return m * ROTATIONS + (4 * g + u + 1)

        def last_use(blk, layer):
            m = layer * BATCH
            return [(filled, m * FILLS - FILLS + (2 + UNIT_AT[0][5])), (filled, m * FILLS - FILLS + (12 + UNIT_AT[1][5])),
                    (attn_projected, m), (wide_filled, m * WIDE_FILLS - 3), (wide_filled, m * WIDE_FILLS), (h_used, m * 3 + 1)][blk]

        def staged(blk):
            if blk < 2:
                return staging[:].rearrange("p (k c n) -> p k c n", k=HALVES, c=3)
            if blk == 2:
                return staging[:, 0:PAIRS * DIM].rearrange("p (k n) -> p k n", k=PAIRS)
            if blk == 5:
                return staging[:, 0:FFN_TILES * DIM].rearrange("p (k n) -> p k n", k=FFN_TILES)
            at = 0 if blk == 3 else STAGING - HALVES * FFN
            return staging[:, at:at + HALVES * FFN].rearrange("p (k n) -> p k n", k=HALVES)

        def split_views(blk):
            s = staged(blk)
            if blk < 2:
                return [(s[:, k], w_qkv[0][:, k, :, blk, :], w_qkv[1][:, k, :, blk, :]) for k in range(HALVES)]
            if blk == 2:
                return [(s, w_out[0][:], w_out[1][:])]
            if blk < 5:
                cols = slice(FFN, 2 * FFN) if blk == 3 else slice(0, FFN)
                return [(s, w_up[0][:, :, cols], w_up[1][:, :, cols])]
            return [(s[:, 0:FFN_TILES - 1], w_down[0][:, 0:FFN_TILES - 1], w_down[1][:, 0:FFN_TILES - 1]),
                    (s[0:FFN_REST, FFN_TILES - 1], w_down[0][0:FFN_REST, FFN_TILES - 1], w_down[1][0:FFN_REST, FFN_TILES - 1])]

        @block.sync
        def _(sp):
            def stage(blk, layer):
                if blk != 4:
                    wait(sp, w_low, layer * WEIGHT_BLOCKS + (4 if blk == 5 else blk))
                dst = staged(blk)
                if blk < 2:
                    src = D["w_qkv"][layer].rearrange("(k p) (c g n) -> k p c g n", p=P, c=3, g=GROUPS)
                    for k in range(HALVES):
                        sp.dma_start(dst[:, k], src[k, :, :, blk, :]).then_inc(w_loaded, 16)
                elif blk == 2:
                    sp.dma_start(dst, D["w_out"][layer].rearrange("(k p) n -> p k n", p=P)).then_inc(w_loaded, 16)
                elif blk < 5:
                    cols = slice(FFN, 2 * FFN) if blk == 3 else slice(0, FFN)
                    sp.dma_start(dst, D["w_up"][layer][:, cols].rearrange("(k p) n -> p k n", p=P)).then_inc(w_loaded, 16)
                else:
                    full = (FFN_TILES - 1) * P
                    sp.dma_start(dst[:, 0:FFN_TILES - 1],
                                 D["w_down"][layer][0:full, :].rearrange("(k p) n -> p k n", p=P)).then_inc(w_loaded, 16)
                    sp.dma_start(dst[0:FFN_REST, FFN_TILES - 1], D["w_down"][layer][full:FFN, :]).then_inc(w_loaded, 16)

            def load_tables(layer):
                wait(sp, parts_ready, layer * (BATCH * ROTATIONS))
                sp.dma_start(tables[:], D["rope"]).then_inc(tables_loaded, 16)

            def load_scales(layer):
                wait(sp, tables_built, layer)
                sp.dma_start(qk_scales[:], D["qk_scales"][layer].rearrange("(a b c) -> a b c", a=2, b=2).unsqueeze(0)
                             .broadcast_to([P, 2, 2, HEAD_DIM // 2])).then_inc(scales_loaded, 16)

            def load_params(layer):
                wait(sp, acc_read, layer * (2 * BATCH) + 1)
                sp.dma_start(params[:], D["params"][layer]).then_inc(params_loaded, 16)
                sp.dma_start(b_down[:], D["b_down"][layer].unsqueeze(0).broadcast_to([P, DIM])).then_inc(params_loaded, 16)

            def slot(s):
                n = s.n
                f = n - 1
                if s.early:
                    wait(sp, filled, n * FILLS + 2)
                    sp.dma_start(y_in[:], as_tiles(D["y"][s.next_batch])).then_inc(y_loaded, 16)
                if isinstance(n, int) and n == -1:
                    load_tables(0)
                    load_scales(0)
                    load_params(0)
                    for blk in range(WEIGHT_BLOCKS):
                        stage(blk, 0)
                if s.ffn:
                    wait(sp, y_stored, f * 16 + 1)
                    sp.dma_start(res[:], as_tiles(D["y"][s.ffn_batch])).then_inc(res_loaded, 16)
                if s.switch == "projections":
                    load_tables(s.layer + 1)
                if s.ffn:
                    wait(sp, acc_read, f * 2 + 1 + 1)
                    wait(sp, xn_low, f + 1)
                    sp.dma_start(xn[1:P, :, P:DIM], res[0:P - 1, :, P:DIM]).then_inc(shifted, 16)
                    sp.dma_start(xn[0:1, 1, P:DIM], res[P - 1:P, 0, P:DIM]).then_inc(shifted, 16)
                if s.switch == "projections":
                    stage(1, s.layer + 1)
                    stage(2, s.layer + 1)
                if s.switch == "ffn":
                    stage(3, s.layer + 1)
                    stage(4, s.layer + 1)
                    stage(5, s.layer + 1)
                if s.ffn:
                    wait(sp, acc_read, f * 2 + 2 + 1)
                    sp.dma_start(as_tiles(D["y"][s.ffn_batch]), res[:]).then_inc(y_stored, 16)
                if s.switch == "ffn":
                    load_params(s.layer + 1)

            def before_layer(layer):
                stage(0, layer + 1)
                load_scales(layer + 1)

            sp.sem_inc(y_stored, 1)
            sp.sem_inc(final_out, 1)
            run_slots(sp, slot, before_layer)
            sp.wait_ge(y_stored, STEPS * 16 + 1)
            with sp.Fori(0, BATCH) as b:
                sp.wait_ge(final_out, b * 16 + 1)
                sp.dma_start(y_in[:], as_tiles(D["y"][b])).then_inc(final_in, 16)
                sp.dma_start(res[:], as_tiles(D["x2"][b])).then_inc(final_in, 16)
                sp.wait_ge(final_added, b + 1)
                sp.dma_start(as_tiles(D["out"][b]), res[:]).then_inc(final_out, 16)
            sp.wait_ge(final_out, BATCH * 16 + 1)

        @block.tensor
        def _(pe):
            PASSES = ((0, 0), (1, 0), (0, 1))

            def bank_free(x, m):
                y = x - 2
                step = m
                if y <= 0:
                    y, step = y + FILLS, m - 1
                if isinstance(step, int) and step < 0:
                    return
                wait(pe, act_read, step * FILLS + y)
                if y <= DVE_READS:
                    wait(pe, dve_read, step * DVE_READS + y)

            def dense(s, item):
                n, kind = s.n, item[0]
                f = n - 1
                if kind == "input":
                    m = n + 1
                    pe.wait_ge(y_loaded, m * 16 + 16)
                    for h in range(HALVES):
                        bank_free(h + 1, m)
                        for t in range(TILES):
                            last = pe.transpose(project[h][:, t * P:(t + 1) * P], y_in[:, t, h * P:(h + 1) * P], ident[:])
                        last.then_inc(filled, 1)
                elif kind == "unit":
                    g, u = item[1:]
                    m = n if g else n + 1
                    c, t = (u % 2, u // 2) if u < 4 else (2, u - 4)
                    if u == 0:
                        pe.wait_ge(w_low, (s.late_layer if g else s.early_layer) * WEIGHT_BLOCKS + (g + 1))
                        pe.wait_ge(act_read, m * FILLS + 2)
                        pe.wait_ge(dve_read, m * DVE_READS + 2)
                    x = 2 + 10 * g + UNIT_AT[g][u]
                    bank_free(x, m)
                    for h in range(HALVES):
                        for a, w in PASSES:
                            last = pe.matmul(project[(x - 1) % 2][:], xT[a][:, h, t * P:(t + 1) * P], w_qkv[w][:, h, c, g, :],
                                             start=(h == 0 and (a, w) == PASSES[0]), stop=(h == HALVES - 1 and (a, w) == PASSES[-1]))
                    last.then_inc(filled, 1)
                elif kind == "turn":
                    g, u = item[1:]
                    m = n if g else n + 1
                    x = 2 + 10 * g + TRANSPOSE_AT[g][u]
                    pe.wait_ge(rotated, rotation(m, g, u))
                    bank_free(x, m)
                    for p in range(4):
                        last = pe.transpose(project[(x - 1) % 2][:, p * P:(p + 1) * P], with_cos[:, u, p * P:(p + 1) * P], ident[:])
                    last.then_inc(filled, 1)
                elif kind == "project_out":
                    t = item[1]
                    if t == 0:
                        pe.wait_ge(w_low, s.layer * WEIGHT_BLOCKS + 3)
                        pe.wait_ge(out_split, f * PAIRS + PAIRS)
                        wait(pe, acc_read, f * 2 + 1)
                    for p in range(PAIRS):
                        for a, w in PASSES:
                            last = pe.matmul(acc[:, t, :], oT[a][:, p, t * P:(t + 1) * P], w_out[w][:, p, :],
                                             start=(p == 0 and (a, w) == PASSES[0]), stop=(p == PAIRS - 1 and (a, w) == PASSES[-1]))
                    if t == TILES - 1:
                        last.then_inc(attn_projected, 1)
                elif kind == "norm_turn":
                    pe.wait_ge(ln_done, f + 1)
                    wait(pe, wide_read, f * WIDE_FILLS + 1)
                    for h in range(HALVES):
                        for t in range(TILES):
                            last = pe.transpose(wide[:, h, t * P:(t + 1) * P], xn[:, t, h * P:(h + 1) * P], ident[:])
                    last.then_inc(wide_filled, 1)
                elif kind in ("gate", "value"):
                    i = item[1]
                    x = 2 + i if kind == "gate" else 5 + i
                    if x == 2:
                        pe.wait_ge(w_low, s.layer * WEIGHT_BLOCKS + 5)
                        pe.wait_ge(xn_low, f + 1 + 1)
                    pe.wait_ge(wide_read, f * WIDE_FILLS + x - 1 + 1)
                    for k in range(2):
                        col = (2 * i + k) * P + (FFN if kind == "gate" else 0)
                        for h in range(HALVES):
                            for a, w in PASSES:
                                last = pe.matmul(wide[:, k, :], w_up[w][:, h, col:col + P], xnT[a][:, h, :],
                                                 start=(h == 0 and (a, w) == PASSES[0]), stop=(h == HALVES - 1 and (a, w) == PASSES[-1]))
                    last.then_inc(wide_filled, 1)
                elif kind == "down":
                    i = item[1]
                    if i == 0:
                        pe.wait_ge(w_low, s.layer * WEIGHT_BLOCKS + 6)
                        pe.wait_ge(acc_read, f * 2 + 1 + 1)
                    pe.wait_ge(h_low, f * 3 + i + 1 + 1)
                    for k in range(2):
                        j = 2 * i + k
                        rows = P if j < FFN_TILES - 1 else FFN_REST
                        for t in range(TILES):
                            for a, w in PASSES:
                                last = pe.matmul(acc[:, t, :], hT[a][0:rows, k, t * P:(t + 1) * P], w_down[w][0:rows, j, :],
                                                 start=(j == 0 and t == 0 and (a, w) == PASSES[0]),
                                                 stop=(j == FFN_TILES - 1 and (a, w) == PASSES[-1]), skip_group_check=True)
                    last.then_inc(h_used, 1)

            def scores(s, t, H):
                g = t // GROUP_HEADS
                if t % GROUP_HEADS == 0:
                    pe.wait_ge(act_read, s.n * FILLS + (12 + 10 * g))
                wait(pe, scores_masked, H - 1)
                rows = slice(HEAD_DIM * (t % 2), HEAD_DIM * (t % 2) + HEAD_DIM)
                pe.matmul(score[t % 2][:, 0:BAND0], qT[rows, t // 2, 0:P], kT[rows, t // 2, 0:P], start=True, stop=True)
                pe.matmul(score[t % 2][:, BAND0:BAND], qT[rows, t // 2, P:TOKENS], kT[rows, t // 2, P - WINDOW:TOKENS],
                          start=True, stop=True).then_inc(scores_ready, 1)

            def turn_probs(t, H):
                pe.wait_ge(probs_scaled, H + 1)
                wait(pe, probsT_copied, H)
                pr = probs[:, t % 4, :]
                pe.transpose(turned[:, 0:P], pr[:, 0:P], ident[:])
                pe.transpose(turned[:, P:2 * P], pr[:, 2 * P:3 * P], ident[:])
                pe.transpose(turned[:, 2 * P:2 * P + WINDOW], pr[0:WINDOW, P:2 * P], ident[0:WINDOW, 0:WINDOW]).then_inc(probs_turned, 1)

            def mix_values(t, H, Q):
                pe.wait_ge(probsT_copied, H + 1)
                if t % 2 == 0:
                    wait(pe, out_split, Q)
                rows = slice(HEAD_DIM * (t % 2), HEAD_DIM * (t % 2) + HEAD_DIM)
                cols = slice(t * HEAD_DIM, (t + 1) * HEAD_DIM)
                o = mix[rows, (t // 2) % 2, :]
                pT = probsT[:, t % 2, :]
                pe.matmul(o[:, 0:P], v[:, 0, cols], pT[:, 0:P], start=True, stop=True)
                pe.matmul(o[:, P:TOKENS], v[:, 1, cols], pT[:, P:2 * P], start=True, stop=False)
                pe.matmul(o[:, P:P + WINDOW], v[:, 0, cols], pT[:, 2 * P:BAND], start=False, stop=True).then_inc(mixed, 1)

            def slot(s):
                if isinstance(s.n, int) and s.n == -1:
                    pe.wait_ge(cleared, 5)
                for t in range(HEADS):
                    if s.head(t, 2) is not None:
                        turn_probs((t - 2) % HEADS, s.head(t, 2))
                    if s.head(t, 0) is not None:
                        scores(s, t, s.head(t, 0))
                    if s.head(t, 3) is not None:
                        h = (t - 3) % HEADS
                        mix_values(h, s.head(t, 3), s.n * PAIRS + (t - 3) // 2)
                    for item in s.dense(t):
                        dense(s, item)

            pe.sem_inc(h_used, 1)
            run_slots(pe, slot)

        @block.scalar
        def _(act):
            def split(blk, layer):
                act.wait_ge(w_loaded, layer * WEIGHT_LOADS[-1] + WEIGHT_LOADS[blk])
                if not isinstance(layer, int):
                    sem_used, value = last_use(blk, layer)
                    act.wait_ge(sem_used, value)
                for raw, high, _ in split_views(blk):
                    last = act.copy(high, raw)
                last.then_inc(w_high, 1)

            def dense(s, item):
                n, kind = s.n, item[0]
                f = n - 1
                if kind == "input":
                    m = n + 1
                    for h in range(HALVES):
                        act.wait_ge(filled, m * FILLS + h + 1)
                        act.copy(xT[0][:, h, h:h + TOKENS], project[h][:, 0:TOKENS]).then_inc(act_read, 1)
                elif kind == "unit":
                    g, u = item[1:]
                    m = n if g else n + 1
                    bank = project[(2 + 10 * g + UNIT_AT[g][u] - 1) % 2]
                    act.wait_ge(filled, unit_fill(m, g, u))
                    if u < 4:
                        if g == 1:
                            act.wait_ge(filled, turn_fill(m, 0, u))
                        elif not (isinstance(m, int) and m == 0):
                            act.wait_ge(filled, turn_fill(m - 1, 1, u))
                        act.activation(with_sin[:, u, :], bank[:], ACT.Square, scale=1.0 if u % 2 else 1.0 / QK_SCALE)
                        act.copy(with_cos[:, u, :], bank[:]).then_inc(act_read, 1)
                    else:
                        wait(act, mixed, m * HEADS - HEADS + GROUP_HEADS * (g + 1) if not (isinstance(m, int) and m == 0) else 0)
                        act.copy(v[:, u - 4, g * GROUP:(g + 1) * GROUP], bank[:]).then_inc(act_read, 1)
                elif kind == "turn":
                    g, u = item[1:]
                    m = n if g else n + 1
                    bank = project[(2 + 10 * g + TRANSPOSE_AT[g][u] - 1) % 2]
                    act.wait_ge(filled, turn_fill(m, g, u))
                    wait(act, scores_ready, m * HEADS - HEADS + GROUP_HEADS * (g + 1) if not (isinstance(m, int) and m == 0) else 0)
                    dst = (kT if u % 2 else qT)[:, 4 * g:4 * g + 4, (u // 2) * P:(u // 2 + 1) * P]
                    act.copy(dst, bank[:].rearrange("p (a b) -> p a b", a=4)).then_inc(act_read, 1)
                elif kind == "norm_turn":
                    act.wait_ge(wide_filled, f * WIDE_FILLS + 1)
                    act.wait_ge(params_loaded, s.layer * 32 + 32)
                    at = 2 * FFN_TILES
                    for h in range(HALVES):
                        last = act.activation(xn[:, h, :], wide[:, h, :], ACT.Identity, bias=params[:, at + HALVES + h:at + HALVES + h + 1],
                                              scale=params[:, at + h:at + h + 1])
                    last.then_inc(wide_read, 1)
                    act.wait_ge(wide_read, f * WIDE_FILLS + 1 + 1)
                    act.copy(xnT[0][:], xn[:]).then_inc(xn_high, 1)
                elif kind == "gelu":
                    act.wait_ge(wide_read, f * WIDE_FILLS + 4 + 1)
                    act.activation(gates[:], gates[:], ACT.Gelu).then_inc(gelu_done, 1)
                elif kind == "value":
                    i = item[1]
                    act.wait_ge(wide_read, f * WIDE_FILLS + 5 + i + 1)
                    wait(act, h_used, f * 3 + i + 1)
                    if i < 2:
                        act.copy(hT[0][:], gates[:, 2 * i:2 * i + 2, :]).then_inc(h_high, 1)
                    else:
                        act.copy(hT[0][:, 0, :], gates[:, 4, :])
                        act.copy(hT[0][0:FFN_REST, 1, :], gates[0:FFN_REST, 5, :]).then_inc(h_high, 1)

            def slot(s):
                if isinstance(s.n, int) and s.n == -1:
                    act.wait_ge(cleared, 5)
                    for blk in range(WEIGHT_BLOCKS):
                        split(blk, 0)
                for t in range(HEADS):
                    H = s.head(t, 2)
                    if H is not None and t % 2 == 0:
                        act.wait_ge(probs_turned, H + 1)
                        wait(act, mixed, H - 1)
                        act.copy(probsT[:, t % 2, :], turned[:, 0:BAND]).then_inc(probsT_copied, 1)
                    H = s.head(t, 0)
                    if H is not None:
                        act.wait_ge(scores_masked, H + 1)
                        wait(act, probs_turned, H - 3)
                        for i, (a, b, at) in enumerate(((0, BAND0, 0), (BAND0, BAND, P + WINDOW))):
                            last = act.activation(probs[:, t % 4, at:at + b - a], masked[:, t % 2, a:b], ACT.Exp,
                                                  bias=shift[:, t % 2, i:i + 1], scale=-1.0, accum_out=sums[:, t % 4, i:i + 1])
                        last.then_inc(exp_done, 1)
                    H = s.head(t, 3)
                    if H is not None and (t - 3) % 2 == 1:
                        pair = ((t - 3) % HEADS) // 2
                        act.wait_ge(mixed, H + 1)
                        if pair == 0:
                            wait(act, attn_projected, s.n)
                        act.copy(oT[0][:, pair, :], mix[:, pair % 2, :]).then_inc(out_high, 1)
                    for item in s.dense(t):
                        dense(s, item)
                    for blk in s.splits(t):
                        split(blk, s.layer + 1)

            run_slots(act, slot)

        @block.gpsimd
        def _(pool):
            pool.sem_inc(h_low, 1)
            pool.memset(probs[:], 0.0).then_inc(cleared, 1)
            pool.memset(xn[0:1, 0, P:DIM], 0.0).then_inc(row_cleared, 1)
            for part in range(2):
                pool.memset(xT[part][:].bitcast(FP32), 0.0).then_inc(cleared, 1)
                pool.memset(w_up[part][:].bitcast(FP32), 0.0).then_inc(cleared, 1)

            def dense(s, item):
                n, kind = s.n, item[0]
                f = n - 1
                if kind == "unit" and item[2] < 4:
                    g, u = item[1:]
                    m = n if g else n + 1
                    k = rotation(m, g, u)
                    if u % 2 == 0:
                        wait(pool, scores_masked, m * HEADS - HEADS + GROUP_HEADS * (g + 1) if not (isinstance(m, int) and m == 0) else 0)
                    pool.wait_ge(floored, k)
                    if u % 2 == 0:
                        pool.tensor_tensor(query_scale[:, u // 2, g * GROUP_HEADS:(g + 1) * GROUP_HEADS], sums_sq[:, u, :],
                                           half[:, 0:GROUP_HEADS], ALU.pow)
                    else:
                        pool.tensor_tensor(inv_norm[:, u // 2, :], sums_sq[:, u, :], half[:, 0:GROUP_HEADS], ALU.pow)
                    pool.wait_ge(parts_ready, k)
                    add = pool.tensor_tensor(with_cos[:, u, :], with_cos[:, u, :], with_sin[:, u, :], ALU.add)
                    if u % 2 == 0:
                        add.then_inc(rotated, 1)
                    else:
                        add.then_inc(pool_step, 1)
                        pool.wait_ge(pool_step, m * 4 + 2 * g + (u + 1) // 2)
                        view = with_cos[:, u, :].rearrange("p (h d) -> p h d", h=GROUP_HEADS)
                        pool.tensor_tensor(view, view, inv_norm[:, u // 2, :].unsqueeze(2).broadcast_to([P, GROUP_HEADS, HEAD_DIM]),
                                           ALU.mult).then_inc(rotated, 1)
                elif kind == "norm_stats":
                    wait_apart(pool, ln_moments, f + 1, passed)
                    pool.tensor_scalar(ln_mv[:, :, 1], ln_mv[:, :, 1], EPS, None, ALU.add).then_inc(ln_floor, 1)
                    pool.wait_ge(ln_floor, f + 1)
                    pool.tensor_tensor(ln_rstd[:], ln_mv[:, :, 1], half[:, 0:TILES], ALU.pow).then_inc(ln_root, 1)
                elif kind == "norm_turn":
                    wait_apart(pool, xn_low, f + 1 + 1, passed)
                    pool.memset(xn[0:1, 0, P:DIM], 0.0).then_inc(row_cleared, 1)
                    pool.wait_ge(params_loaded, s.layer * 32 + 32)
                    pool.tensor_tensor(res[:], res[:], b_down[:].unsqueeze(1).broadcast_to([P, TILES, DIM]), ALU.add).then_inc(res_ready, 1)
                elif kind == "value":
                    i = item[1]
                    pool.wait_ge(h_high, f * 3 + i + 1)
                    if i < 2:
                        pool.tensor_tensor(hT[1][:], gates[:, 2 * i:2 * i + 2, :], hT[0][:].bitcast(FP32), ALU.subtract).then_inc(h_low, 1)
                    else:
                        pool.tensor_tensor(hT[1][:, 0, :], gates[:, 4, :], hT[0][:, 0, :].bitcast(FP32), ALU.subtract)
                        pool.tensor_tensor(hT[1][0:FFN_REST, 1, :], gates[0:FFN_REST, 5, :], hT[0][0:FFN_REST, 1, :].bitcast(FP32),
                                           ALU.subtract).then_inc(h_low, 1)

            def slot(s):
                for t in range(HEADS):
                    for item in s.vector_dense(t):
                        dense(s, item)

            run_slots(pool, slot)

        @block.vector
        def _(dve):
            def split(blk, layer):
                dve.wait_ge(w_high, layer * WEIGHT_BLOCKS + blk + 1)
                for raw, high, low in split_views(blk):
                    last = dve.tensor_tensor(low, raw, high.bitcast(FP32), ALU.subtract)
                last.then_inc(w_low, 1)

            def build_tables(layer):
                dve.wait_ge(scales_loaded, layer * 16 + 16)
                dve.wait_ge(tables_loaded, layer * 16 + 16)
                for part in range(2):
                    scale = qk_scales[:, part].unsqueeze(1).broadcast_to([P, TILES, 2, HEAD_DIM // 2])
                    for k, sc in ((0, scale), (1, scale[:, :, ::-1, :])):
                        last = dve.tensor_tensor(tables[:, 2 * part + k].rearrange("p t (a b) -> p t a b", a=2),
                                                 tables[:, 2 * part + k].rearrange("p t (a b) -> p t a b", a=2), sc, ALU.mult)
                last.then_inc(tables_built, 1)
                dve.wait_ge(tables_built, layer + 1)

            def dense(s, item):
                n, kind = s.n, item[0]
                f = n - 1
                if kind == "input":
                    m = n + 1
                    for h in range(HALVES):
                        dve.wait_ge(act_read, m * FILLS + h + 1)
                        dve.tensor_tensor(xT[1][:, h, h:h + TOKENS], project[h][:, 0:TOKENS], xT[0][:, h, h:h + TOKENS].bitcast(FP32),
                                          ALU.subtract).then_inc(dve_read, 1)
                elif kind == "unit" and item[2] < 4:
                    g, u = item[1:]
                    m = n if g else n + 1
                    c, t = u % 2, u // 2
                    k = rotation(m, g, u)
                    dve.wait_ge(act_read, unit_fill(m, g, u))

                    def heads(ap):
                        return ap.rearrange("p (h a b) -> p h a b", h=GROUP_HEADS, a=2)

                    def table(k):
                        return tables[:, k, t, :].rearrange("p (a b) -> p a b", a=2).unsqueeze(1)\
                            .broadcast_to([P, GROUP_HEADS, 2, HEAD_DIM // 2])

                    dve.tensor_reduce(sums_sq[:, u, :], with_sin[:, u, :].rearrange("p (h d) -> p h d", h=GROUP_HEADS), AXIS_X,
                                      ALU.add).then_inc(squares_summed, 1)
                    dve.wait_ge(squares_summed, k)
                    dve.tensor_tensor(heads(with_sin[:, u, :]), heads(with_cos[:, u, :])[:, :, ::-1, :], table(2 * c + 1), ALU.mult)
                    floor = NORM_FLOOR if c else NORM_FLOOR / QK_SCALE ** 2
                    dve.tensor_scalar(sums_sq[:, u, :], sums_sq[:, u, :], floor, None, ALU.max).then_inc(floored, 1)
                    dve.wait_ge(floored, k)
                    dve.tensor_tensor(heads(with_cos[:, u, :]), heads(with_cos[:, u, :]), table(2 * c), ALU.mult).then_inc(parts_ready, 1)
                elif kind == "project_out" and item[1] == 1:
                    dve.wait_ge(attn_projected, f + 1)
                    dve.wait_ge(res_loaded, f * 16 + 16)
                    dve.tensor_tensor(res[:], acc[:], res[:], ALU.add).then_inc(acc_read, 1)
                elif kind == "norm_stats":
                    dve.wait_ge(shifted, f * 32 + 32)
                    dve.wait_ge(row_cleared, f + 1)
                    dve.wait_ge(acc_read, f * 2 + 1 + 1)
                    for t in range(TILES):
                        dve.bn_stats(ln_stats[:, t, 0, :], res[:, t, 0:P])
                        last = dve.bn_stats(ln_stats[:, t, 1, :], xn[:, t, P:DIM])
                    last.then_inc(ln_stated, 1)
                    wait_apart(dve, ln_stated, f + 1, passed)
                    for t in range(TILES):
                        last = dve.bn_aggr(ln_mv[:, t, :], ln_stats[:, t].rearrange("p a b -> p (a b)"))
                    last.then_inc(ln_moments, 1)
                elif kind == "norm_apply":
                    dve.wait_ge(ln_root, f + 1)
                    for t in range(TILES):
                        dve.tensor_scalar(xn[:, t, 0:P], res[:, t, 0:P], ln_mv[:, t, 0:1], ln_rstd[:, t:t + 1], ALU.subtract, ALU.mult)
                        last = dve.tensor_scalar(xn[:, t, P:DIM], xn[:, t, P:DIM], ln_mv[:, t, 0:1], ln_rstd[:, t:t + 1],
                                                 ALU.subtract, ALU.mult)
                    last.then_inc(ln_done, 1)
                elif kind == "norm_turn":
                    dve.wait_ge(xn_high, f + 1)
                    dve.tensor_tensor(xnT[1][:], xn[:], xnT[0][:].bitcast(FP32), ALU.subtract).then_inc(xn_low, 1)
                elif kind == "gate":
                    i = item[1]
                    dve.wait_ge(wide_filled, f * WIDE_FILLS + 2 + i)
                    if i == 0:
                        dve.wait_ge(params_loaded, s.layer * 32 + 32)
                        wait(dve, h_low, f * 3 + 1)
                    for k in range(2):
                        j = FFN_TILES + 2 * i + k
                        last = dve.tensor_scalar(gates[:, 2 * i + k, :], wide[:, k, :], params[:, j:j + 1], None, ALU.add)
                    last.then_inc(wide_read, 1)
                elif kind == "value":
                    i = item[1]
                    dve.wait_ge(wide_filled, f * WIDE_FILLS + 5 + i)
                    dve.wait_ge(gelu_done, f + 1)
                    for k in range(2):
                        j = 2 * i + k
                        rows = P if j < FFN_TILES - 1 else FFN_REST
                        last = dve.scalar_tensor_tensor(gates[0:rows, j, :], wide[0:rows, k, :], params[0:rows, j:j + 1],
                                                        gates[0:rows, j, :], ALU.add, ALU.mult)
                    last.then_inc(wide_read, 1)
                elif kind == "residual":
                    dve.wait_ge(h_used, f * 3 + 3 + 1)
                    dve.wait_ge(res_ready, f + 1)
                    dve.tensor_tensor(res[:], acc[:], res[:], ALU.add).then_inc(acc_read, 1)

            def slot(s):
                if isinstance(s.n, int) and s.n == -1:
                    for blk in range(WEIGHT_BLOCKS):
                        split(blk, 0)
                    build_tables(0)
                for t in range(HEADS):
                    h4 = (t - 1) % 4
                    before = s.head(t, 1)
                    if before is not None:
                        dve.wait_ge(exp_done, before + 1)
                        dve.reciprocal(inv_sums[:, h4, :], sums[:, h4, :]).then_inc(sums_inverted, 1)
                    H = s.head(t, 0)
                    if H is not None:
                        if t % GROUP_HEADS == 0:
                            dve.wait_ge(rotated, s.n * ROTATIONS + 4 * (t // GROUP_HEADS) + 4)
                        dve.wait_ge(scores_ready, H + 1)
                        wait(dve, exp_done, H - 1)
                        dve.sem_inc(passed, 1)
                        for i, (a, b) in enumerate(((0, BAND0), (BAND0, BAND))):
                            last = dve.tensor_tensor_reduce(out=masked[:, t % 2, a:b], in0=score[t % 2][:, a:b], in1=mask[:, a:b],
                                                            scale=query_scale[:, i, t:t + 1], scalar=3e38, op0=ALU.add, op1=ALU.min,
                                                            accum_out=shift[:, t % 2, i:i + 1])
                        last.then_inc(scores_masked, 1)
                    if before is not None:
                        dve.wait_ge(sums_inverted, before + 1)
                        for i, (a, b) in enumerate(((0, P), (P + WINDOW, PROBS))):
                            last = dve.tensor_scalar(probs[:, h4, a:b], probs[:, h4, a:b], inv_sums[:, h4, i:i + 1], None, ALU.mult)
                        last.then_inc(probs_scaled, 1)
                    H = s.head(t, 2)
                    if H is not None and t % 2 == 1:
                        dve.wait_ge(probs_turned, H + 1)
                        wait(dve, mixed, H - 1)
                        dve.tensor_copy(probsT[:, t % 2, :], turned[:, 0:BAND]).then_inc(probsT_copied, 1)
                    H = s.head(t, 3)
                    if H is not None and (t - 3) % 2 == 1:
                        pair = ((t - 3) % HEADS) // 2
                        dve.wait_ge(out_high, s.n * PAIRS + (t - 3) // 2 + 1)
                        dve.tensor_tensor(oT[1][:, pair, :], mix[:, pair % 2, :], oT[0][:, pair, :].bitcast(FP32),
                                          ALU.subtract).then_inc(out_split, 1)
                    for item in s.vector_dense(t):
                        dense(s, item)
                    for blk in s.splits(t):
                        split(blk, s.layer + 1)
                    if s.switch == "projections" and t == TABLES_TICK:
                        build_tables(s.layer + 1)

            for semaphore in (acc_read, xn_low, wide_read):
                dve.sem_inc(semaphore, 1)
            run_slots(dve, slot)
            with dve.Fori(0, BATCH) as b:
                dve.wait_ge(final_in, b * 32 + 32)
                dve.tensor_tensor(res[:], y_in[:], res[:], ALU.add).then_inc(final_added, 1)


def decoder_kernel(nc, D):
    with ExitStack() as ctx:
        T = {
            "ident": ctx.enter_context(nc.sbuf_tensor("ident", [P, P], FP32)),
            "mask": ctx.enter_context(nc.sbuf_tensor("mask", [P, BAND], FP32)),
            "half": ctx.enter_context(nc.sbuf_tensor("half", [P, GROUP_HEADS], FP32)),
        }
        front(nc, T, D, None)
        layers(nc, T, D)


def shape_constants():
    import numpy as np
    f32 = np.float32
    i = np.arange(TOKENS)
    allowed = (i[:, None] >= i[None, :]) & (i[:, None] <= i[None, :] + WINDOW)
    band = np.where(allowed, 0.0, MASKED).astype(f32)
    mask = np.concatenate([band[0:P, 0:P], band[P:TOKENS, P - WINDOW:TOKENS]], axis=1)
    halfdim = np.arange(0, HEAD_DIM, 2, dtype=f32)
    inv_freq = (f32(1.0) / f32(10000.0) ** (halfdim / f32(HEAD_DIM))).astype(f32)
    t = np.arange(TOKENS, dtype=f32)
    freqs = (t[:, None] * inv_freq[None, :]).astype(f32)
    base = ((halfdim + f32(0.4 * HEAD_DIM)) / f32(1.4 * HEAD_DIM)).astype(f32)
    power = ((t - TOKENS // 2) / f32(WINDOW // 2)).astype(f32)
    scale = (base[None, :] ** power[:, None]).astype(f32)
    cos, sin = np.cos(freqs), np.sin(freqs)
    parts = []
    for cs, sn, sign in ((cos * scale, sin * scale, 1.0), (cos / scale, sin / scale, -1.0)):
        parts += [sign * np.concatenate([cs, cs], 1), sign * np.concatenate([-sn, sn], 1)]
    rope = np.stack(parts).astype(f32).reshape(4, TILES, P, HEAD_DIM).transpose(2, 0, 1, 3)
    return {"ident": np.eye(P, dtype=f32), "mask": mask, "rope": np.ascontiguousarray(rope)}


def kernel(**inputs):
    import numpy as np
    import concourse.bacc as bacc
    from concourse.bass_utils import run_bass_kernel_spmd

    a = {k: np.asarray(v) for k, v in inputs.items()}

    def columns(rows):
        tiles = (rows.shape[1] + P - 1) // P
        padded = np.zeros((rows.shape[0], tiles * P), rows.dtype)
        padded[:, :rows.shape[1]] = rows
        return padded.reshape(rows.shape[0], tiles, P).transpose(0, 2, 1)

    b1 = a["L0_ffn_b1"]
    arrays = {
        "x": a["x"],
        "ctxT": a["ctx_1024"].transpose(0, 2, 1),
        "mem_wk": a["L0_attn_W_K"],
        "mem_w1t": a["L0_attn_W1"].T,
        "mem_w2t": a["L0_attn_W2"].T,
        "cross_wq": a["L0_xattn_Wq"],
        "cross_wk": a["L0_xattn_Wk"],
        "cross_wv": a["L0_xattn_Wv"],
        "cross_bqk": np.concatenate([columns(a["L0_xattn_bq"][None])[0], columns(a["L0_xattn_bk"][None])[0]], axis=1),
        "cross_bv": a["L0_xattn_bv"][None],
        "w_qkv": a["L0_ffn_Wqkv"],
        "w_out": a["L0_ffn_Wo"],
        "w_up": a["L0_ffn_W1"],
        "w_down": a["L0_ffn_W2"],
        "b_down": a["L0_ffn_b2"],
        "params": np.concatenate([columns(b1[:, :FFN]), columns(b1[:, FFN:]), columns(a["L0_ffn_ln_g"]),
                                  columns(a["L0_ffn_ln_b"])], axis=2),
        "qk_scales": np.concatenate([a["L0_ffn_q_scale"], a["L0_ffn_k_scale"]], axis=1),
    }
    arrays.update(shape_constants())
    arrays = {k: np.ascontiguousarray(v) for k, v in arrays.items()}

    nc = bacc.Bacc("TRN2", target_bir_lowering=False, num_devices=1)
    D = {name: nc.dram_tensor(f"in_{name}", v.shape, mybir.dt.from_np(v.dtype), kind="ExternalInput").ap()
         for name, v in arrays.items()}
    D["out"] = nc.dram_tensor("out", (BATCH, TOKENS, DIM), FP32, kind="ExternalOutput").ap()
    for name in ("x2", "y"):
        D[name] = nc.dram_tensor(f"{name}_scratch", (BATCH, TOKENS, DIM), FP32, kind="Internal").ap()
    decoder_kernel(nc, D)
    r = run_bass_kernel_spmd(nc, [{f"in_{name}": v for name, v in arrays.items()}], core_ids=[0])
    return r.results[0]["out"]
```

```python
import concourse.bass as bass
from concourse import mybir
from contextlib import ExitStack

FP32 = mybir.dt.float32
FP32R = mybir.dt.float32r
ALU = mybir.AluOpType
ACT = mybir.ActivationFunctionType
AXIS_X = mybir.AxisListType.X

P = 128
BATCH, TOKENS, DIM = 8, 256, 256
TILES = TOKENS // P
HALVES = DIM // P
MEMORY = 64
DEPTH, HEADS, HEAD_DIM, WINDOW = 6, 16, 64, 64
INNER = HEADS * HEAD_DIM
FFN = int(DIM * 4 * 2 / 3)
FFN_TILES = (FFN + P - 1) // P
FFN_REST = FFN - (FFN_TILES - 1) * P
QK_SCALE = 8.0
EPS = 1e-5
NORM_FLOOR = 1e-24
MASKED = 1e30

STEPS = DEPTH * BATCH
PAIRS = HEADS // 2
GROUPS = 2
GROUP_HEADS = HEADS // GROUPS
GROUP = GROUP_HEADS * HEAD_DIM
W1_COLS = 2 * FFN + FFN_TILES * P - FFN
BAND0, BAND1 = P, P + WINDOW
BAND = BAND0 + BAND1
PROBS = P + WINDOW + BAND1

FILLS = 22
DVE_READS = 2
ROTATIONS = 8
WIDE_FILLS = 7
WEIGHT_PIECES = (6, 6, 4, 3, 3, 3)
LAYER_PIECES = sum(WEIGHT_PIECES)
PIECES_UPTO = [sum(WEIGHT_PIECES[:blk]) for blk in range(len(WEIGHT_PIECES) + 1)]
WEIGHT_LOADS = (32, 64, 80, 112, 112, 144)

SCHEDULE = {
    0: [("unit", 1, 0)],
    1: [("rotate", 1, 0), ("unit", 1, 1), ("rotate", 1, 1), ("unit", 1, 2)],
    2: [("unit", 1, 3), ("rotate", 1, 2), ("turn", 1, 0)],
    3: [("rotate", 1, 3), ("project_out", 0), ("turn", 1, 1)],
    4: [("project_out", 1), ("turn", 1, 2), ("add_out",)],
    5: [("unit", 1, 4)],
    6: [("turn", 1, 3), ("unit", 1, 5), ("norm_stats",), ("input",)],
    7: [("unit", 0, 0), ("norm_apply",)],
    8: [("rotate", 0, 0), ("norm_turn",)],
    9: [("unit", 0, 1), ("gate", 0), ("rotate", 0, 1), ("unit", 0, 2), ("gate", 1)],
    10: [("rotate", 0, 2), ("unit", 0, 3), ("turn", 0, 0), ("gate", 2), ("gelu",)],
    11: [("value", 0), ("rotate", 0, 3), ("turn", 0, 1), ("unit", 0, 4), ("low", 0)],
    12: [("value", 1), ("down", 0), ("turn", 0, 2), ("low", 1)],
    13: [("value", 2), ("down", 1), ("turn", 0, 3), ("low", 2)],
    14: [("down", 2)],
    15: [("unit", 0, 5), ("residual",)],
}
SPLITS = {
    "projections": {0: [(0, 0), (0, 1)], 3: [(0, 2), (0, 3)], 4: [(0, 4), (0, 5)],
                    8: [(1, 0)], 9: [(1, 1)], 11: [(1, 2)], 12: [(1, 3)], 13: [(1, 4)], 14: [(1, 5)]},
    "ffn": {7: [(2, 0), (2, 1)], 8: [(2, 2), (2, 3)], 11: [(3, 0), (3, 1)], 12: [(3, 2)], 13: [(4, 0), (4, 1)],
            14: [(4, 2), (5, 0)], 15: [(5, 1), (5, 2)]},
}
TABLES_TICK = 6
UNIT_AT, TRANSPOSE_AT = [{}, {}], [{}, {}]
for _tick in range(HEADS):
    for _item in SCHEDULE[_tick]:
        if _item[0] in ("unit", "turn"):
            _g, _u = _item[1:]
            (UNIT_AT if _item[0] == "unit" else TRANSPOSE_AT)[_g][_u] = len(UNIT_AT[_g]) + len(TRANSPOSE_AT[_g]) + 1


def wait(eng, semaphore, value):
    if not isinstance(value, int) or value > 0:
        eng.wait_ge(semaphore, value)


def wait_apart(eng, semaphore, value, passed):
    eng.wait_ge(semaphore, value)
    eng.sem_inc(passed, 1)


class Slot:

    def __init__(self, n, layer=0, attend=True, ffn=True, late=True, early=True,
                 late_layer=None, early_layer=None, switch=None, next_batch=None, ffn_batch=None):
        self.n, self.layer, self.attend, self.ffn, self.late, self.early = n, layer, attend, ffn, late, early
        self.late_layer = layer if late_layer is None else late_layer
        self.early_layer = layer if early_layer is None else early_layer
        self.switch = switch
        self.last = isinstance(layer, int) and layer == DEPTH - 1
        self.next_batch, self.ffn_batch = next_batch, ffn_batch

    def head(self, t, lag):
        if isinstance(self.n, int) and HEADS * self.n + t - lag < 0:
            return None
        if not self.attend and t >= lag:
            return None
        return HEADS * self.n + t - lag

    def dense(self, t):
        for item in SCHEDULE[t]:
            kind = item[0]
            if kind in ("unit", "rotate", "turn"):
                if (self.late if item[1] else self.early):
                    yield item
            elif kind == "input":
                if self.early:
                    yield item
            elif self.ffn:
                yield item

    def splits(self, t):
        return SPLITS.get(self.switch, {}).get(t, [])


def run_slots(eng, slot, before_layer=None):
    slot(Slot(-1, attend=False, ffn=False, late=False, next_batch=0))
    slot(Slot(0, ffn=False, next_batch=1))
    with eng.Fori(0, DEPTH - 1) as layer:
        if before_layer:
            before_layer(layer)
        with eng.Fori(1, BATCH - 1) as b:
            slot(Slot(layer * BATCH + b, layer, next_batch=b + 1, ffn_batch=b - 1))
        slot(Slot(layer * BATCH + (BATCH - 1), layer, early_layer=layer + 1, switch="projections",
                  next_batch=0, ffn_batch=BATCH - 2))
        slot(Slot(layer * BATCH + BATCH, layer, late_layer=layer + 1, early_layer=layer + 1,
                  switch="ffn", next_batch=1, ffn_batch=BATCH - 1))
    last = DEPTH - 1
    with eng.Fori(1, BATCH - 1) as b:
        slot(Slot(last * BATCH + b, last, next_batch=b + 1, ffn_batch=b - 1))
    slot(Slot(STEPS - 1, last, early=False, ffn_batch=BATCH - 2))
    slot(Slot(STEPS, last, attend=False, late=False, early=False, ffn_batch=BATCH - 1))


class Weights:
    STAGING = HALVES * 3 * GROUP

    def __init__(self, nc, ctx, D):
        def two(name, shape):
            return [ctx.enter_context(nc.sbuf_tensor(f"{name}{part}", shape, FP32R)) for part in range(2)]

        self.D = D
        self.qkv = two("w_qkv", [P, HALVES, 3, GROUPS, GROUP])
        self.out = two("w_out", [P, PAIRS, DIM])
        self.up = two("w_up", [P, HALVES, W1_COLS])
        self.down = two("w_down", [P, FFN_TILES, DIM])
        self.staging = ctx.enter_context(nc.sbuf_tensor("staging", [P, self.STAGING], FP32))
        self.loaded, self.high, self.low = (ctx.enter_context(nc.semaphore(name)) for name in ("w_loaded", "w_high", "w_low"))

    def staged(self, blk):
        if blk < 2:
            return self.staging[:].rearrange("p (k c n) -> p k c n", k=HALVES, c=3)
        if blk == 2:
            return self.staging[:, 0:PAIRS * DIM].rearrange("p (k n) -> p k n", k=PAIRS)
        if blk == 5:
            return self.staging[:, 0:FFN_TILES * DIM].rearrange("p (k n) -> p k n", k=FFN_TILES)
        at = 0 if blk == 3 else self.STAGING - HALVES * FFN
        return self.staging[:, at:at + HALVES * FFN].rearrange("p (k n) -> p k n", k=HALVES)

    def split_views(self, blk):
        """The pieces of a block, each a list of (staged values, high part, low part)."""
        s = self.staged(blk)
        if blk < 2:
            return [[(s[:, k, c], self.qkv[0][:, k, c, blk, :], self.qkv[1][:, k, c, blk, :])] for k in range(HALVES) for c in range(3)]
        if blk == 2:
            return [[(s[:, k:k + 2], self.out[0][:, k:k + 2], self.out[1][:, k:k + 2])] for k in range(0, PAIRS, 2)]
        if blk < 5:
            pieces = []
            for a in range(0, FFN, 2 * P):
                b = min(a + 2 * P, FFN)
                at = FFN if blk == 3 else 0
                pieces.append([(s[:, :, a:b], self.up[0][:, :, at + a:at + b], self.up[1][:, :, at + a:at + b])])
            return pieces
        pieces = [[(s[:, k:k + 2], self.down[0][:, k:k + 2], self.down[1][:, k:k + 2])] for k in (0, 2)]
        return pieces + [[(s[0:rows, k], self.down[0][0:rows, k], self.down[1][0:rows, k])
                          for k, rows in ((FFN_TILES - 2, P), (FFN_TILES - 1, FFN_REST))]]

    def stage(self, sp, blk, layer):
        if blk != 4:
            wait(sp, self.low, layer * LAYER_PIECES + PIECES_UPTO[4 if blk == 5 else blk])
        dst = self.staged(blk)
        if blk < 2:
            src = self.D["w_qkv"][layer].rearrange("(k p) (c g n) -> k p c g n", p=P, c=3, g=GROUPS)
            for k in range(HALVES):
                sp.dma_start(dst[:, k], src[k, :, :, blk, :]).then_inc(self.loaded, 16)
        elif blk == 2:
            sp.dma_start(dst, self.D["w_out"][layer].rearrange("(k p) n -> p k n", p=P)).then_inc(self.loaded, 16)
        elif blk < 5:
            cols = slice(FFN, 2 * FFN) if blk == 3 else slice(0, FFN)
            sp.dma_start(dst, self.D["w_up"][layer][:, cols].rearrange("(k p) n -> p k n", p=P)).then_inc(self.loaded, 16)
        else:
            full = (FFN_TILES - 1) * P
            sp.dma_start(dst[:, 0:FFN_TILES - 1],
                         self.D["w_down"][layer][0:full, :].rearrange("(k p) n -> p k n", p=P)).then_inc(self.loaded, 16)
            sp.dma_start(dst[0:FFN_REST, FFN_TILES - 1], self.D["w_down"][layer][full:FFN, :]).then_inc(self.loaded, 16)

    def split_high(self, act, blk, piece, layer):
        act.wait_ge(self.loaded, layer * WEIGHT_LOADS[-1] + WEIGHT_LOADS[blk])
        for raw, high, _ in self.split_views(blk)[piece]:
            last = act.copy(high, raw)
        last.then_inc(self.high, 1)

    def split_low(self, dve, blk, piece, layer):
        dve.wait_ge(self.high, layer * LAYER_PIECES + PIECES_UPTO[blk] + piece + 1)
        for raw, high, low in self.split_views(blk)[piece]:
            last = dve.tensor_tensor(low, raw, high.bitcast(FP32), ALU.subtract)
        last.then_inc(self.low, 1)


def front(nc, T, D, W):
    with ExitStack() as ctx:
        def sb(name, shape, dt=FP32):
            return ctx.enter_context(nc.sbuf_tensor(name, shape, dt))

        def sem(name):
            return ctx.enter_context(nc.semaphore(name))

        QUAD = 4
        wk_mem = sb("wk_mem", [P, HALVES, DIM])
        w1t_mem = sb("w1t_mem", [P, HALVES, MEMORY])
        hidden_w = sb("hidden_w", [P, HALVES, MEMORY])
        w2t_mem = sb("w2t_mem", [MEMORY, DIM])
        wq = sb("wq_cross", [P, HALVES, DIM])
        wk = sb("wk_cross", [P, HALVES, DIM])
        wv = sb("wv_cross", [P, HALVES, DIM])
        bqk = sb("bqk", [P, 2 * HALVES])
        bv = sb("bv", [P, DIM])
        x = [sb(f"x{k}", [P, TILES, DIM]) for k in range(BATCH)]
        xn = [sb(f"xn{j}", [P, TILES, DIM]) for j in range(QUAD)]
        xnT = [sb(f"xnT{j}", [P, HALVES, TOKENS]) for j in range(QUAD)]
        ctxT = [sb(f"ctxT{j}", [P, HALVES, TOKENS]) for j in range(QUAD)]
        hidT = [sb(f"hidT{j}", [MEMORY, TOKENS]) for j in range(QUAD)]
        qT = [sb(f"fqT{j}", [P, HALVES, TOKENS]) for j in range(QUAD)]
        y = qT
        kT = [sb(f"fkT{j}", [P, HALVES, TOKENS]) for j in range(QUAD)]
        v = [sb(f"fv{j}", [P, TILES, DIM]) for j in range(QUAD)]
        pr = xnT
        prT = [sb(f"fpT{j}", [P, TILES, TOKENS]) for j in range(QUAD)]
        st = [sb(f"fst{j}", [P, TILES, 6]) for j in range(QUAD)]
        mv = [sb(f"fmv{j}", [P, TILES, 2]) for j in range(QUAD)]
        rstd = [sb(f"frstd{j}", [P, TILES]) for j in range(QUAD)]
        mx = [sb(f"fmx{j}", [P, TILES]) for j in range(QUAD)]
        nb = [sb(f"fnb{j}", [P, TILES]) for j in range(QUAD)]
        sm = [sb(f"fsm{j}", [P, TILES]) for j in range(QUAD)]
        rs = [sb(f"frs{j}", [P, TILES]) for j in range(QUAD)]
        bank = [[ctx.enter_context(nc.psum_tensor(f"fb{j}{i}", [P, 2, DIM], FP32)) for i in range(2)]
                for j in range(QUAD)]

        weights_in = sem("f_weights_in")
        x_in, ctx_in = [sem(f"f_x_in{i}") for i in range(2)], sem("f_ctx_in")
        folded_ready, folded = sem("f_folded_ready"), sem("f_folded")
        stats, moments, root, normed = sem("f_stats"), sem("f_moments"), sem("f_root"), sem("f_normed")
        pool_step = sem("f_pool_step")
        turned, turned_out = sem("f_turned"), sem("f_turned_out")
        hid_ready, hid_act = sem("f_hid_ready"), sem("f_hid_act")
        read_ready, read_added = sem("f_read_ready"), sem("f_read_added")
        kv_ready, k_out, v_out = sem("f_kv_ready"), sem("f_k_out"), sem("f_v_out")
        q_ready, q_out = sem("f_q_ready"), sem("f_q_out")
        score_ready, top, shift = sem("f_score_ready"), sem("f_top"), sem("f_shift")
        probs, inverse = sem("f_probs"), sem("f_inverse")
        probs_turned, probs_out = sem("f_probs_turned"), sem("f_probs_out")
        cross_ready, cross_added = sem("f_cross_ready"), sem("f_cross_added")
        x2_stored, y_stored = sem("f_x2_stored"), sem("f_y_stored")
        passed = sem("f_passed")
        block = ctx.enter_context(nc.Block())
        ident = T["ident"]
        QUADS = BATCH // QUAD

        def as_tiles(seq):
            return seq.rearrange("(t p) d -> p t d", p=P)

        LN_ORDER = [(0, 0), (0, 1), (1, 0), (0, 2), (1, 1), (1, 2)]

        def ln_index(i, s, j):
            return LN_ORDER.index((i, s)) * QUAD + j

        @block.sync
        def _(sp):
            for k in range(QUAD):
                sp.dma_start(x[k][:], as_tiles(D["x"][k])).then_inc(x_in[0], 16)
            sp.dma_start(T["ident"][:], D["ident"]).then_inc(weights_in, 16)
            sp.dma_start(T["mask"][:], D["mask"]).then_inc(weights_in, 16)
            for dst, src in ((wk_mem, "mem_wk"), (w1t_mem, "mem_w1t"), (wq, "cross_wq"), (wk, "cross_wk"), (wv, "cross_wv")):
                sp.dma_start(dst[:], D[src].rearrange("(k p) n -> p k n", p=P)).then_inc(weights_in, 16)
            sp.dma_start(w2t_mem[:], D["mem_w2t"]).then_inc(weights_in, 16)
            sp.dma_start(bqk[:], D["cross_bqk"]).then_inc(weights_in, 16)
            sp.dma_start(bv[:], D["cross_bv"].broadcast_to([P, DIM])).then_inc(weights_in, 16)
            def load_context(k):
                sp.dma_start(ctxT[k % QUAD][:], D["ctxT"][k].rearrange("(k p) t -> p k t", p=P)).then_inc(ctx_in, 16)

            for k in range(QUAD):
                load_context(k)
            for k in range(QUAD, BATCH):
                sp.dma_start(x[k][:], as_tiles(D["x"][k])).then_inc(x_in[1], 16)
            for blk in range(len(WEIGHT_PIECES) - 1):
                W.stage(sp, blk, 0)
            for i in range(QUADS):
                if i > 0:
                    sp.wait_ge(kv_ready, i * (2 * QUAD))
                    for j in range(QUAD):
                        load_context(i * QUAD + j)
                    W.stage(sp, len(WEIGHT_PIECES) - 1, 0)
                for j in range(QUAD):
                    k = i * QUAD + j
                    sp.wait_ge(cross_added, k + 1)
                    sp.dma_start(as_tiles(D["x2"][k]), x[k][:]).then_inc(x2_stored, 16)
                for j in range(QUAD):
                    k = i * QUAD + j
                    sp.wait_ge(normed, ln_index(i, 2, j) + 1)
                    sp.dma_start(as_tiles(D["y"][k]), y[j][:]).then_inc(y_stored, 16)
            sp.wait_ge(x2_stored, BATCH * 16)
            sp.wait_ge(y_stored, BATCH * 16)

        @block.tensor
        def _(pe):
            pe.wait_ge(weights_in, 16 * 10)
            for h in range(HALVES):
                for k in range(HALVES):
                    last = pe.matmul(bank[0][1][:, h, 0:MEMORY], wk_mem[:, k, h * P:(h + 1) * P], w1t_mem[:, k, :],
                                     start=(k == 0), stop=(k == HALVES - 1))
            last.then_inc(folded_ready, 1)
            pe.wait_ge(folded, 1)

            def turn(i, s, j):
                pe.wait_ge(normed, ln_index(i, s, j) + 1)
                for h in range(HALVES):
                    for t in range(TILES):
                        last = pe.transpose(bank[j][0][:, h, t * P:(t + 1) * P], xn[j][:, t, h * P:(h + 1) * P], ident[:])
                last.then_inc(turned, 1)

            for i in range(QUADS):
                for j in range(QUAD):
                    turn(i, 0, j)
                for j in range(QUAD):
                    pe.wait_ge(turned_out, (i * 2 + 0) * QUAD + j + 1)
                    for h in range(HALVES):
                        last = pe.matmul(bank[j][1][0:MEMORY, 0, :], hidden_w[:, h, :], xnT[j][:, h, :],
                                         start=(h == 0), stop=(h == HALVES - 1))
                    last.then_inc(hid_ready, 1)
                for j in range(QUAD):
                    pe.wait_ge(hid_act, i * QUAD + j + 1)
                    for t in range(TILES):
                        last = pe.matmul(bank[j][0][:, t, :], hidT[j][:, t * P:(t + 1) * P], w2t_mem[:],
                                         start=True, stop=True)
                    last.then_inc(read_ready, 1)
                for j in range(QUAD):
                    pe.wait_ge(ctx_in, (i + 1) * QUAD * 16)
                    for m in range(HALVES):
                        for h in range(HALVES):
                            last = pe.matmul(bank[j][1][:, m, :], wk[:, h, m * P:(m + 1) * P], ctxT[j][:, h, :],
                                             start=(h == 0), stop=(h == HALVES - 1))
                    last.then_inc(kv_ready, 1)
                for j in range(QUAD):
                    turn(i, 1, j)
                for j in range(QUAD):
                    pe.wait_ge(k_out, i * QUAD + j + 1)
                    for t in range(TILES):
                        for h in range(HALVES):
                            last = pe.matmul(bank[j][1][:, t, :], ctxT[j][:, h, t * P:(t + 1) * P], wv[:, h, :],
                                             start=(h == 0), stop=(h == HALVES - 1))
                    last.then_inc(kv_ready, 1)
                for j in range(QUAD):
                    pe.wait_ge(turned_out, (i * 2 + 1) * QUAD + j + 1)
                    for m in range(HALVES):
                        for h in range(HALVES):
                            last = pe.matmul(bank[j][0][:, m, :], wq[:, h, m * P:(m + 1) * P], xnT[j][:, h, :],
                                             start=(h == 0), stop=(h == HALVES - 1))
                    last.then_inc(q_ready, 1)
                for j in range(QUAD):
                    pe.wait_ge(q_out, i * QUAD + j + 1)
                    pe.wait_ge(v_out, i * QUAD + j + 1)
                    for t in range(TILES):
                        for h in range(HALVES):
                            last = pe.matmul(bank[j][1][:, t, :], qT[j][:, h, t * P:(t + 1) * P], kT[j][:, h, :],
                                             start=(h == 0), stop=(h == HALVES - 1))
                    last.then_inc(score_ready, 1)
                for j in range(QUAD):
                    pe.wait_ge(probs, i * QUAD + j + 1)
                    for kt in range(TILES):
                        for t in range(TILES):
                            last = pe.transpose(bank[j][0][:, kt, t * P:(t + 1) * P], pr[j][:, t, kt * P:(kt + 1) * P], ident[:])
                    last.then_inc(probs_turned, 1)
                for j in range(QUAD):
                    pe.wait_ge(probs_out, i * QUAD + j + 1)
                    for t in range(TILES):
                        for kt in range(TILES):
                            last = pe.matmul(bank[j][1][:, t, :], prT[j][:, kt, t * P:(t + 1) * P], v[j][:, kt, :],
                                             start=(kt == 0), stop=(kt == TILES - 1))
                    last.then_inc(cross_ready, 1)

        @block.scalar
        def _(act):
            for i in range(QUADS):
                for j in range(QUAD):
                    act.wait_ge(turned, (i * 2 + 0) * QUAD + j + 1)
                    act.copy(xnT[j][:], bank[j][0][:]).then_inc(turned_out, 1)
                for piece in range(WEIGHT_PIECES[3 * i]):
                    W.split_high(act, 3 * i, piece, 0)
                for j in range(QUAD):
                    act.wait_ge(hid_ready, i * QUAD + j + 1)
                    act.activation(hidT[j][:], bank[j][1][0:MEMORY, 0, :], ACT.Gelu).then_inc(hid_act, 1)
                for j in range(QUAD):
                    act.wait_ge(kv_ready, i * (2 * QUAD) + j + 1)
                    for m in range(HALVES):
                        last = act.activation(kT[j][:, m, :], bank[j][1][:, m, :], ACT.Identity,
                                              bias=bqk[:, HALVES + m:HALVES + m + 1])
                    last.then_inc(k_out, 1)
                for j in range(QUAD):
                    act.wait_ge(turned, (i * 2 + 1) * QUAD + j + 1)
                    act.copy(xnT[j][:], bank[j][0][:]).then_inc(turned_out, 1)
                for piece in range(WEIGHT_PIECES[1 + 3 * i]):
                    W.split_high(act, 1 + 3 * i, piece, 0)
                for j in range(QUAD):
                    act.wait_ge(q_ready, i * QUAD + j + 1)
                    if i > 0:
                        act.wait_ge(y_stored, i * (16 * QUAD))
                    for m in range(HALVES):
                        last = act.activation(qT[j][:, m, :], bank[j][0][:, m, :], ACT.Identity, bias=bqk[:, m:m + 1])
                    last.then_inc(q_out, 1)
                for j in range(QUAD):
                    act.wait_ge(shift, i * QUAD + j + 1)
                    for t in range(TILES):
                        last = act.activation(pr[j][:, t, :], bank[j][1][:, t, :], ACT.Exp, bias=nb[j][:, t:t + 1],
                                              scale=DIM ** -0.5, accum_out=sm[j][:, t:t + 1])
                    last.then_inc(probs, 1)
                for piece in range(WEIGHT_PIECES[2 + 3 * i]):
                    W.split_high(act, 2 + 3 * i, piece, 0)
                for j in range(QUAD):
                    act.wait_ge(probs_turned, i * QUAD + j + 1)
                    act.copy(prT[j][:], bank[j][0][:]).then_inc(probs_out, 1)

        @block.gpsimd
        def _(pool):
            nc.gpsimd.memset(T["half"][:], -0.5).then_inc(pool_step, 1)
            pool.wait_ge(pool_step, 1)
            for part in W.up:
                pool.memset(part[:, :, 2 * FFN:W1_COLS].bitcast(FP32), 0.0)
            for i, s in LN_ORDER:
                for j in range(QUAD):
                    k = ln_index(i, s, j)
                    wait_apart(pool, moments, k + 1, passed)
                    pool.tensor_scalar(mv[j][:, :, 1], mv[j][:, :, 1], EPS, None, ALU.add).then_inc(pool_step, 1)
                    pool.wait_ge(pool_step, k + 2)
                    pool.tensor_tensor(rstd[j][:], mv[j][:, :, 1], T["half"][:, 0:TILES], ALU.pow).then_inc(root, 1)
                for blk in {(0, 0): (0,), (0, 1): (1, 2), (0, 2): (3,), (1, 1): (4, 5)}.get((i, s), ()):
                    for piece in range(WEIGHT_PIECES[blk]):
                        W.split_low(pool, blk, piece, 0)

        @block.vector
        def _(dve):
            dve.wait_ge(folded_ready, 1)
            dve.tensor_copy(hidden_w[:], bank[0][1][:, :, 0:MEMORY]).then_inc(folded, 1)

            def layer_norm(i, s, arrived):
                for j in range(QUAD):
                    arrived(j)
                    for t in range(TILES):
                        last = dve.bn_stats(st[j][:, t, :], x[i * QUAD + j][:, t, :])
                    last.then_inc(stats, 1)
                    if j > 0:
                        aggregate(i, s, j - 1)
                aggregate(i, s, QUAD - 1)
                for j in range(QUAD):
                    dve.wait_ge(root, ln_index(i, s, j) + 1)
                    for t in range(TILES):
                        last = dve.tensor_scalar((y if s == 2 else xn)[j][:, t, :], x[i * QUAD + j][:, t, :], mv[j][:, t, 0:1], rstd[j][:, t:t + 1],
                                                 ALU.subtract, ALU.mult)
                    last.then_inc(normed, 1)

            def aggregate(i, s, j):
                wait_apart(dve, stats, ln_index(i, s, j) + 1, passed)
                for t in range(TILES):
                    last = dve.bn_aggr(mv[j][:, t, :], st[j][:, t, :])
                last.then_inc(moments, 1)

            for i in range(QUADS):
                if i == 0:
                    layer_norm(0, 0, lambda j: dve.wait_ge(x_in[0], QUAD * 16))
                for j in range(QUAD):
                    dve.wait_ge(read_ready, i * QUAD + j + 1)
                    dve.tensor_tensor(x[i * QUAD + j][:], bank[j][0][:], x[i * QUAD + j][:], ALU.add).then_inc(read_added, 1)
                layer_norm(i, 1, lambda j: dve.wait_ge(read_added, i * QUAD + j + 1))
                for j in range(QUAD):
                    dve.wait_ge(kv_ready, i * (2 * QUAD) + QUAD + j + 1)
                    dve.tensor_tensor(v[j][:], bank[j][1][:], bv[:].unsqueeze(1).broadcast_to([P, TILES, DIM]),
                                      ALU.add).then_inc(v_out, 1)
                for j in range(QUAD):
                    k = i * QUAD + j
                    dve.wait_ge(score_ready, k + 1)
                    dve.tensor_reduce(mx[j][:], bank[j][1][:], AXIS_X, ALU.max).then_inc(top, 1)
                    dve.wait_ge(top, k + 1)
                    dve.tensor_scalar(nb[j][:], mx[j][:], -(DIM ** -0.5), None, ALU.mult).then_inc(shift, 1)
                for j in range(QUAD):
                    dve.wait_ge(probs, i * QUAD + j + 1)
                    dve.reciprocal(rs[j][:], sm[j][:]).then_inc(inverse, 1)
                for j in range(QUAD):
                    k = i * QUAD + j
                    dve.wait_ge(cross_ready, k + 1)
                    dve.wait_ge(inverse, k + 1)
                    for t in range(TILES):
                        last = dve.scalar_tensor_tensor(x[k][:, t, :], bank[j][1][:, t, :], rs[j][:, t:t + 1],
                                                        x[k][:, t, :], ALU.mult, ALU.add)
                    last.then_inc(cross_added, 1)
                if i == 0:
                    layer_norm(1, 0, lambda j: dve.wait_ge(x_in[1], QUAD * 16))
                layer_norm(i, 2, lambda j: dve.wait_ge(cross_added, i * QUAD + j + 1))


def layers(nc, T, D, W):
    with ExitStack() as ctx:
        def sb(name, shape, dt=FP32):
            return ctx.enter_context(nc.sbuf_tensor(name, shape, dt))

        def sem(name):
            return ctx.enter_context(nc.semaphore(name))

        w_qkv, w_out, w_up, w_down = W.qkv, W.out, W.up, W.down
        params = sb("params", [P, 2 * FFN_TILES + 2 * HALVES])
        b_down = sb("b_down", [P, DIM])
        qk_scales = sb("qk_scales", [P, 2, 2, HEAD_DIM // 2])
        tables = sb("tables", [P, 4, TILES, HEAD_DIM])

        y_in = sb("y_in", [P, TILES, DIM])
        xT = [sb(f"xT{s}", [P, HALVES, TOKENS + 2], FP32R) for s in range(2)]
        sums_sq = sb("sums_sq", [P, 4, GROUP_HEADS])
        inv_norm = sb("inv_norm", [P, 2, GROUP_HEADS])
        query_scale = sb("query_scale", [P, TILES, HEADS])
        with_cos = sb("with_cos", [P, 4, GROUP])
        with_sin = sb("with_sin", [P, 4, GROUP])
        qT = sb("qT", [P, PAIRS, TOKENS])
        kT = sb("kT", [P, PAIRS, TOKENS])
        v = sb("v", [P, TILES, INNER])

        masked = sb("masked", [P, 2, BAND])
        shift = sb("shift", [P, 2, TILES])
        sums = sb("sums", [P, 4, TILES])
        inv_sums = sb("inv_sums", [P, 4, TILES])
        probs = sb("probs", [P, 4, PROBS])
        probsT = sb("probsT", [P, 2, BAND])
        oT = [sb(f"oT{s}", [P, PAIRS, TOKENS], FP32R) for s in range(2)]

        res = sb("res", [P, TILES, DIM])
        ln_stats = sb("ln_stats", [P, TILES, HALVES, 6])
        ln_mv = sb("ln_mv", [P, TILES, 2])
        ln_rstd = sb("ln_rstd", [P, TILES])
        xn = sb("xn", [P, TILES, DIM])
        xnT = [sb(f"nT{s}", [P, HALVES, TOKENS], FP32R) for s in range(2)]
        gates = sb("gates", [P, FFN_TILES, TOKENS])
        hT = [sb(f"hT{s}", [P, 2, TOKENS], FP32R) for s in range(2)]

        project = [ctx.enter_context(nc.psum_tensor(f"project{i}", [P, GROUP], FP32)) for i in range(2)]
        score = [ctx.enter_context(nc.psum_tensor(f"score{i}", [P, GROUP], FP32)) for i in range(2)]
        turned = ctx.enter_context(nc.psum_tensor("turned", [P, GROUP], FP32))
        mix = ctx.enter_context(nc.psum_tensor("mix", [P, 2, TOKENS], FP32))
        wide = ctx.enter_context(nc.psum_tensor("wide", [P, 2, TOKENS], FP32))
        acc = ctx.enter_context(nc.psum_tensor("acc", [P, TILES, DIM], FP32))

        w_low = W.low
        params_loaded, scales_loaded, tables_built = sem("params_loaded"), sem("scales_loaded"), sem("tables_built")
        cleared = sem("cleared")
        y_loaded, res_loaded, y_stored = sem("y_loaded"), sem("res_loaded"), sem("y_stored")
        filled, act_read, dve_read = sem("filled"), sem("act_read"), sem("dve_read")
        squares_summed, floored, parts_ready = sem("squares_summed"), sem("floored"), sem("parts_ready")
        rotated, pool_step, tables_loaded, row_cleared = sem("rotated"), sem("pool_step"), sem("tables_loaded"), sem("row_cleared")
        scores_ready, scores_masked, exp_done = sem("scores_ready"), sem("scores_masked"), sem("exp_done")
        sums_inverted, probs_scaled = sem("sums_inverted"), sem("probs_scaled")
        probs_turned, probsT_copied, mixed = sem("probs_turned"), sem("probsT_copied"), sem("mixed")
        out_high, out_split = sem("out_high"), sem("out_split")
        attn_projected, acc_read, shifted = sem("attn_projected"), sem("acc_read"), sem("shifted")
        ln_stated, ln_moments, ln_root, ln_done = sem("ln_stated"), sem("ln_moments"), sem("ln_root"), sem("ln_done")
        ln_floor = sem("ln_floor")
        wide_filled, wide_read = sem("wide_filled"), sem("wide_read")
        xn_high, xn_low, gelu_done = sem("xn_high"), sem("xn_low"), sem("gelu_done")
        h_high, h_low, h_used, res_ready = sem("h_high"), sem("h_low"), sem("h_used"), sem("res_ready")
        x2_loaded, bias_added, x2_added = sem("x2_loaded"), sem("bias_added"), sem("x2_added")
        passed = sem("passed")
        block = ctx.enter_context(nc.Block())
        ident, mask, half = T["ident"], T["mask"], T["half"]

        def as_tiles(seq):
            return seq.rearrange("(t p) d -> p t d", p=P)

        def unit_fill(m, g, u):
            return m * FILLS + (2 + 10 * g + UNIT_AT[g][u])

        def turn_fill(m, g, u):
            return m * FILLS + (2 + 10 * g + TRANSPOSE_AT[g][u])

        def rotation(m, g, u):
            return m * ROTATIONS + (4 * g + u + 1)

        def last_use(blk, piece, layer):
            m = layer * BATCH
            return [(filled, m * FILLS - FILLS + (2 + UNIT_AT[0][5])), (filled, m * FILLS - FILLS + (12 + UNIT_AT[1][5])),
                    (attn_projected, m), (wide_filled, m * WIDE_FILLS - WIDE_FILLS + 2 + piece),
                    (wide_filled, m * WIDE_FILLS - WIDE_FILLS + 5 + piece), (h_used, m * 3 - 3 + piece + 1 + 1)][blk]

        @block.sync
        def _(sp):
            def load_tables(layer):
                wait(sp, parts_ready, layer * (BATCH * ROTATIONS))
                sp.dma_start(tables[:], D["rope"]).then_inc(tables_loaded, 16)

            def load_scales(layer):
                wait(sp, tables_built, layer)
                sp.dma_start(qk_scales[:], D["qk_scales"][layer].rearrange("(a b c) -> a b c", a=2, b=2).unsqueeze(0)
                             .broadcast_to([P, 2, 2, HEAD_DIM // 2])).then_inc(scales_loaded, 16)

            def load_params(layer):
                wait(sp, acc_read, layer * (2 * BATCH) + 1)
                sp.dma_start(params[:], D["params"][layer]).then_inc(params_loaded, 16)
                sp.dma_start(b_down[:], D["b_down"][layer].unsqueeze(0).broadcast_to([P, DIM])).then_inc(params_loaded, 16)

            def slot(s):
                n = s.n
                f = n - 1
                if s.early:
                    wait(sp, filled, n * FILLS + 2)
                    sp.dma_start(y_in[:], as_tiles(D["y"][s.next_batch])).then_inc(y_loaded, 16)
                if isinstance(n, int) and n == -1:
                    load_tables(0)
                    load_scales(0)
                    load_params(0)
                if s.ffn:
                    wait(sp, y_stored, f * 16 + 1)
                    sp.dma_start(res[:], as_tiles(D["y"][s.ffn_batch])).then_inc(res_loaded, 16)
                if s.switch == "projections":
                    load_tables(s.layer + 1)
                if s.ffn:
                    wait(sp, acc_read, f * 2 + 1 + 1)
                    if s.last:
                        sp.wait_ge(res_ready, f)
                    else:
                        wait(sp, xn_low, f + 1)
                    sp.dma_start(xn[1:P, :, P:DIM], res[0:P - 1, :, P:DIM]).then_inc(shifted, 16)
                    sp.dma_start(xn[0:1, 1, P:DIM], res[P - 1:P, 0, P:DIM]).then_inc(shifted, 16)
                if s.switch == "projections":
                    W.stage(sp, 1, s.layer + 1)
                    W.stage(sp, 2, s.layer + 1)
                if s.switch == "ffn":
                    W.stage(sp, 3, s.layer + 1)
                    W.stage(sp, 4, s.layer + 1)
                    W.stage(sp, 5, s.layer + 1)
                if s.ffn and s.last:
                    sp.wait_ge(xn_low, f + 1 + 1)
                    sp.dma_start(xn[:], as_tiles(D["x2"][s.ffn_batch])).then_inc(x2_loaded, 16)
                if s.ffn:
                    wait(sp, acc_read, f * 2 + 2 + 1)
                    sp.dma_start(as_tiles(D["out" if s.last else "y"][s.ffn_batch]), res[:]).then_inc(y_stored, 16)
                if s.switch == "ffn":
                    load_params(s.layer + 1)

            def before_layer(layer):
                W.stage(sp, 0, layer + 1)
                load_scales(layer + 1)

            sp.sem_inc(y_stored, 1)
            run_slots(sp, slot, before_layer)
            sp.wait_ge(y_stored, STEPS * 16 + 1)

        @block.tensor
        def _(pe):
            PASSES = ((0, 0), (1, 0), (0, 1))

            def bank_free(x, m):
                y = x - 2
                step = m
                if y <= 0:
                    y, step = y + FILLS, m - 1
                if isinstance(step, int) and step < 0:
                    return
                wait(pe, act_read, step * FILLS + y)
                if y <= DVE_READS:
                    wait(pe, dve_read, step * DVE_READS + y)

            def dense(s, item):
                n, kind = s.n, item[0]
                f = n - 1
                if kind == "input":
                    m = n + 1
                    pe.wait_ge(y_loaded, m * 16 + 16)
                    for h in range(HALVES):
                        bank_free(h + 1, m)
                        for t in range(TILES):
                            last = pe.transpose(project[h][:, t * P:(t + 1) * P], y_in[:, t, h * P:(h + 1) * P], ident[:])
                        last.then_inc(filled, 1)
                elif kind == "unit":
                    g, u = item[1:]
                    m = n if g else n + 1
                    c, t = (u % 2, u // 2) if u < 4 else (2, u - 4)
                    if u == 0:
                        pe.wait_ge(w_low, (s.late_layer if g else s.early_layer) * LAYER_PIECES + PIECES_UPTO[g + 1])
                        if g == 0:
                            pe.wait_ge(act_read, m * FILLS + 2)
                            pe.wait_ge(dve_read, m * DVE_READS + 2)
                    x = 2 + 10 * g + UNIT_AT[g][u]
                    bank_free(x, m)
                    for h in range(HALVES):
                        for a, w in PASSES:
                            last = pe.matmul(project[(x - 1) % 2][:], xT[a][:, h, t * P:(t + 1) * P], w_qkv[w][:, h, c, g, :],
                                             start=(h == 0 and (a, w) == PASSES[0]), stop=(h == HALVES - 1 and (a, w) == PASSES[-1]))
                    last.then_inc(filled, 1)
                elif kind == "turn":
                    g, u = item[1:]
                    m = n if g else n + 1
                    x = 2 + 10 * g + TRANSPOSE_AT[g][u]
                    pe.wait_ge(rotated, rotation(m, g, u))
                    bank_free(x, m)
                    for p in range(4):
                        last = pe.transpose(project[(x - 1) % 2][:, p * P:(p + 1) * P], with_cos[:, u, p * P:(p + 1) * P], ident[:])
                    last.then_inc(filled, 1)
                elif kind == "project_out":
                    t = item[1]
                    if t == 0:
                        pe.wait_ge(w_low, s.layer * LAYER_PIECES + PIECES_UPTO[3])
                        pe.wait_ge(out_split, f * PAIRS + PAIRS)
                        wait(pe, acc_read, f * 2 + 1)
                    for p in range(PAIRS):
                        for a, w in PASSES:
                            last = pe.matmul(acc[:, t, :], oT[a][:, p, t * P:(t + 1) * P], w_out[w][:, p, :],
                                             start=(p == 0 and (a, w) == PASSES[0]), stop=(p == PAIRS - 1 and (a, w) == PASSES[-1]))
                    if t == TILES - 1:
                        last.then_inc(attn_projected, 1)
                elif kind == "norm_turn":
                    pe.wait_ge(ln_done, f + 1)
                    wait(pe, wide_read, f * WIDE_FILLS + 1)
                    for h in range(HALVES):
                        for t in range(TILES):
                            last = pe.transpose(wide[:, h, t * P:(t + 1) * P], xn[:, t, h * P:(h + 1) * P], ident[:])
                    last.then_inc(wide_filled, 1)
                elif kind in ("gate", "value"):
                    i = item[1]
                    x = 2 + i if kind == "gate" else 5 + i
                    if x == 2:
                        pe.wait_ge(w_low, s.layer * LAYER_PIECES + PIECES_UPTO[5])
                        pe.wait_ge(xn_low, f + 1 + 1)
                    pe.wait_ge(wide_read, f * WIDE_FILLS + x - 1 + 1)
                    for k in range(2):
                        col = (2 * i + k) * P + (FFN if kind == "gate" else 0)
                        for h in range(HALVES):
                            for a, w in PASSES:
                                last = pe.matmul(wide[:, k, :], w_up[w][:, h, col:col + P], xnT[a][:, h, :],
                                                 start=(h == 0 and (a, w) == PASSES[0]), stop=(h == HALVES - 1 and (a, w) == PASSES[-1]))
                    last.then_inc(wide_filled, 1)
                elif kind == "down":
                    i = item[1]
                    if i == 0:
                        pe.wait_ge(w_low, s.layer * LAYER_PIECES + PIECES_UPTO[6])
                        pe.wait_ge(acc_read, f * 2 + 1 + 1)
                    pe.wait_ge(h_low, f * 3 + i + 1 + 1)
                    for k in range(2):
                        j = 2 * i + k
                        rows = P if j < FFN_TILES - 1 else FFN_REST
                        for t in range(TILES):
                            for a, w in PASSES:
                                last = pe.matmul(acc[:, t, :], hT[a][0:rows, k, t * P:(t + 1) * P], w_down[w][0:rows, j, :],
                                                 start=(j == 0 and t == 0 and (a, w) == PASSES[0]),
                                                 stop=(j == FFN_TILES - 1 and (a, w) == PASSES[-1]), skip_group_check=True)
                    last.then_inc(h_used, 1)

            def scores(s, t, H):
                g = t // GROUP_HEADS
                if t % GROUP_HEADS == 0:
                    pe.wait_ge(act_read, turn_fill(s.n, g, 3))
                wait(pe, scores_masked, H - 1)
                rows = slice(HEAD_DIM * (t % 2), HEAD_DIM * (t % 2) + HEAD_DIM)
                pe.matmul(score[t % 2][:, 0:BAND0], qT[rows, t // 2, 0:P], kT[rows, t // 2, 0:P], start=True, stop=True)
                pe.matmul(score[t % 2][:, BAND0:BAND], qT[rows, t // 2, P:TOKENS], kT[rows, t // 2, P - WINDOW:TOKENS],
                          start=True, stop=True).then_inc(scores_ready, 1)

            def turn_probs(t, H):
                pe.wait_ge(probs_scaled, H + 1)
                wait(pe, probsT_copied, H)
                pr = probs[:, t % 4, :]
                pe.transpose(turned[:, 0:P], pr[:, 0:P], ident[:])
                pe.transpose(turned[:, P:2 * P], pr[:, 2 * P:3 * P], ident[:])
                pe.transpose(turned[:, 2 * P:2 * P + WINDOW], pr[0:WINDOW, P:2 * P], ident[0:WINDOW, 0:WINDOW]).then_inc(probs_turned, 1)

            def mix_values(n, t, H, Q):
                if t % GROUP_HEADS == 0:
                    pe.wait_ge(act_read, unit_fill(n, t // GROUP_HEADS, 5))
                pe.wait_ge(probsT_copied, H + 1)
                if t % 2 == 0:
                    wait(pe, out_split, Q)
                rows = slice(HEAD_DIM * (t % 2), HEAD_DIM * (t % 2) + HEAD_DIM)
                cols = slice(t * HEAD_DIM, (t + 1) * HEAD_DIM)
                o = mix[rows, (t // 2) % 2, :]
                pT = probsT[:, t % 2, :]
                pe.matmul(o[:, 0:P], v[:, 0, cols], pT[:, 0:P], start=True, stop=True)
                pe.matmul(o[:, P:TOKENS], v[:, 1, cols], pT[:, P:2 * P], start=True, stop=False)
                pe.matmul(o[:, P:P + WINDOW], v[:, 0, cols], pT[:, 2 * P:BAND], start=False, stop=True).then_inc(mixed, 1)

            def slot(s):
                if isinstance(s.n, int) and s.n == -1:
                    pe.wait_ge(cleared, 3)
                for t in range(HEADS):
                    if s.head(t, 0) is not None:
                        scores(s, t, s.head(t, 0))
                    if s.head(t, 2) is not None:
                        turn_probs((t - 2) % HEADS, s.head(t, 2))
                    if s.head(t, 3) is not None:
                        h = (t - 3) % HEADS
                        mix_values(s.n, h, s.head(t, 3), s.n * PAIRS + (t - 3) // 2)
                    for item in s.dense(t):
                        dense(s, item)

            pe.sem_inc(h_used, 1)
            run_slots(pe, slot)

        @block.scalar
        def _(act):
            def dense(s, item):
                n, kind = s.n, item[0]
                f = n - 1
                if kind == "input":
                    m = n + 1
                    for h in range(HALVES):
                        act.wait_ge(filled, m * FILLS + h + 1)
                        act.copy(xT[0][:, h, h:h + TOKENS], project[h][:, 0:TOKENS]).then_inc(act_read, 1)
                elif kind == "unit":
                    g, u = item[1:]
                    m = n if g else n + 1
                    bank = project[(2 + 10 * g + UNIT_AT[g][u] - 1) % 2]
                    act.wait_ge(filled, unit_fill(m, g, u))
                    if u < 4:
                        if g == 1:
                            act.wait_ge(filled, turn_fill(m, 0, u))
                        elif not (isinstance(m, int) and m == 0):
                            act.wait_ge(filled, turn_fill(m - 1, 1, u))
                        act.activation(with_sin[:, u, :], bank[:], ACT.Square, scale=1.0 if u % 2 else 1.0 / QK_SCALE)
                        act.copy(with_cos[:, u, :], bank[:]).then_inc(act_read, 1)
                    else:
                        wait(act, mixed, m * HEADS - HEADS + GROUP_HEADS * (g + 1) if not (isinstance(m, int) and m == 0) else 0)
                        act.copy(v[:, u - 4, g * GROUP:(g + 1) * GROUP], bank[:]).then_inc(act_read, 1)
                elif kind == "turn":
                    g, u = item[1:]
                    m = n if g else n + 1
                    bank = project[(2 + 10 * g + TRANSPOSE_AT[g][u] - 1) % 2]
                    act.wait_ge(filled, turn_fill(m, g, u))
                    wait(act, scores_ready, m * HEADS - HEADS + GROUP_HEADS * (g + 1) if not (isinstance(m, int) and m == 0) else 0)
                    dst = (kT if u % 2 else qT)[:, 4 * g:4 * g + 4, (u // 2) * P:(u // 2 + 1) * P]
                    act.copy(dst, bank[:].rearrange("p (a b) -> p a b", a=4)).then_inc(act_read, 1)
                elif kind == "norm_turn":
                    act.wait_ge(wide_filled, f * WIDE_FILLS + 1)
                    act.wait_ge(params_loaded, s.layer * 32 + 32)
                    at = 2 * FFN_TILES
                    for h in range(HALVES):
                        last = act.activation(xn[:, h, :], wide[:, h, :], ACT.Identity, bias=params[:, at + HALVES + h:at + HALVES + h + 1],
                                              scale=params[:, at + h:at + h + 1])
                    last.then_inc(wide_read, 1)
                    act.wait_ge(wide_read, f * WIDE_FILLS + 1 + 1)
                    act.copy(xnT[0][:], xn[:]).then_inc(xn_high, 1)
                elif kind == "gelu":
                    act.wait_ge(wide_read, f * WIDE_FILLS + 4 + 1)
                    act.activation(gates[:], gates[:], ACT.Gelu).then_inc(gelu_done, 1)
                elif kind == "value":
                    i = item[1]
                    act.wait_ge(wide_read, f * WIDE_FILLS + 5 + i + 1)
                    wait(act, h_used, f * 3 + i + 1)
                    if i < 2:
                        act.copy(hT[0][:], gates[:, 2 * i:2 * i + 2, :]).then_inc(h_high, 1)
                    else:
                        act.copy(hT[0][:, 0, :], gates[:, 4, :])
                        act.copy(hT[0][0:FFN_REST, 1, :], gates[0:FFN_REST, 5, :]).then_inc(h_high, 1)

            def slot(s):
                if isinstance(s.n, int) and s.n == -1:
                    act.wait_ge(cleared, 3)
                for t in range(HEADS):
                    H = s.head(t, 2)
                    if H is not None and t % 2 == 0:
                        act.wait_ge(probs_turned, H + 1)
                        wait(act, mixed, H - 1)
                        act.copy(probsT[:, t % 2, :], turned[:, 0:BAND]).then_inc(probsT_copied, 1)
                    H = s.head(t, 3)
                    if H is not None and (t - 3) % 2 == 1:
                        pair = ((t - 3) % HEADS) // 2
                        act.wait_ge(mixed, H + 1)
                        if pair == 0:
                            wait(act, attn_projected, s.n)
                        act.copy(oT[0][:, pair, :], mix[:, pair % 2, :]).then_inc(out_high, 1)
                    H = s.head(t, 0)
                    if H is not None:
                        act.wait_ge(scores_masked, H + 1)
                        wait(act, probs_turned, H - 3)
                        for i, (a, b, at) in enumerate(((0, BAND0, 0), (BAND0, BAND, P + WINDOW))):
                            last = act.activation(probs[:, t % 4, at:at + b - a], masked[:, t % 2, a:b], ACT.Exp,
                                                  bias=shift[:, t % 2, i:i + 1], scale=-1.0, accum_out=sums[:, t % 4, i:i + 1])
                        last.then_inc(exp_done, 1)
                    for item in s.dense(t):
                        dense(s, item)
                    for blk, piece in s.splits(t):
                        act.wait_ge(*last_use(blk, piece, s.layer + 1))
                        W.split_high(act, blk, piece, s.layer + 1)

            run_slots(act, slot)

        @block.gpsimd
        def _(pool):
            pool.memset(probs[:], 0.0).then_inc(cleared, 1)
            pool.memset(xn[0:1, 0, P:DIM], 0.0).then_inc(row_cleared, 1)
            for part in range(2):
                pool.memset(xT[part][:].bitcast(FP32), 0.0).then_inc(cleared, 1)

            def dense(s, item):
                n, kind = s.n, item[0]
                f = n - 1
                if kind == "rotate":
                    g, u = item[1:]
                    m = n if g else n + 1
                    k = rotation(m, g, u)
                    if u % 2 == 0:
                        wait(pool, scores_masked, m * HEADS - HEADS + GROUP_HEADS * (g + 1) if not (isinstance(m, int) and m == 0) else 0)
                    pool.wait_ge(floored, k)
                    if u % 2 == 0:
                        pool.tensor_tensor(query_scale[:, u // 2, g * GROUP_HEADS:(g + 1) * GROUP_HEADS], sums_sq[:, u, :],
                                           half[:, 0:GROUP_HEADS], ALU.pow)
                    else:
                        pool.tensor_tensor(inv_norm[:, u // 2, :], sums_sq[:, u, :], half[:, 0:GROUP_HEADS], ALU.pow)
                    pool.wait_ge(parts_ready, k)
                    add = pool.tensor_tensor(with_cos[:, u, :], with_cos[:, u, :], with_sin[:, u, :], ALU.add)
                    if u % 2 == 0:
                        add.then_inc(rotated, 1)
                    else:
                        add.then_inc(pool_step, 1)
                        pool.wait_ge(pool_step, m * 4 + 2 * g + (u + 1) // 2)
                        view = with_cos[:, u, :].rearrange("p (h d) -> p h d", h=GROUP_HEADS)
                        pool.tensor_tensor(view, view, inv_norm[:, u // 2, :].unsqueeze(2).broadcast_to([P, GROUP_HEADS, HEAD_DIM]),
                                           ALU.mult).then_inc(rotated, 1)
                elif kind == "norm_stats":
                    wait_apart(pool, ln_moments, f + 1, passed)
                    pool.tensor_scalar(ln_mv[:, :, 1], ln_mv[:, :, 1], EPS, None, ALU.add).then_inc(ln_floor, 1)
                    pool.wait_ge(ln_floor, f + 1)
                    pool.tensor_tensor(ln_rstd[:], ln_mv[:, :, 1], half[:, 0:TILES], ALU.pow).then_inc(ln_root, 1)
                elif kind == "norm_turn":
                    wait_apart(pool, xn_low, f + 1 + 1, passed)
                    if not s.last:
                        pool.memset(xn[0:1, 0, P:DIM], 0.0).then_inc(row_cleared, 1)
                    pool.wait_ge(params_loaded, s.layer * 32 + 32)
                    add = pool.tensor_tensor(res[:], res[:], b_down[:].unsqueeze(1).broadcast_to([P, TILES, DIM]), ALU.add)
                    if s.last:
                        add.then_inc(bias_added, 1)
                        pool.wait_ge(bias_added, s.ffn_batch + 1)
                        pool.wait_ge(x2_loaded, s.ffn_batch * 16 + 16)
                        add = pool.tensor_tensor(res[:], res[:], xn[:], ALU.add)
                        add.then_inc(x2_added, 1)
                        pool.wait_ge(x2_added, s.ffn_batch + 1)
                        pool.sem_inc(res_ready, 1)
                        pool.memset(xn[0:1, 0, P:DIM], 0.0).then_inc(row_cleared, 1)
                    else:
                        add.then_inc(res_ready, 1)

            def slot(s):
                for t in range(HEADS):
                    for item in s.dense(t):
                        dense(s, item)

            run_slots(pool, slot)

        @block.vector
        def _(dve):
            def build_tables(layer):
                dve.wait_ge(scales_loaded, layer * 16 + 16)
                dve.wait_ge(tables_loaded, layer * 16 + 16)
                for part in range(2):
                    scale = qk_scales[:, part].unsqueeze(1).broadcast_to([P, TILES, 2, HEAD_DIM // 2])
                    for k, sc in ((0, scale), (1, scale[:, :, ::-1, :])):
                        last = dve.tensor_tensor(tables[:, 2 * part + k].rearrange("p t (a b) -> p t a b", a=2),
                                                 tables[:, 2 * part + k].rearrange("p t (a b) -> p t a b", a=2), sc, ALU.mult)
                last.then_inc(tables_built, 1)
                dve.wait_ge(tables_built, layer + 1)

            def dense(s, item):
                n, kind = s.n, item[0]
                f = n - 1
                if kind == "input":
                    m = n + 1
                    for h in range(HALVES):
                        dve.wait_ge(act_read, m * FILLS + h + 1)
                        dve.tensor_tensor(xT[1][:, h, h:h + TOKENS], project[h][:, 0:TOKENS], xT[0][:, h, h:h + TOKENS].bitcast(FP32),
                                          ALU.subtract).then_inc(dve_read, 1)
                elif kind == "rotate":
                    g, u = item[1:]
                    m = n if g else n + 1
                    c, t = u % 2, u // 2
                    k = rotation(m, g, u)
                    dve.wait_ge(act_read, unit_fill(m, g, u))

                    def heads(ap):
                        return ap.rearrange("p (h a b) -> p h a b", h=GROUP_HEADS, a=2)

                    def table(k):
                        return tables[:, k, t, :].rearrange("p (a b) -> p a b", a=2).unsqueeze(1)\
                            .broadcast_to([P, GROUP_HEADS, 2, HEAD_DIM // 2])

                    dve.tensor_reduce(sums_sq[:, u, :], with_sin[:, u, :].rearrange("p (h d) -> p h d", h=GROUP_HEADS), AXIS_X,
                                      ALU.add).then_inc(squares_summed, 1)
                    dve.wait_ge(squares_summed, k)
                    dve.tensor_tensor(heads(with_sin[:, u, :]), heads(with_cos[:, u, :])[:, :, ::-1, :], table(2 * c + 1), ALU.mult)
                    floor = NORM_FLOOR if c else NORM_FLOOR / QK_SCALE ** 2
                    dve.tensor_scalar(sums_sq[:, u, :], sums_sq[:, u, :], floor, None, ALU.max).then_inc(floored, 1)
                    dve.wait_ge(floored, k)
                    dve.tensor_tensor(heads(with_cos[:, u, :]), heads(with_cos[:, u, :]), table(2 * c), ALU.mult).then_inc(parts_ready, 1)
                elif kind == "add_out":
                    dve.wait_ge(attn_projected, f + 1)
                    dve.wait_ge(res_loaded, f * 16 + 16)
                    dve.tensor_tensor(res[:], acc[:], res[:], ALU.add).then_inc(acc_read, 1)
                elif kind == "norm_stats":
                    dve.wait_ge(shifted, f * 32 + 32)
                    dve.wait_ge(row_cleared, f + 1)
                    dve.wait_ge(acc_read, f * 2 + 1 + 1)
                    for t in range(TILES):
                        dve.bn_stats(ln_stats[:, t, 0, :], res[:, t, 0:P])
                        last = dve.bn_stats(ln_stats[:, t, 1, :], xn[:, t, P:DIM])
                    last.then_inc(ln_stated, 1)
                    wait_apart(dve, ln_stated, f + 1, passed)
                    for t in range(TILES):
                        last = dve.bn_aggr(ln_mv[:, t, :], ln_stats[:, t].rearrange("p a b -> p (a b)"))
                    last.then_inc(ln_moments, 1)
                elif kind == "norm_apply":
                    dve.wait_ge(ln_root, f + 1)
                    for t in range(TILES):
                        dve.tensor_scalar(xn[:, t, 0:P], res[:, t, 0:P], ln_mv[:, t, 0:1], ln_rstd[:, t:t + 1], ALU.subtract, ALU.mult)
                        last = dve.tensor_scalar(xn[:, t, P:DIM], xn[:, t, P:DIM], ln_mv[:, t, 0:1], ln_rstd[:, t:t + 1],
                                                 ALU.subtract, ALU.mult)
                    last.then_inc(ln_done, 1)
                elif kind == "norm_turn":
                    dve.wait_ge(xn_high, f + 1)
                    dve.tensor_tensor(xnT[1][:], xn[:], xnT[0][:].bitcast(FP32), ALU.subtract).then_inc(xn_low, 1)
                elif kind == "gate":
                    i = item[1]
                    dve.wait_ge(wide_filled, f * WIDE_FILLS + 2 + i)
                    if i == 0:
                        dve.wait_ge(params_loaded, s.layer * 32 + 32)
                        wait(dve, h_low, f * 3 + 1)
                    for k in range(2):
                        j = FFN_TILES + 2 * i + k
                        last = dve.tensor_scalar(gates[:, 2 * i + k, :], wide[:, k, :], params[:, j:j + 1], None, ALU.add)
                    last.then_inc(wide_read, 1)
                elif kind == "value":
                    i = item[1]
                    dve.wait_ge(wide_filled, f * WIDE_FILLS + 5 + i)
                    dve.wait_ge(gelu_done, f + 1)
                    for k in range(2):
                        j = 2 * i + k
                        rows = P if j < FFN_TILES - 1 else FFN_REST
                        last = dve.scalar_tensor_tensor(gates[0:rows, j, :], wide[0:rows, k, :], params[0:rows, j:j + 1],
                                                        gates[0:rows, j, :], ALU.add, ALU.mult)
                    last.then_inc(wide_read, 1)
                elif kind == "low":
                    i = item[1]
                    dve.wait_ge(h_high, f * 3 + i + 1)
                    if i < 2:
                        dve.tensor_tensor(hT[1][:], gates[:, 2 * i:2 * i + 2, :], hT[0][:].bitcast(FP32), ALU.subtract).then_inc(h_low, 1)
                    else:
                        dve.tensor_tensor(hT[1][:, 0, :], gates[:, 4, :], hT[0][:, 0, :].bitcast(FP32), ALU.subtract)
                        dve.tensor_tensor(hT[1][0:FFN_REST, 1, :], gates[0:FFN_REST, 5, :], hT[0][0:FFN_REST, 1, :].bitcast(FP32),
                                          ALU.subtract).then_inc(h_low, 1)
                elif kind == "residual":
                    dve.wait_ge(h_used, f * 3 + 3 + 1)
                    dve.wait_ge(res_ready, f + 1)
                    dve.tensor_tensor(res[:], acc[:], res[:], ALU.add).then_inc(acc_read, 1)

            def slot(s):
                if isinstance(s.n, int) and s.n == -1:
                    build_tables(0)
                for t in range(HEADS):
                    h4 = (t - 1) % 4
                    before = s.head(t, 1)
                    if before is not None:
                        dve.wait_ge(exp_done, before + 1)
                        dve.reciprocal(inv_sums[:, h4, :], sums[:, h4, :]).then_inc(sums_inverted, 1)
                    H = s.head(t, 0)
                    if H is not None:
                        if t % GROUP_HEADS == 0:
                            dve.wait_ge(rotated, s.n * ROTATIONS + 4 * (t // GROUP_HEADS) + 4)
                        dve.wait_ge(scores_ready, H + 1)
                        wait(dve, exp_done, H - 1)
                        dve.sem_inc(passed, 1)
                        for i, (a, b) in enumerate(((0, BAND0), (BAND0, BAND))):
                            last = dve.tensor_tensor_reduce(out=masked[:, t % 2, a:b], in0=score[t % 2][:, a:b], in1=mask[:, a:b],
                                                            scale=query_scale[:, i, t:t + 1], scalar=3e38, op0=ALU.add, op1=ALU.min,
                                                            accum_out=shift[:, t % 2, i:i + 1])
                        last.then_inc(scores_masked, 1)
                    H = s.head(t, 2)
                    if H is not None and t % 2 == 1:
                        dve.wait_ge(probs_turned, H + 1)
                        wait(dve, mixed, H - 1)
                        dve.tensor_copy(probsT[:, t % 2, :], turned[:, 0:BAND]).then_inc(probsT_copied, 1)
                    if before is not None:
                        dve.wait_ge(sums_inverted, before + 1)
                        for i, (a, b) in enumerate(((0, P), (P + WINDOW, PROBS))):
                            last = dve.tensor_scalar(probs[:, h4, a:b], probs[:, h4, a:b], inv_sums[:, h4, i:i + 1], None, ALU.mult)
                        last.then_inc(probs_scaled, 1)
                    H = s.head(t, 3)
                    if H is not None and (t - 3) % 2 == 1:
                        pair = ((t - 3) % HEADS) // 2
                        dve.wait_ge(out_high, s.n * PAIRS + (t - 3) // 2 + 1)
                        dve.tensor_tensor(oT[1][:, pair, :], mix[:, pair % 2, :], oT[0][:, pair, :].bitcast(FP32),
                                          ALU.subtract).then_inc(out_split, 1)
                    for item in s.dense(t):
                        dense(s, item)
                    for blk, piece in s.splits(t):
                        W.split_low(dve, blk, piece, s.layer + 1)
                    if s.switch == "projections" and t == TABLES_TICK:
                        build_tables(s.layer + 1)

            for semaphore in (acc_read, xn_low, wide_read, h_low):
                dve.sem_inc(semaphore, 1)
            run_slots(dve, slot)


def decoder_kernel(nc, D):
    with ExitStack() as ctx:
        T = {
            "ident": ctx.enter_context(nc.sbuf_tensor("ident", [P, P], FP32)),
            "mask": ctx.enter_context(nc.sbuf_tensor("mask", [P, BAND], FP32)),
            "half": ctx.enter_context(nc.sbuf_tensor("half", [P, GROUP_HEADS], FP32)),
        }
        W = Weights(nc, ctx, D)
        front(nc, T, D, W)
        layers(nc, T, D, W)


def shape_constants():
    import numpy as np
    f32 = np.float32
    i = np.arange(TOKENS)
    allowed = (i[:, None] >= i[None, :]) & (i[:, None] <= i[None, :] + WINDOW)
    band = np.where(allowed, 0.0, MASKED).astype(f32)
    mask = np.concatenate([band[0:P, 0:P], band[P:TOKENS, P - WINDOW:TOKENS]], axis=1)
    halfdim = np.arange(0, HEAD_DIM, 2, dtype=f32)
    inv_freq = (f32(1.0) / f32(10000.0) ** (halfdim / f32(HEAD_DIM))).astype(f32)
    t = np.arange(TOKENS, dtype=f32)
    freqs = (t[:, None] * inv_freq[None, :]).astype(f32)
    base = ((halfdim + f32(0.4 * HEAD_DIM)) / f32(1.4 * HEAD_DIM)).astype(f32)
    power = ((t - TOKENS // 2) / f32(WINDOW // 2)).astype(f32)
    scale = (base[None, :] ** power[:, None]).astype(f32)
    cos, sin = np.cos(freqs), np.sin(freqs)
    parts = []
    for cs, sn, sign in ((cos * scale, sin * scale, 1.0), (cos / scale, sin / scale, -1.0)):
        parts += [sign * np.concatenate([cs, cs], 1), sign * np.concatenate([-sn, sn], 1)]
    rope = np.stack(parts).astype(f32).reshape(4, TILES, P, HEAD_DIM).transpose(2, 0, 1, 3)
    return {"ident": np.eye(P, dtype=f32), "mask": mask, "rope": np.ascontiguousarray(rope)}


def kernel(**inputs):
    import numpy as np
    import concourse.bacc as bacc
    from concourse.bass_utils import run_bass_kernel_spmd

    a = {k: np.asarray(v) for k, v in inputs.items()}

    def columns(rows):
        tiles = (rows.shape[1] + P - 1) // P
        padded = np.zeros((rows.shape[0], tiles * P), rows.dtype)
        padded[:, :rows.shape[1]] = rows
        return padded.reshape(rows.shape[0], tiles, P).transpose(0, 2, 1)

    b1 = a["L0_ffn_b1"]
    arrays = {
        "x": a["x"],
        "ctxT": a["ctx_1024"].transpose(0, 2, 1),
        "mem_wk": a["L0_attn_W_K"],
        "mem_w1t": a["L0_attn_W1"].T,
        "mem_w2t": a["L0_attn_W2"].T,
        "cross_wq": a["L0_xattn_Wq"],
        "cross_wk": a["L0_xattn_Wk"],
        "cross_wv": a["L0_xattn_Wv"],
        "cross_bqk": np.concatenate([columns(a["L0_xattn_bq"][None])[0], columns(a["L0_xattn_bk"][None])[0]], axis=1),
        "cross_bv": a["L0_xattn_bv"][None],
        "w_qkv": a["L0_ffn_Wqkv"],
        "w_out": a["L0_ffn_Wo"],
        "w_up": a["L0_ffn_W1"],
        "w_down": a["L0_ffn_W2"],
        "b_down": a["L0_ffn_b2"],
        "params": np.concatenate([columns(b1[:, :FFN]), columns(b1[:, FFN:]), columns(a["L0_ffn_ln_g"]),
                                  columns(a["L0_ffn_ln_b"])], axis=2),
        "qk_scales": np.concatenate([a["L0_ffn_q_scale"], a["L0_ffn_k_scale"]], axis=1),
    }
    arrays.update(shape_constants())
    arrays = {k: np.ascontiguousarray(v) for k, v in arrays.items()}

    nc = bacc.Bacc("TRN2", target_bir_lowering=False, num_devices=1)
    D = {name: nc.dram_tensor(f"in_{name}", v.shape, mybir.dt.from_np(v.dtype), kind="ExternalInput").ap()
         for name, v in arrays.items()}
    D["out"] = nc.dram_tensor("out", (BATCH, TOKENS, DIM), FP32, kind="ExternalOutput").ap()
    for name in ("x2", "y"):
        D[name] = nc.dram_tensor(f"{name}_scratch", (BATCH, TOKENS, DIM), FP32, kind="Internal").ap()
    decoder_kernel(nc, D)
    r = run_bass_kernel_spmd(nc, [{f"in_{name}": v for name, v in arrays.items()}], core_ids=[0])
    return r.results[0]["out"]
```
